# Optimizing a Trainium2 kernel written in Bass

```python
import numpy as np
import jax
import jax.numpy as jnp

def _softmax(x, axis=-1):
    return jax.nn.softmax(x, axis=axis)

def _gelu(x):
    return jax.nn.gelu(x, approximate=True)

def _silu(x):
    return jax.nn.silu(x)

def _sigmoid(x):
    return jax.nn.sigmoid(x)

def _layernorm(x, axis=-1, eps=1e-05):
    m = jnp.mean(x, axis=axis, keepdims=True)
    v = jnp.var(x, axis=axis, keepdims=True)
    return (x - m) / jnp.sqrt(v + eps)

def _scatter_add(tgt, idx, src, axis=0):
    return tgt.at[idx].add(src)

def _segment_sum(src, seg, n):
    return jax.ops.segment_sum(src, seg, n)
kernel_name = 'mk_conv_attn_hybrid_d2_conv_nhwc256_r2_506969'

def setup_inputs(seed: int=0):
    np.random.seed(seed)
    _w = jnp.asarray

    def _rec_inputs():
        import jax
        import jax.numpy as jnp
        _gk = jax.random.key(seed)
        x = -0.0006128 + 1 * jax.random.normal(jax.random.fold_in(_gk, 1), (8, 32, 25, 128), jnp.float32)
        return x
    x = _rec_inputs()

    def _L0_conv_setup():
        import jax, jax.numpy as jnp
        import numpy as np
        D_MODEL = 128
        D_INNER = 256
        D_STATE = 16
        D_CONV = 4
        DT_RANK = 16

        def _mamba_block(x, W_in, conv_w, conv_b, W_xproj, W_dt, b_dt, A_log, D_skip, W_out, ln_w):
            N, T, J, C = x.shape
            res = x
            xr = jnp.transpose(x, (0, 2, 1, 3)).reshape(N * J, T, C)
            B = N * J
            xz = jnp.einsum('btc,ec->bte', xr, W_in)
            xc, z = jnp.split(xz, 2, axis=-1)
            xp = jnp.pad(xc, ((0, 0), (D_CONV - 1, 0), (0, 0)))
            xw = jnp.stack([xp[:, k:k + T, :] for k in range(D_CONV)], axis=-1)
            xc = jnp.einsum('btdk,dk->btd', xw, conv_w) + conv_b
            xc = jax.nn.silu(xc)
            x_dbl = jnp.einsum('btd,ed->bte', xc, W_xproj)
            dt_in = x_dbl[..., :DT_RANK]
            Bm = x_dbl[..., DT_RANK:DT_RANK + D_STATE]
            Cm = x_dbl[..., DT_RANK + D_STATE:]
            dt = jax.nn.softplus(jnp.einsum('btr,dr->btd', dt_in, W_dt) + b_dt)
            A = -jnp.exp(A_log)
            dA = jnp.exp(jnp.einsum('btd,ds->btds', dt, A))
            dBu = jnp.einsum('btd,bts->btds', dt * xc, Bm)

            def step(h, inp):
                dA_t, dBu_t, C_t = inp
                h = dA_t * h + dBu_t
                y = jnp.einsum('bds,bs->bd', h, C_t)
                return (h, y)
            h0 = jnp.zeros((B, D_INNER, D_STATE), xc.dtype)
            _, ys = jax.lax.scan(step, h0, (jnp.swapaxes(dA, 0, 1), jnp.swapaxes(dBu, 0, 1), jnp.swapaxes(Cm, 0, 1)))
            y = jnp.swapaxes(ys, 0, 1)
            y = y + xc * D_skip
            y = y * jax.nn.silu(z)
            out = jnp.einsum('btd,cd->btc', y, W_out)
            out = out * jax.lax.rsqrt(jnp.mean(out * out, axis=-1, keepdims=True) + 1e-06) * ln_w
            out = jnp.transpose(out.reshape(N, J, T, C), (0, 2, 1, 3))
            return out + res
        key = jax.random.key(seed)
        ks = jax.random.split(key, 10)
        N, T, J, C = (8, 32, 25, D_MODEL)
        x = jax.random.normal(ks[0], (N, T, J, C), jnp.float32)
        W_in = jax.random.normal(ks[1], (2 * D_INNER, D_MODEL), jnp.float32) * 0.02
        conv_w = jax.random.normal(ks[2], (D_INNER, D_CONV), jnp.float32) * 0.2
        conv_b = jax.random.normal(ks[3], (D_INNER,), jnp.float32) * 0.02
        W_xproj = jax.random.normal(ks[4], (DT_RANK + 2 * D_STATE, D_INNER), jnp.float32) * 0.02
        W_dt = jax.random.normal(ks[5], (D_INNER, DT_RANK), jnp.float32) * 0.1
        b_dt = jax.random.normal(ks[6], (D_INNER,), jnp.float32) * 0.1 - 4.0
        A_log = jnp.log(jnp.broadcast_to(jnp.arange(1, D_STATE + 1, dtype=jnp.float32), (D_INNER, D_STATE)))
        D_skip = jnp.ones((D_INNER,), jnp.float32)
        W_out = jax.random.normal(ks[7], (D_MODEL, D_INNER), jnp.float32) * 0.02
        ln_w = jnp.ones((D_MODEL,), jnp.float32)
        return {'x': x, 'W_in': W_in, 'conv_w': conv_w, 'conv_b': conv_b, 'W_xproj': W_xproj, 'W_dt': W_dt, 'b_dt': b_dt, 'A_log': A_log, 'D_skip': D_skip, 'W_out': W_out, 'ln_w': ln_w}
    _L0_conv_all = _L0_conv_setup()
    _L0_conv_in = {k: v for k, v in _L0_conv_all.items() if k in ('W_in', 'conv_w', 'conv_b', 'W_xproj', 'W_dt', 'b_dt', 'A_log', 'D_skip', 'W_out', 'ln_w')}
    del _L0_conv_all

    def _L1_attn_setup():
        import jax, jax.numpy as jnp
        import numpy as np
        OUT_DIM = 128
        K_HEAD = 8
        key = jax.random.key(seed)
        k1, k2, k3 = jax.random.split(key, 3)
        B, N, Cin = (8, 1024, 128)
        input_feature = jax.random.normal(k1, (B, N, Cin), dtype=jnp.float32)
        W = jax.random.normal(k2, (Cin, OUT_DIM * 3), dtype=jnp.float32) * 0.05
        proj_w = jax.random.normal(k3, (OUT_DIM, OUT_DIM), dtype=jnp.float32) * 0.05
        proj_b = jnp.zeros((OUT_DIM,), dtype=jnp.float32)
        return {'input_feature': input_feature, 'W': W, 'proj_w': proj_w, 'proj_b': proj_b}
    _L1_attn_all = _L1_attn_setup()
    _L1_attn_in = {k: v for k, v in _L1_attn_all.items() if k in ('W', 'proj_w', 'proj_b')}
    del _L1_attn_all

    def _L1_ffn_setup():
        import math
        import jax, jax.numpy as jnp
        import numpy as np
        CAPACITY_FACTOR = 1.25
        TOP_K = 2
        LN_EPS = 1e-05

        def _layer_norm(x, gamma, beta):
            mu = jnp.mean(x, axis=-1, keepdims=True)
            var = jnp.var(x, axis=-1, keepdims=True)
            return (x - mu) * jax.lax.rsqrt(var + LN_EPS) * gamma + beta
        key = jax.random.key(seed)
        ks = jax.random.split(key, 4)
        B, S, D, F, E = (8, 2048, 128, 256, 8)
        x = jax.random.normal(ks[0], (B, S, D), dtype=jnp.float32)
        Wr = jax.random.normal(ks[1], (D, E), dtype=jnp.float32) / np.sqrt(D)
        br = jnp.zeros((E,), jnp.float32)
        W1 = jax.random.normal(ks[2], (E, D, F), dtype=jnp.float32) / np.sqrt(D)
        b1 = jnp.zeros((E, F), jnp.float32)
        W2 = jax.random.normal(ks[3], (E, F, D), dtype=jnp.float32) / np.sqrt(F)
        b2 = jnp.zeros((E, D), jnp.float32)
        gamma = jnp.ones((D,), jnp.float32)
        beta = jnp.zeros((D,), jnp.float32)
        return {'x': x, 'Wr': Wr, 'br': br, 'W1': W1, 'b1': b1, 'W2': W2, 'b2': b2, 'gamma': gamma, 'beta': beta}
    _L1_ffn_all = _L1_ffn_setup()
    _L1_ffn_in = {k: v for k, v in _L1_ffn_all.items() if k in ('Wr', 'br', 'W1', 'b1', 'W2', 'b2', 'gamma', 'beta')}
    del _L1_ffn_all
    return {'x': x, 'L0_conv_W_in': _L0_conv_in['W_in'], 'L0_conv_conv_w': _L0_conv_in['conv_w'], 'L0_conv_conv_b': _L0_conv_in['conv_b'], 'L0_conv_W_xproj': _L0_conv_in['W_xproj'], 'L0_conv_W_dt': _L0_conv_in['W_dt'], 'L0_conv_b_dt': _L0_conv_in['b_dt'], 'L0_conv_A_log': _L0_conv_in['A_log'], 'L0_conv_D_skip': _L0_conv_in['D_skip'], 'L0_conv_W_out': _L0_conv_in['W_out'], 'L0_conv_ln_w': _L0_conv_in['ln_w'], 'L1_attn_W': _L1_attn_in['W'], 'L1_attn_proj_w': _L1_attn_in['proj_w'], 'L1_attn_proj_b': _L1_attn_in['proj_b'], 'L1_ffn_Wr': _L1_ffn_in['Wr'], 'L1_ffn_br': _L1_ffn_in['br'], 'L1_ffn_W1': _L1_ffn_in['W1'], 'L1_ffn_b1': _L1_ffn_in['b1'], 'L1_ffn_W2': _L1_ffn_in['W2'], 'L1_ffn_b2': _L1_ffn_in['b2'], 'L1_ffn_gamma': _L1_ffn_in['gamma'], 'L1_ffn_beta': _L1_ffn_in['beta']}

def reference(x, L0_conv_W_in, L0_conv_conv_w, L0_conv_conv_b, L0_conv_W_xproj, L0_conv_W_dt, L0_conv_b_dt, L0_conv_A_log, L0_conv_D_skip, L0_conv_W_out, L0_conv_ln_w, L1_attn_W, L1_attn_proj_w, L1_attn_proj_b, L1_ffn_Wr, L1_ffn_br, L1_ffn_W1, L1_ffn_b1, L1_ffn_W2, L1_ffn_b2, L1_ffn_gamma, L1_ffn_beta):
    import jax
    import jax.numpy as jnp

    def _L0_conv_ref(x, W_in, conv_w, conv_b, W_xproj, W_dt, b_dt, A_log, D_skip, W_out, ln_w):
        import jax, jax.numpy as jnp
        import numpy as np
        D_MODEL = 128
        D_INNER = 256
        D_STATE = 16
        D_CONV = 4
        DT_RANK = 16

        def _mamba_block(x, W_in, conv_w, conv_b, W_xproj, W_dt, b_dt, A_log, D_skip, W_out, ln_w):
            N, T, J, C = x.shape
            res = x
            xr = jnp.transpose(x, (0, 2, 1, 3)).reshape(N * J, T, C)
            B = N * J
            xz = jnp.einsum('btc,ec->bte', xr, W_in)
            xc, z = jnp.split(xz, 2, axis=-1)
            xp = jnp.pad(xc, ((0, 0), (D_CONV - 1, 0), (0, 0)))
            xw = jnp.stack([xp[:, k:k + T, :] for k in range(D_CONV)], axis=-1)
            xc = jnp.einsum('btdk,dk->btd', xw, conv_w) + conv_b
            xc = jax.nn.silu(xc)
            x_dbl = jnp.einsum('btd,ed->bte', xc, W_xproj)
            dt_in = x_dbl[..., :DT_RANK]
            Bm = x_dbl[..., DT_RANK:DT_RANK + D_STATE]
            Cm = x_dbl[..., DT_RANK + D_STATE:]
            dt = jax.nn.softplus(jnp.einsum('btr,dr->btd', dt_in, W_dt) + b_dt)
            A = -jnp.exp(A_log)
            dA = jnp.exp(jnp.einsum('btd,ds->btds', dt, A))
            dBu = jnp.einsum('btd,bts->btds', dt * xc, Bm)

            def step(h, inp):
                dA_t, dBu_t, C_t = inp
                h = dA_t * h + dBu_t
                y = jnp.einsum('bds,bs->bd', h, C_t)
                return (h, y)
            h0 = jnp.zeros((B, D_INNER, D_STATE), xc.dtype)
            _, ys = jax.lax.scan(step, h0, (jnp.swapaxes(dA, 0, 1), jnp.swapaxes(dBu, 0, 1), jnp.swapaxes(Cm, 0, 1)))
            y = jnp.swapaxes(ys, 0, 1)
            y = y + xc * D_skip
            y = y * jax.nn.silu(z)
            out = jnp.einsum('btd,cd->btc', y, W_out)
            out = out * jax.lax.rsqrt(jnp.mean(out * out, axis=-1, keepdims=True) + 1e-06) * ln_w
            out = jnp.transpose(out.reshape(N, J, T, C), (0, 2, 1, 3))
            return out + res
        return _mamba_block(x, W_in, conv_w, conv_b, W_xproj, W_dt, b_dt, A_log, D_skip, W_out, ln_w)

    def _L1_attn_ref(input_feature, W, proj_w, proj_b):
        import jax, jax.numpy as jnp
        import numpy as np
        OUT_DIM = 128
        K_HEAD = 8
        B, N, _ = input_feature.shape
        C = OUT_DIM
        h = K_HEAD
        d = C // h
        qkv = jnp.matmul(input_feature, W)
        qkv = qkv.reshape(B, N, 3, h, d).transpose(2, 0, 3, 1, 4)
        q, k, v = (qkv[0], qkv[1], qkv[2])
        attn = jnp.einsum('bhnd,bhmd->bhnm', q, k) * C ** (-0.5)
        attn = jax.nn.softmax(attn, axis=-1)
        x = jnp.einsum('bhnm,bhmd->bhnd', attn, v)
        x = x.reshape(B, N, C)
        out = jax.nn.relu(jnp.matmul(x, proj_w) + proj_b)
        return out

    def _L1_ffn_ref(x, Wr, br, W1, b1, W2, b2, gamma, beta):
        import math
        import jax, jax.numpy as jnp
        import numpy as np
        CAPACITY_FACTOR = 1.25
        TOP_K = 2
        LN_EPS = 1e-05

        def _layer_norm(x, gamma, beta):
            mu = jnp.mean(x, axis=-1, keepdims=True)
            var = jnp.var(x, axis=-1, keepdims=True)
            return (x - mu) * jax.lax.rsqrt(var + LN_EPS) * gamma + beta
        B, S, D = x.shape
        E = Wr.shape[1]
        N = B * S
        K = TOP_K
        logits = jnp.mean(x, axis=1) @ Wr + br
        routing_weights = jax.nn.softmax(logits, axis=-1)
        capacity = float(math.ceil(N * CAPACITY_FACTOR / E))
        expected_loads = routing_weights.sum(axis=0) * (N / B)
        scale = jnp.where(expected_loads > capacity, capacity / expected_loads, 1.0)
        routing_weights = jax.nn.softmax(routing_weights * scale, axis=-1)
        rw_tok = jnp.broadcast_to(routing_weights[:, None, :], (B, S, E)).reshape(N, E)
        top_w, top_i = jax.lax.top_k(rw_tok, K)
        top_w = jax.nn.softmax(top_w, axis=-1)
        xf = x.reshape(N, D)
        h = jax.nn.gelu(jnp.einsum('nd,edf->enf', xf, W1) + b1[:, None, :], approximate=False)
        y = jnp.einsum('enf,efd->end', h, W2) + b2[:, None, :]
        w_dense = jnp.zeros((N, E), x.dtype).at[jnp.arange(N)[:, None], top_i].add(top_w)
        out = jnp.einsum('ne,end->nd', w_dense, y).reshape(B, S, D)
        out = _layer_norm(out + x, gamma, beta)
        return out

    def _gn(v, G=32, eps=1e-05):
        B_, H_, W_, C_ = v.shape
        g = v.reshape(B_, H_, W_, G, C_ // G)
        m = jnp.mean(g, axis=(1, 2, 4), keepdims=True)
        s = jnp.var(g, axis=(1, 2, 4), keepdims=True)
        return ((g - m) / jnp.sqrt(s + eps)).reshape(v.shape)

    def _ln_c(v, eps=1e-06):
        m = jnp.mean(v, axis=-1, keepdims=True)
        s = jnp.var(v, axis=-1, keepdims=True)
        return (v - m) / jnp.sqrt(s + eps)

    def _ln_t(v, eps=1e-05):
        m = jnp.mean(v, axis=-1, keepdims=True)
        s = jnp.var(v, axis=-1, keepdims=True)
        return (v - m) / jnp.sqrt(s + eps)

    def _to_tokens(v):
        B_, H_, W_, C_ = v.shape
        return v.reshape(B_, H_ * W_, C_)

    def _from_tokens(t, like):
        return t.reshape(like.shape)
    x = x + _L0_conv_ref(_gn(x), L0_conv_W_in, L0_conv_conv_w, L0_conv_conv_b, L0_conv_W_xproj, L0_conv_W_dt, L0_conv_b_dt, L0_conv_A_log, L0_conv_D_skip, L0_conv_W_out, L0_conv_ln_w)
    t = _to_tokens(x)
    t = t + _L1_attn_ref(_ln_t(t), L1_attn_W, L1_attn_proj_w, L1_attn_proj_b)
    t = t + _L1_ffn_ref(_ln_t(t), L1_ffn_Wr, L1_ffn_br, L1_ffn_W1, L1_ffn_b1, L1_ffn_W2, L1_ffn_b2, L1_ffn_gamma, L1_ffn_beta)
    x = _from_tokens(t, x)
    return x

_drawn_inputs = setup_inputs


def setup_inputs(seed=0):
    import zlib

    import numpy as np

    out = dict(_drawn_inputs(seed))
    spreads = {'L0_conv_D_skip': (1.0, 0.2),
     'L0_conv_ln_w': (1.0, 0.2),
     'L1_attn_proj_b': (0.0, 0.8),
     'L1_ffn_br': (0.0, 0.1),
     'L1_ffn_b1': (0.0, 2.0),
     'L1_ffn_b2': (0.0, 1.468),
     'L1_ffn_gamma': (1.0, 0.6),
     'L1_ffn_beta': (0.0, 0.8)}
    factors = {'L0_conv_W_xproj': 8.0,
     'L0_conv_W_dt': 8.0,
     'L0_conv_b_dt': 8.0,
     'L0_conv_A_log': 8.0,
     'L1_attn_W': 8.0,
     'L1_attn_proj_w': 8.0}
    for name, (base, spread) in spreads.items():
        noise = np.random.default_rng([zlib.crc32(name.encode()), seed]).standard_normal(out[name].shape)
        drawn = base * np.exp(spread * noise) if base else spread * noise
        out[name] = jnp.asarray(drawn.astype(out[name].dtype))
    for name, factor in factors.items():
        out[name] = (out[name] * factor).astype(out[name].dtype)
    return out
```

```python
import concourse.bass as bass
from concourse import mybir
from contextlib import ExitStack


class Signal:

    def __init__(self, sem, per_turn, primed=0):
        self.sem = sem
        self.per_turn = per_turn
        self.primed = primed

    def at(self, turn, k):
        return turn * self.per_turn + k + self.primed


class Order:

    def __init__(self, sem, per_turn):
        self.sem = sem
        self.per_turn = per_turn
        self.count = 0

    def after(self, engine, turn, ins):
        self.count += 1
        ins.then_inc(self.sem, 1)
        engine.wait_ge(self.sem, turn * self.per_turn + self.count)


def mamba_attention_moe(nc, x, w_in_t, conv_w, conv_b, w_xp_t, w_dt_t, b_dt, a_log, d_skip, w_out_t,
                        ln_w, w_qkv, proj_w, proj_b, w_r, b_r, w1, b1, w2, b2, gamma, beta, out):
    f32 = mybir.dt.float32
    bf16 = mybir.dt.bfloat16
    u32 = mybir.dt.uint32
    ACT = mybir.ActivationFunctionType
    ALU = mybir.AluOpType
    X = mybir.AxisListType.X

    B, T, J, C = x.shape
    TOK = T * J
    P = 128
    GROUP = C // 32
    DI = w_out_t.shape[0]
    NC_ = DI // P
    NS = a_log.shape[1]
    TAPS = conv_w.shape[1]
    RANK = w_dt_t.shape[0]
    H = 8
    HD = C // H
    NE, _, F = w1.shape
    FC = F // P
    TOPK = 2
    TT = 100
    NT = TOK // TT
    HALF = TOK // 2
    ST = [(k * P, min(P, TOK - k * P)) for k in range((TOK + P - 1) // P)]
    NST = len(ST)
    BANK = 512
    SPANS = [(0, BANK), (BANK, TOK - BANK)]
    ATT_SCALE = float(C) ** -0.5
    CAPACITY = float(-(-(B * TOK * 5 // 4) // NE))
    Q_PARTS = [0, 0, 1, 1, 0, 2]
    K_PARTS = [0, 1, 0, 1, 2, 0]
    KST = len(Q_PARTS) * HD
    C_ROWS = 3 * 32
    DT0 = 96

    x_v = x.rearrange("n t j c -> n (t j) c").rearrange("n (k p) c -> n p k c", p=TT)
    out_v = out.rearrange("n t j c -> n (t j) c").rearrange("n (k p) c -> n p k c", p=TT)

    ctx = ExitStack()
    with ctx:
        def sb(name, shape, dt=f32):
            return ctx.enter_context(nc.sbuf_tensor(name, shape, dt))

        def sem(name):
            return ctx.enter_context(nc.semaphore(name))

        def sig(name, per_turn=1):
            return Signal(sem(name), per_turn)

        freed = []

        def freeing(name, per_turn=1):
            freed.append(Signal(sem(name), per_turn, primed=1))
            return freed[-1]

        w_in_sb = sb("w_in_sb", [P, 2 * DI])
        conv_w_sb = sb("conv_w_sb", [P, NC_, TAPS])
        conv_b_sb = sb("conv_b_sb", [P, NC_])
        w_xp_sb = sb("w_xp_sb", [P, NC_, P])
        w_dt_sb = sb("w_dt_sb", [P, DI])
        b_dt_sb = sb("b_dt_sb", [P, NC_])
        a_sb = sb("a_sb", [P, NC_, NS])
        d_skip_sb = sb("d_skip_sb", [P, NC_])
        w_out_sb = sb("w_out_sb", [P, NC_, C])
        ln_w_sb = sb("ln_w_sb", [TT, C])
        w_qkv_sb = sb("w_qkv_sb", [P, 3 * C])
        proj_w_sb = sb("proj_w_sb", [P, C])
        proj_b_sb = sb("proj_b_sb", [1, C])
        w_r_sb = sb("w_r_sb", [P, NE])
        b_r_sb = sb("b_r_sb", [1, NE])
        gamma_sb = sb("gamma_sb", [TT, C])
        beta_sb = sb("beta_sb", [TT, C])
        ident = sb("ident", [P, P])
        group_avg = sb("group_avg", [P, P])
        ones = sb("ones", [P, P])
        neg_half = sb("neg_half", [P, NT])
        pick_c = sb("pick_c", [C_ROWS, NS, P], bf16)
        t2 = sb("t2", [TT, B, NT, C])
        x_mean = sb("x_mean", [P, B])
        x_tok = sb("x_tok", [TT, NT, C])
        chan_stats = sb("chan_stats", [P, 2, 6])
        NPART = 4
        part_mean = chan_stats[:, :, :].rearrange("p a (b c) -> p (a b) c", c=3)[:, :, 1]
        part_m2 = chan_stats[:, :, :].rearrange("p a (b c) -> p (a b) c", c=3)[:, :, 2]
        part_dev = sb("part_dev", [P, NPART])
        grp = sb("grp", [P, 6])
        xnT = sb("xnT", [P, TOK])
        big = sb("big", [P, 6 * NC_ * TOK])
        conv_acc = big[:, 0:NC_ * TOK].rearrange("p (c t) -> p c t", c=NC_)
        z_act = big[:, NC_ * TOK:2 * NC_ * TOK].rearrange("p (c t) -> p c t", c=NC_)
        xc = big[:, 2 * NC_ * TOK:3 * NC_ * TOK].rearrange("p (c t) -> p c t", c=NC_)
        dt_sb = big[:, 3 * NC_ * TOK:4 * NC_ * TOK].rearrange("p (c t) -> p c t", c=NC_)
        sp_e = big[:, 4 * NC_ * TOK:5 * NC_ * TOK].rearrange("p (c t) -> p c t", c=NC_)
        sp_l = big[:, 5 * NC_ * TOK:6 * NC_ * TOK].rearrange("p (c t) -> p c t", c=NC_)
        xd = sb("xd", [P, TOK])
        c_rest = sb("c_rest", [C_ROWS, TOK])
        c_mid = sb("c_mid", [C_ROWS, TOK], bf16)
        c_parts = sb("c_parts", [C_ROWS, TOK], bf16)
        b_tok = sb("b_tok", [P, NST, NS])
        u_tok = sb("u_tok", [P, NST, DI])
        dbu_tok = sb("dbu_tok", [P, 2, NST, P])
        dA = sb("dA", [P, 2, TOK])
        hst = sb("hst", [P, 2, TOK])
        g = sb("g", [P, 2, TOK])
        o_rms = sb("o_rms", [TT, NT, C])
        sq = sb("sq", [TT, NT, C])
        tok_stats = sb("tok_stats", [TT, NT, 6])
        tok_mv = sb("tok_mv", [TT, 3, NT])
        tok_r = sb("tok_r", [TT, 3, NT])
        t1 = sb("t1", [TT, NT, C])
        ln_tok = sb("ln_tok", [TT, NT, C])
        lnT = sb("lnT", [P, TOK])
        q_part = big[:, 0:3 * TOK // 2].bitcast(bf16).rearrange("p (a t) -> p a t", a=3)
        k_part = big[:, 3 * TOK // 2:3 * TOK].bitcast(bf16).rearrange("p (a t) -> p a t", a=3)
        v_ext = big[:, 3 * TOK:3 * TOK + NST * H * 32].rearrange("p (k h d) -> p k h d", k=NST, h=H)
        E0 = 3 * TOK + NST * H * 32
        probs = big[:, E0:E0 + 4 * 4 * HALF // 2].rearrange("p (b a t) -> p b a t", b=4, a=2)
        E1 = E0 + 8 * HALF
        o_raw = u_tok[:, :, :].rearrange("p k d -> p (k d)")[:, 0:2 * TOK].rearrange("p (g t) -> p g t", g=2)
        assert E1 <= 6 * NC_ * TOK
        q_stack = sb("q_stack", [KST + 3, H, TOK], bf16)
        k_stack = sb("k_stack", [KST + 3, H, TOK], bf16)
        part_rest = sb("part_rest", [P, TOK])
        q_max = sb("q_max", [P, NST, H])
        m_row = sb("m_row", [H, TOK])
        m_rest = sb("m_rest", [H, TOK])
        m_part = sb("m_part", [H, 3, TOK], bf16)
        o_rec = sb("o_rec", [TT, NT * H])
        o_tok = sb("o_tok", [TT, H, NT, HD])
        oT = sb("oT", [P, TOK])
        o_tok_v = o_tok[:, :, :, :].rearrange("p h i d -> p h (i d)")
        E2 = TOPK * FC * TOK
        E3, E4 = E2 + TOPK * F, E2 + TOPK * F + TOPK * FC * C
        w1_e = big[:, E2:E3].rearrange("p (k f) -> p k f", k=TOPK)
        w2_e = big[:, E3:E4].rearrange("p (k a c) -> p k a c", k=TOPK, a=FC)
        b1_e = sb("b1_e", [P, TOPK, FC])
        b2_e = sb("b2_e", [1, TOPK, C])
        w2_s = big[:, E4:2 * E4 - E3].rearrange("p (k a c) -> p k a c", k=TOPK, a=FC)
        b2_s = sb("b2_s", [1, C])
        hidden = big[:, 0:TOPK * FC * TOK].rearrange("p (k t) -> p k t", k=TOPK * FC)
        rt = sb("rt", [NE, 16, NE])
        top_v = sb("top_v", [B, 8])
        top_i = sb("top_i", [B, 8], u32)
        top_w = sb("top_w", [B, 4])
        w_diag = sb("w_diag", [B, B, TOPK])
        w_all = sb("w_all", [P, B * TOPK])
        idx = sb("idx", [1, B * TOPK], u32)

        PS = ctx.enter_context(nc.psum_tensor("PS", [P, 8 * BANK], f32))

        def bank(b, cols=BANK):
            return PS[:, b * BANK:b * BANK + cols]

        def wide(b):
            return PS[:, b * BANK:b * BANK + TOK]

        def halves(b):
            return PS[:, b * BANK:(b + 2) * BANK].rearrange("p (a t) -> p a t", a=2)[:, :, 0:HALF]

        def head_pair(b):
            return PS[:, b * BANK:(b + 4) * BANK].rearrange("p (a t) -> p a t", a=2)[:, :, 0:TOK]

        parts_dram = nc.dram_tensor("parts_dram", (2, P, 3, TOK), bf16).ap()
        max_dram = nc.dram_tensor("max_dram", (H, 3, TOK), bf16).ap()
        top_dram = nc.dram_tensor("top_dram", (B, TOPK), u32).ap()

        weights_in = sem("weights_in")
        weights_set = sem("weights_set")
        consts_pool = sem("consts_pool")
        consts_dve = sem("consts_dve")
        a_exp = sem("a_exp")
        x_in = sig("x_in", 16)
        xT_up = sig("xT_up")
        chan_ready = sig("chan_ready")
        gmean_up = sig("gmean_up")
        gdev_ready = sig("gdev_ready")
        gvar_up = sig("gvar_up")
        gvar_ready = sig("gvar_ready")
        pool_pow = sig("pool_pow", 4)
        var_ready = sig("var_ready", 3)
        xn_ready = sig("xn_ready")
        xz_up = sig("xz_up", 4)
        conv_done = sig("conv_done", 2)
        silu_done = sig("silu_done", 4)
        gn_tok_up = sig("gn_tok_up")
        xs_ready = freeing("xs_ready")
        xd_up = sig("xd_up")
        xd_ready = sig("xd_ready")
        bT_up = sig("bT_up")
        b_tok_ready = sig("b_tok_ready")
        dt_up = sig("dt_up", 2)
        dt_abs = sig("dt_abs", 2)
        dt_relu = sig("dt_relu", 2)
        sp_exp = sig("sp_exp")
        sp_ln = sig("sp_ln")
        dt_ready = sig("dt_ready")
        u_ready = sig("u_ready")
        uT_up = sig("uT_up")
        u_tok_ready = sig("u_tok_ready")
        c_ready = sig("c_ready")
        NSTEP = NC_ * NS
        dbu_ready = sig("dbu_ready", NSTEP)
        dbuT_up = sig("dbuT_up", NSTEP)
        dA_ready = sig("dA_ready", NSTEP)
        scan_done = sig("scan_done", NSTEP)
        cb_up = sig("cb_up", NSTEP)
        g_ready = sig("g_ready", NSTEP)
        y_up = sig("y_up", NSTEP)
        y_ready = sig("y_ready", NC_)
        out_up = sig("out_up")
        v_copied = sig("v_copied")
        rms_sq = sig("rms_sq")
        ln1_ready = sig("ln1_ready")
        ln1T_up = sig("ln1T_up")
        ln1T_ready = sig("ln1T_ready")
        q_up = sig("q_up")
        k_up = sig("k_up")
        v_up = sig("v_up")
        qk_first = sig("qk_first", 2)
        qk_parts = sig("qk_parts", 2)
        v_ready = sig("v_ready")
        parts_out = sig("parts_out", 32)
        NSTK = 2 * len(Q_PARTS)
        stacks_in = sig("stacks_in", 16 * NSTK)
        NMAX = NST * H // 2
        smax_up = sig("smax_up", NMAX)
        smax_read = sig("smax_read", NMAX)
        maxT_up = sig("maxT_up")
        m_parts = sig("m_parts")
        max_out = sig("max_out", 16)
        max_in = sig("max_in", 16 * 3)
        NPAIR = 2 * 2 * NST * 2
        s_up = sig("s_up", NPAIR)
        probs_ready = sig("probs_ready", NPAIR)
        pv_up = sig("pv_up", NPAIR)
        o_copied = sig("o_copied", 4)
        oTok_up = sig("oTok_up")
        o_tok_ready = sig("o_tok_ready")
        oT_up = sig("oT_up")
        oT_ready = sig("oT_ready")
        proj_up = sig("proj_up")
        t2_ready = sig("t2_ready")
        ln2_ready = sig("ln2_ready")
        mean_up = sig("mean_up")
        mean_read = freeing("mean_read")
        logits_up = sem("logits_up")
        rt_ready = sem("rt_ready")
        rt_exp = sem("rt_exp")
        loads_up = sem("loads_up")
        top_ready_rw = sem("top_ready_rw")
        top_ready = sem("top_ready")
        top_moved = sem("top_moved")
        w_diag_ready = sem("w_diag_ready")
        w_all_up = sem("w_all_up")
        w_all_ready = sem("w_all_ready")
        e_w1_in = sig("e_w1_in", 16 * 2 * TOPK)
        e_w2_in = sig("e_w2_in", 16 * 2 * TOPK)
        e_w2_scaled = freeing("e_w2_scaled")
        f_var = sig("f_var", 2)
        f_pow = sig("f_pow", 2)
        f_ready = sig("f_ready")
        fT_up = sig("fT_up")
        fT_ready = sig("fT_ready")
        h_up = sig("h_up", TOPK * FC)
        h_ready = freeing("h_ready", TOPK * FC)
        y_e_up = freeing("y_e_up")
        res_read = freeing("res_read")
        lnf_ready = freeing("lnf_ready")
        fin_ready = freeing("fin_ready")
        out_stored = freeing("out_stored", 16)

        dve_order = Order(sem("dve_order"), 40)
        dve_order_rt = Order(sem("dve_order_rt"), 0)
        dve_order_e = Order(sem("dve_order_e"), 9)
        act_order = Order(sem("act_order"), 0)
        pool_order = Order(sem("pool_order"), 0)
        pool_order_e = Order(sem("pool_order_e"), 2)

        block = ctx.enter_context(nc.Block())

        NW = [0]
        @block.sync
        def _(sp):
            def load(dst, src):
                NW[0] += 16
                sp.dma_start(dst, src).then_inc(weights_in, 16)

            load(w_in_sb[:, :], w_in_t)
            load(conv_w_sb[:, :, :], conv_w.rearrange("(c p) k -> p c k", p=P))
            load(conv_b_sb[:, :], conv_b)
            load(b_dt_sb[:, :], b_dt)
            load(a_sb[:, :, :], a_log.rearrange("(c p) s -> p c s", p=P))
            load(d_skip_sb[:, :], d_skip)
            load(w_out_sb[:, :, :], w_out_t.rearrange("(c p) o -> p c o", p=P))
            load(ln_w_sb[:, :], ln_w.rearrange("(o c) -> o c", o=1).to_broadcast([TT, C]))
            load(w_qkv_sb[:, :], w_qkv)
            load(proj_w_sb[:, :], proj_w)
            load(proj_b_sb[:, :], proj_b.rearrange("(o c) -> o c", o=1))
            load(w_r_sb[:, :], w_r)
            load(b_r_sb[:, :], b_r.rearrange("(o c) -> o c", o=1))
            load(gamma_sb[:, :], gamma.rearrange("(o c) -> o c", o=1).to_broadcast([TT, C]))
            load(beta_sb[:, :], beta.rearrange("(o c) -> o c", o=1).to_broadcast([TT, C]))
            sp.wait_ge(weights_set, 1)
            xp_v = w_xp_t.rearrange("(c p) e -> p c e", p=P)
            for q in range(3):
                load(w_xp_sb[:, :, 32 * q:32 * q + NS], xp_v[:, :, RANK + NS:RANK + 2 * NS])
            load(w_xp_sb[:, :, DT0:DT0 + RANK + NS], xp_v[:, :, 0:RANK + NS])
            load(w_dt_sb[DT0:DT0 + RANK, :], w_dt_t)

            with nc.sync.Fori(0, B) as n:
                sp.wait_ge(xs_ready.sem, xs_ready.at(n, 0))
                sp.dma_start(x_tok[:, :, :], x_v[bass.ds(n, 1)].rearrange("o p k c -> (o p) k c")).then_inc(x_in.sem, 16)
                for i, part in enumerate((q_part, k_part)):
                    sp.wait_ge(qk_parts.sem, qk_parts.at(n, i + 1))
                    sp.dma_start(parts_dram[i], part).then_inc(parts_out.sem, 16)
                sp.wait_ge(parts_out.sem, parts_out.at(n, 32))
                for i, (stack, which) in enumerate(((q_stack, Q_PARTS), (k_stack, K_PARTS))):
                    for r, a in enumerate(which):
                        sp.dma_start(stack[HD * r:HD * (r + 1), :, :],
                                     parts_dram[i, :, a, :].rearrange("(h d) t -> d h t", h=H)
                                     ).then_inc(stacks_in.sem, 16)
                sp.wait_ge(m_parts.sem, m_parts.at(n, 1))
                sp.dma_start(max_dram, m_part[:, :, :]).then_inc(max_out.sem, 16)
                sp.wait_ge(max_out.sem, max_out.at(n, 16))
                for a in range(3):
                    sp.dma_start(q_stack[KST + a:KST + a + 1, :, :],
                                 max_dram[:, a, :].rearrange("(o h) t -> o h t", o=1)).then_inc(max_in.sem, 16)

            sp.wait_ge(top_ready, 1)
            sp.dma_start(top_dram, top_i[:, 0:TOPK]).then_inc(top_moved, 16)
            sp.wait_ge(top_moved, 16)
            sp.dma_start(idx[:, :], top_dram.rearrange("(o b) k -> o (b k)", o=1)).then_inc(top_moved, 16)
            sp.wait_ge(top_moved, 32)
            with nc.sync.Fori(0, B) as n:
                for k in range(TOPK):
                    e = nc.sync.value_load(idx[0:1, bass.ds(n * TOPK + k, 1)], min_val=0, max_val=NE - 1)
                    if k == 0:
                        sp.wait_ge(h_ready.sem, h_ready.at(n, 0))
                    sp.dma_start(w1_e[:, k, :], w1[bass.ds(e, 1)].rearrange("o d f -> (o d) f")).then_inc(e_w1_in.sem, 16)
                    sp.dma_start(b1_e[:, k, :], b1[bass.ds(e, 1)].rearrange("o p c -> (o p) c")).then_inc(e_w1_in.sem, 16)
                    if k == 0:
                        sp.wait_ge(e_w2_scaled.sem, e_w2_scaled.at(n, 0))
                    sp.dma_start(w2_e[:, k, :, :], w2[bass.ds(e, 1)].rearrange("o (c p) d -> (o p) c d", p=P)).then_inc(e_w2_in.sem, 16)
                    sp.dma_start(b2_e[:, k, :], b2[bass.ds(e, 1)]).then_inc(e_w2_in.sem, 16)
                sp.wait_ge(fin_ready.sem, fin_ready.at(n, 1))
                sp.dma_start(out_v[bass.ds(n, 1)].rearrange("o p k c -> (o p) k c"), o_rms[:, :, :]).then_inc(out_stored.sem, 16)
            sp.wait_ge(out_stored.sem, out_stored.at(B, 0))

        @block.gpsimd
        def _(pool):
            nc.gpsimd.memset(w_xp_sb[:, :, :], 0.0)
            nc.gpsimd.memset(w_dt_sb[:, :], 0.0).then_inc(weights_set, 1)
            nc.gpsimd.memset(ones[:, :], 1.0)
            nc.gpsimd.memset(neg_half[:, :], -0.5)
            pool_order.after(pool, 0, nc.gpsimd.memset(ident[:, :], 0.0))
            nc.gpsimd.affine_select(out=ident[:, :], in_=ident[:, :], compare_op=ALU.not_equal, fill=1.0,
                                    base=0, pattern=[[-1, P]], channel_multiplier=1)
            pool_order.after(pool, 0, nc.gpsimd.memset(group_avg[:, :], 1.0 / GROUP))
            ga = group_avg[:, :].rearrange("p (g i) -> p g i", i=GROUP)
            pool_order.after(pool, 0, nc.gpsimd.affine_select(
                out=ga, in_=ga, compare_op=ALU.is_ge, fill=0.0, base=0,
                pattern=[[-GROUP, P // GROUP], [0, GROUP]], channel_multiplier=1))
            nc.gpsimd.affine_select(out=ga, in_=ga, compare_op=ALU.is_ge, fill=0.0, base=GROUP - 1,
                                    pattern=[[GROUP, P // GROUP], [0, GROUP]],
                                    channel_multiplier=-1).then_inc(consts_pool, 1)

            with nc.gpsimd.Fori(0, B) as n:
                pool.wait_ge(gvar_ready.sem, gvar_ready.at(n, 1))
                nc.gpsimd.tensor_tensor(grp[:, 4:5], grp[:, 3:4], neg_half[:, 0:1], ALU.pow).then_inc(pool_pow.sem, 1)
                pool.wait_ge(u_tok_ready.sem, u_tok_ready.at(n, 1))
                pool.wait_ge(b_tok_ready.sem, b_tok_ready.at(n, 1))
                for i in range(NSTEP):
                    ck, s = divmod(i, NS)
                    if i >= 2:
                        pool.wait_ge(dbuT_up.sem, dbuT_up.at(n, i - 1))
                    nc.gpsimd.tensor_tensor(dbu_tok[:, i % 2, :, :], u_tok[:, :, ck * P:(ck + 1) * P],
                                            b_tok[:, :, s:s + 1].to_broadcast([P, NST, P]),
                                            ALU.mult).then_inc(dbu_ready.sem, 1)
                for i in range(3):
                    pool.wait_ge(var_ready.sem, var_ready.at(n, i + 1))
                    nc.gpsimd.tensor_tensor(tok_r[:, 2, :], tok_r[:, 1, :], neg_half[0:TT, 0:NT],
                                            ALU.pow).then_inc(pool_pow.sem, 1)

            with nc.gpsimd.Fori(0, B) as n:
                for i in range(2):
                    pool.wait_ge(f_var.sem, f_var.at(n, i + 1))
                    nc.gpsimd.tensor_tensor(tok_r[:, 2, :], tok_r[:, 1, :], neg_half[0:TT, 0:NT],
                                            ALU.pow).then_inc(f_pow.sem, 1)
                pool.wait_ge(lnf_ready.sem, lnf_ready.at(n, 1))
                pool.wait_ge(out_stored.sem, out_stored.at(n, 0))
                pool_order_e.count = 0
                pool_order_e.after(pool, n, nc.gpsimd.tensor_tensor(
                    o_rms[:, :, :], ln_tok[:, :, :], gamma_sb[:, :].unsqueeze(1).to_broadcast([TT, NT, C]), ALU.mult))
                pool_order_e.after(pool, n, nc.gpsimd.tensor_tensor(
                    o_rms[:, :, :], o_rms[:, :, :], beta_sb[:, :].unsqueeze(1).to_broadcast([TT, NT, C]), ALU.add))
                nc.gpsimd.tensor_tensor(o_rms[:, :, :], o_rms[:, :, :],
                                        t2[:, bass.ds(n, 1), :, :].rearrange("p o k c -> p (o k) c"),
                                        ALU.add).then_inc(fin_ready.sem, 1)

        @block.scalar
        def _(act):
            act.wait_ge(weights_in, NW[0])
            act_order.after(act, 0, nc.scalar.activation(a_sb[:, :, :], a_sb[:, :, :], ACT.Exp))
            nc.scalar.mul(a_sb[:, :, :], a_sb[:, :, :], -1.0).then_inc(a_exp, 1)
            act.wait_ge(a_exp, 1)

            def in_jt(ap):
                return ap.rearrange("p (j t) -> p t j", j=J)

            def by_tj(ap):
                return ap.rearrange("p (t j) -> p t j", j=J)

            with nc.scalar.Fori(0, B) as n:
                for ck in range(NC_):
                    act.wait_ge(conv_done.sem, conv_done.at(n, ck + 1))
                    nc.scalar.activation(in_jt(xc[:, ck, :]), by_tj(conv_acc[:, ck, :]), ACT.Silu).then_inc(silu_done.sem, 1)
                for ck in range(NC_):
                    act.wait_ge(xz_up.sem, xz_up.at(n, NC_ + ck + 1))
                    nc.scalar.activation(in_jt(z_act[:, ck, :]), by_tj(wide([6, 0][ck])), ACT.Silu).then_inc(silu_done.sem, 1)
                act.wait_ge(bT_up.sem, bT_up.at(n, 1))
                nc.scalar.copy(b_tok[:, 0:NST - 1, :], bank(6, (NST - 1) * 32).rearrange("p (k s) -> p k s", s=32)[:, :, RANK:32])
                nc.scalar.copy(b_tok[0:32, NST - 1, :], PS[0:32, 6 * BANK + (NST - 1) * 32 + RANK:6 * BANK + NST * 32]
                               ).then_inc(b_tok_ready.sem, 1)
                for ck in range(NC_):
                    act.wait_ge(dt_up.sem, dt_up.at(n, ck + 1))
                    nc.scalar.activation(sp_e[:, ck, :], wide([0, 2][ck]), ACT.Abs, bias=b_dt_sb[:, ck:ck + 1]).then_inc(dt_abs.sem, 1)
                act.wait_ge(dt_abs.sem, dt_abs.at(n, NC_))
                nc.scalar.activation(sp_e, sp_e, ACT.Exp, scale=-1.0).then_inc(sp_exp.sem, 1)
                act.wait_ge(sp_exp.sem, sp_exp.at(n, 1))
                nc.scalar.activation(sp_l, sp_e, ACT.Ln, bias=1.0).then_inc(sp_ln.sem, 1)
                act.wait_ge(uT_up.sem, uT_up.at(n, 1))
                nc.scalar.copy(u_tok[:, 0:NST - 1, :], PS[:, 4 * BANK:4 * BANK + (NST - 1) * DI].rearrange("p (k d) -> p k d", d=DI))
                nc.scalar.copy(u_tok[0:32, NST - 1, :], PS[0:32, 4 * BANK + (NST - 1) * DI:4 * BANK + NST * DI]
                               ).then_inc(u_tok_ready.sem, 1)
                for i in range(NSTEP):
                    ck, s = divmod(i, NS)
                    if i >= 2:
                        act.wait_ge(scan_done.sem, scan_done.at(n, i - 1))
                    nc.scalar.activation(dA[:, i % 2, :].rearrange("p (j t) -> p j t", t=T)[:, :, 1:T],
                                         dt_sb[:, ck, :].rearrange("p (j t) -> p j t", t=T)[:, :, 1:T],
                                         ACT.Exp, scale=a_sb[:, ck, s:s + 1]).then_inc(dA_ready.sem, 1)
                act.wait_ge(out_up.sem, out_up.at(n, 1))
                nc.scalar.activation(sq[:, :, :], PS[0:TT, 2 * BANK:4 * BANK].rearrange("p (k c) -> p k c", c=C), ACT.Square).then_inc(rms_sq.sem, 1)
                act.wait_ge(q_up.sem, q_up.at(n, 1))
                nc.scalar.copy(q_part[:, 0, :], wide(6)).then_inc(qk_first.sem, 1)
                act.wait_ge(k_up.sem, k_up.at(n, 1))
                nc.scalar.copy(k_part[:, 0, :], wide(0)).then_inc(qk_first.sem, 1)
                act.wait_ge(v_up.sem, v_up.at(n, 1))
                act.wait_ge(v_ready.sem, v_ready.at(n, 1))
                nc.scalar.copy(v_ext[:, 0:NST - 1, :, 0:HD],
                               PS[:, 2 * BANK:2 * BANK + (NST - 1) * C].rearrange("p (k h d) -> p k h d", k=NST - 1, h=H))
                nc.scalar.copy(v_ext[0:32, NST - 1, :, 0:HD],
                               PS[0:32, 2 * BANK + (NST - 1) * C:2 * BANK + NST * C].rearrange("p (h d) -> p h d", h=H)
                               ).then_inc(v_copied.sem, 1)
                for i in range(NPAIR):
                    rows = ST[i // 2 % NST][1]
                    act.wait_ge(s_up.sem, s_up.at(n, i + 1))
                    if i >= 4:
                        act.wait_ge(pv_up.sem, pv_up.at(n, i - 3))
                    nc.scalar.activation(probs[0:rows, i % 4, :, :], halves(2 * (i % 3))[0:rows], ACT.Exp,
                                         scale=ATT_SCALE).then_inc(probs_ready.sem, 1)

            for i in range(3):
                act.wait_ge(rt_ready, i + 1)
                src, dst, cols = [(rt[:, 1, :], rt[:, 2, :], NE), (rt[:, 5, :], rt[:, 6, :], NE),
                                  (top_w[:, 0:1], top_w[:, 1:2], 1)][i]
                nc.scalar.activation(dst, src, ACT.Exp).then_inc(rt_exp, 1)

            with nc.scalar.Fori(0, B) as n:
                act.wait_ge(e_w1_in.sem, e_w1_in.at(n, 16 * 2 * TOPK))
                for i in range(TOPK * FC):
                    k, fc = divmod(i, FC)
                    act.wait_ge(h_up.sem, h_up.at(n, i + 1))
                    nc.scalar.activation(hidden[:, i, :], wide(2 * i), ACT.Gelu, bias=b1_e[:, k, fc:fc + 1]).then_inc(h_ready.sem, 1)

        @block.vector
        def _(dve):
            for signal in freed:
                dve.sem_inc(signal.sem, 1)
            nc.vector.memset(dA[:, :, :], 0.0)
            nc.vector.memset(b_tok[:, :, :], 0.0)
            nc.vector.memset(u_tok[:, :, :], 0.0)
            nc.vector.memset(k_stack[KST:KST + 3, :, :], 1.0)
            dve.wait_ge(consts_pool, 1)
            first = nc.vector.tensor_copy(pick_c[:, :, :], ident[0:C_ROWS, 0:NS].unsqueeze(2).to_broadcast([C_ROWS, NS, P]))
            dve_order_rt.after(dve, 0, first)
            for q in range(1, 3):
                last = nc.vector.tensor_tensor(pick_c[:, :, :], pick_c[:, :, :],
                                               ident[0:C_ROWS, 32 * q:32 * q + NS].unsqueeze(2).to_broadcast([C_ROWS, NS, P]),
                                               ALU.add)
                dve_order_rt.after(dve, 0, last)
            nc.vector.memset(w_diag[:, :, :], 0.0).then_inc(consts_dve, 1)
            dve.wait_ge(weights_in, NW[0])

            def token_norm(turn, order, src, dst, eps, var_sig, k_var, pow_sig, k_pow, done):
                for k in range(NT):
                    last = nc.vector.bn_stats(tok_stats[:, k, :], src[:, k, :])
                order.after(dve, turn, last)
                even_m, even_m2, odd_m, odd_m2 = (tok_stats[:, :, c] for c in (1, 2, 4, 5))
                nc.vector.tensor_tensor(tok_mv[:, 0, :], even_m, odd_m, ALU.add)
                nc.vector.tensor_tensor(tok_mv[:, 1, :], even_m, odd_m, ALU.subtract)
                order.after(dve, turn, nc.vector.tensor_tensor(tok_mv[:, 2, :], even_m2, odd_m2, ALU.add))
                nc.vector.tensor_scalar(tok_mv[:, 0, :], tok_mv[:, 0, :], 0.5, None, ALU.mult)
                nc.vector.scalar_tensor_tensor(tok_mv[:, 1, :], tok_mv[:, 1, :], 0.25, tok_mv[:, 1, :], ALU.mult, ALU.mult)
                order.after(dve, turn, nc.vector.tensor_scalar(tok_mv[:, 2, :], tok_mv[:, 2, :], 1.0 / C, eps, ALU.mult, ALU.add))
                nc.vector.tensor_tensor(tok_r[:, 1, :], tok_mv[:, 2, :], tok_mv[:, 1, :], ALU.add).then_inc(var_sig.sem, 1)
                dve.wait_ge(pow_sig.sem, pow_sig.at(turn, k_pow))
                for k in range(NT):
                    last = nc.vector.tensor_scalar(dst[:, k, :], src[:, k, :], tok_mv[:, 0, k:k + 1], tok_r[:, 2, k:k + 1],
                                                   ALU.subtract, ALU.mult)
                last.then_inc(done.sem, 1)

            with nc.vector.Fori(0, B) as n:
                dve_order.count = 0

                def then(ins):
                    dve_order.after(dve, n, ins)

                dve.wait_ge(xT_up.sem, xT_up.at(n, 1))
                nc.vector.bn_stats(chan_stats[:, 0, :], bank(0, HALF))
                nc.vector.bn_stats(chan_stats[:, 1, :], bank(1, HALF)).then_inc(chan_ready.sem, 1)
                dve.wait_ge(gmean_up.sem, gmean_up.at(n, 1))
                then(nc.vector.reduce_sum(grp[:, 1:2], bank(2, NPART), X))
                then(nc.vector.tensor_scalar(grp[:, 0:1], grp[:, 1:2], 1.0 / NPART, None, ALU.mult))
                then(nc.vector.tensor_scalar(part_dev[:, :], part_mean, grp[:, 0:1], None, ALU.subtract))
                then(nc.vector.tensor_tensor(part_dev[:, :], part_dev[:, :], part_dev[:, :], ALU.mult))
                nc.vector.scalar_tensor_tensor(part_dev[:, :], part_m2, float(NPART) / TOK, part_dev[:, :],
                                               ALU.mult, ALU.add).then_inc(gdev_ready.sem, 1)
                dve.wait_ge(gvar_up.sem, gvar_up.at(n, 1))
                then(nc.vector.reduce_sum(grp[:, 2:3], bank(3, NPART), X))
                nc.vector.tensor_scalar(grp[:, 3:4], grp[:, 2:3], 1.0 / NPART, 1e-5, ALU.mult, ALU.add).then_inc(gvar_ready.sem, 1)
                dve.wait_ge(pool_pow.sem, pool_pow.at(n, 1))
                nc.vector.tensor_scalar(xnT[:, :].rearrange("p (a t) -> p a t", a=2), halves(0), grp[:, 0:1], grp[:, 4:5],
                                        ALU.subtract, ALU.mult).then_inc(xn_ready.sem, 1)

                for ck in range(NC_):
                    dve.wait_ge(xz_up.sem, xz_up.at(n, ck + 1))
                    src = wide(2 + 2 * ck)
                    then(nc.vector.tensor_scalar(conv_acc[:, ck, :], src, conv_w_sb[:, ck, TAPS - 1:TAPS],
                                                 conv_b_sb[:, ck:ck + 1], ALU.mult, ALU.add))
                    for back in range(1, TAPS):
                        ins = nc.vector.scalar_tensor_tensor(
                            conv_acc[:, ck, back * J:], src[:, 0:TOK - back * J],
                            conv_w_sb[:, ck, TAPS - 1 - back:TAPS - back], conv_acc[:, ck, back * J:], ALU.mult, ALU.add)
                        if back < TAPS - 1:
                            then(ins)
                    ins.then_inc(conv_done.sem, 1)

                dve.wait_ge(gn_tok_up.sem, gn_tok_up.at(n, 1))
                nc.vector.tensor_tensor(t1[:, :, :], x_tok[:, :, :],
                                        PS[0:TT, 2 * BANK:4 * BANK].rearrange("p (k c) -> p k c", c=C), ALU.add).then_inc(xs_ready.sem, 1)

                dve.wait_ge(xd_up.sem, xd_up.at(n, 1))
                nc.vector.tensor_copy(xd[:, :], wide(4)).then_inc(xd_ready.sem, 1)
                dve.wait_ge(xd_ready.sem, xd_ready.at(n, 1))
                then(nc.vector.tensor_copy(c_parts[:, :], xd[0:C_ROWS, :]))
                then(nc.vector.tensor_tensor(c_rest[:, :], xd[0:C_ROWS, :], c_parts[:, :], ALU.subtract))
                nc.vector.tensor_copy(c_parts[32:64, :], c_rest[32:64, :])
                then(nc.vector.tensor_copy(c_mid[64:96, :], c_rest[64:96, :]))
                nc.vector.tensor_tensor(c_parts[64:96, :], c_rest[64:96, :], c_mid[64:96, :], ALU.subtract).then_inc(c_ready.sem, 1)

                for ck in range(NC_):
                    dve.wait_ge(dt_abs.sem, dt_abs.at(n, ck + 1))
                    ins = nc.vector.tensor_scalar(dt_sb[:, ck, :], wide([0, 2][ck]), b_dt_sb[:, ck:ck + 1], 0.0, ALU.add, ALU.max)
                    ins.then_inc(dt_relu.sem, 1)
                dve.wait_ge(sp_exp.sem, sp_exp.at(n, 1))
                then(nc.vector.tensor_scalar(conv_acc, sp_e, 1.0, 1.0, ALU.add, ALU.subtract))
                then(nc.vector.tensor_tensor(conv_acc, sp_e, conv_acc, ALU.subtract))
                dve.wait_ge(dt_relu.sem, dt_relu.at(n, NC_))
                dve.wait_ge(sp_ln.sem, sp_ln.at(n, 1))
                then(nc.vector.tensor_tensor(conv_acc, conv_acc, sp_l, ALU.add))
                nc.vector.tensor_tensor(dt_sb, dt_sb, conv_acc, ALU.add).then_inc(dt_ready.sem, 1)
                dve.wait_ge(dt_ready.sem, dt_ready.at(n, 1))
                nc.vector.tensor_tensor(sp_l, dt_sb, xc, ALU.mult).then_inc(u_ready.sem, 1)

                for i in range(NSTEP):
                    ck, s = divmod(i, NS)
                    dve.wait_ge(dA_ready.sem, dA_ready.at(n, i + 1))
                    dve.wait_ge(dbuT_up.sem, dbuT_up.at(n, i + 1))
                    nc.vector.tensor_tensor_scan(hst[:, i % 2, :], dA[:, i % 2, :], wide(2 + 2 * (i % 2)), 0.0,
                                                 ALU.mult, ALU.add).then_inc(scan_done.sem, 1)
                    dve.wait_ge(cb_up.sem, cb_up.at(n, i + 1))
                    if i >= 2:
                        dve.wait_ge(y_up.sem, y_up.at(n, i - 1))
                    dve.wait_ge(scan_done.sem, scan_done.at(n, i + 1))
                    nc.vector.tensor_tensor(g[:, i % 2, :], hst[:, i % 2, :], wide(6), ALU.mult).then_inc(g_ready.sem, 1)
                    if s == NS - 1:
                        dve.wait_ge(y_up.sem, y_up.at(n, i + 1))
                        then(nc.vector.scalar_tensor_tensor(xc[:, ck, :], xc[:, ck, :], d_skip_sb[:, ck:ck + 1], wide(0),
                                                            ALU.mult, ALU.add))
                        nc.vector.tensor_tensor(conv_acc[:, ck, :].rearrange("p (t j) -> p j t", j=J),
                                                xc[:, ck, :].rearrange("p (j t) -> p j t", j=J),
                                                z_act[:, ck, :].rearrange("p (j t) -> p j t", j=J),
                                                ALU.mult).then_inc(y_ready.sem, 1)

                dve.wait_ge(rms_sq.sem, rms_sq.at(n, 1))
                then(nc.vector.reduce_sum(tok_r[:, 0, :], sq[:, :, :], X))
                nc.vector.tensor_scalar(tok_r[:, 1, :], tok_r[:, 0, :], 1.0 / C, 1e-6, ALU.mult, ALU.add).then_inc(var_ready.sem, 1)
                dve.wait_ge(pool_pow.sem, pool_pow.at(n, 2))
                then(nc.vector.tensor_tensor(o_rms[:, :, :], PS[0:TT, 2 * BANK:4 * BANK].rearrange("p (k c) -> p k c", c=C),
                                             tok_r[:, 2, :].unsqueeze(2).to_broadcast([TT, NT, C]), ALU.mult))
                then(nc.vector.tensor_tensor(o_rms[:, :, :], o_rms[:, :, :],
                                             ln_w_sb[:, :].unsqueeze(1).to_broadcast([TT, NT, C]), ALU.mult))
                then(nc.vector.tensor_tensor(t1[:, :, :], t1[:, :, :], o_rms[:, :, :], ALU.add))
                token_norm(n, dve_order, t1, ln_tok, 1e-5, var_ready, 2, pool_pow, 3, ln1_ready)
                dve.wait_ge(ln1T_up.sem, ln1T_up.at(n, 1))
                nc.vector.tensor_copy(lnT[:, :].rearrange("p (a t) -> p a t", a=2), halves(4)).then_inc(ln1T_ready.sem, 1)

                nc.vector.memset(v_ext[:, 0:NST - 1, :, :], 1.0)
                then(nc.vector.memset(v_ext[:, NST - 1, :, :], 0.0))
                nc.vector.memset(v_ext[0:ST[-1][1], NST - 1, :, :], 1.0).then_inc(v_ready.sem, 1)
                for i, (part, b) in enumerate(((q_part, 6), (k_part, 0))):
                    dve.wait_ge(qk_first.sem, qk_first.at(n, i + 1))
                    then(nc.vector.tensor_tensor(part_rest[:, :], wide(b), part[:, 0, :], ALU.subtract))
                    then(nc.vector.tensor_copy(part[:, 1, :], part_rest[:, :]))
                    nc.vector.tensor_tensor(part[:, 2, :], part_rest[:, :], part[:, 1, :], ALU.subtract).then_inc(qk_parts.sem, 1)
                    dve.wait_ge(qk_parts.sem, qk_parts.at(n, i + 1))

                for i in range(NMAX):
                    kt, hp = divmod(i, H // 2)
                    rows = ST[kt][1]
                    dve.wait_ge(smax_up.sem, smax_up.at(n, i + 1))
                    nc.vector.tensor_reduce(q_max[0:rows, kt, 2 * hp:2 * hp + 2], head_pair(4 * ((i + 1) % 2))[0:rows], axis=X,
                                            op=ALU.max, negate=True).then_inc(smax_read.sem, 1)
                dve.wait_ge(maxT_up.sem, maxT_up.at(n, 1))
                then(nc.vector.tensor_copy(m_row[:, :], PS[0:H, 0:TOK]))
                then(nc.vector.tensor_copy(m_part[:, 0, :], m_row[:, :]))
                then(nc.vector.tensor_tensor(m_rest[:, :], m_row[:, :], m_part[:, 0, :], ALU.subtract))
                then(nc.vector.tensor_copy(m_part[:, 1, :], m_rest[:, :]))
                nc.vector.tensor_tensor(m_part[:, 2, :], m_rest[:, :], m_part[:, 1, :], ALU.subtract).then_inc(m_parts.sem, 1)

                for i in range(4):
                    dve.wait_ge(pv_up.sem, pv_up.at(n, (i + 1) * 2 * NST))
                    nc.vector.tensor_copy(o_raw[:, i // 2, (i % 2) * HALF:(i % 2 + 1) * HALF],
                                          bank(6 + i % 2, HALF)).then_inc(o_copied.sem, 1)
                dve.wait_ge(oTok_up.sem, oTok_up.at(n, 1))
                for b in range(4):
                    src = PS[0:TT, b * BANK:(b + 1) * BANK].rearrange("p (k d) -> p k d", d=32)
                    last = nc.vector.reciprocal(o_rec[:, 16 * b:16 * (b + 1)], src[:, :, HD])
                then(last)
                for b in range(4):
                    src = PS[0:TT, b * BANK:(b + 1) * BANK].rearrange("p (k d) -> p k d", d=32)
                    rec = o_rec[:, 16 * b:16 * (b + 1)].unsqueeze(2).to_broadcast([TT, 16, HD])
                    last = nc.vector.tensor_tensor(o_tok[:, :, 2 * b:2 * b + 2, :].rearrange("p h i d -> p i h d"),
                                                   src[:, :, 0:HD].rearrange("p (i h) d -> p i h d", h=H),
                                                   rec.rearrange("p (i h) d -> p i h d", h=H), ALU.mult)
                last.then_inc(o_tok_ready.sem, 1)
                dve.wait_ge(oT_up.sem, oT_up.at(n, 1))
                nc.vector.tensor_copy(oT[:, :].rearrange("p (a t) -> p a t", a=2), halves(4)).then_inc(oT_ready.sem, 1)
                dve.wait_ge(proj_up.sem, proj_up.at(n, 1))
                then(nc.vector.scalar_tensor_tensor(t1[:, :, :].rearrange("p k c -> p (k c)"), PS[0:TT, 6 * BANK:8 * BANK], 0.0,
                                                    t1[:, :, :].rearrange("p k c -> p (k c)"), ALU.max, ALU.add))
                nc.vector.tensor_copy(t2[:, bass.ds(n, 1), :, :].rearrange("p o k c -> p (o k) c"), t1[:, :, :]).then_inc(t2_ready.sem, 1)
                token_norm(n, dve_order, t1, ln_tok, 1e-5, var_ready, 3, pool_pow, 4, ln2_ready)
                dve.wait_ge(mean_up.sem, mean_up.at(n, 1))
                nc.vector.tensor_scalar(x_mean[:, bass.ds(n, 1)], bank(0, 1), 1.0 / TOK, None, ALU.mult).then_inc(mean_read.sem, 1)
            assert dve_order.count == dve_order.per_turn, dve_order.count

            def rthen(ins):
                dve_order_rt.after(dve, 0, ins)

            dve.wait_ge(mean_read.sem, mean_read.at(B, 0))
            dve.wait_ge(logits_up, 1)
            rthen(nc.vector.tensor_copy(rt[:, 0, :], PS[0:B, 0:NE]))
            rthen(nc.vector.tensor_reduce(rt[:, 14, 0:1], rt[:, 0, :], axis=X, op=ALU.max))
            nc.vector.tensor_scalar(rt[:, 1, :], rt[:, 0, :], rt[:, 14, 0:1], None, ALU.subtract).then_inc(rt_ready, 1)
            dve.wait_ge(rt_exp, 1)
            rthen(nc.vector.reduce_sum(rt[:, 14, 1:2], rt[:, 2, :], X))
            rthen(nc.vector.reciprocal(rt[:, 14, 2:3], rt[:, 14, 1:2]))
            nc.vector.tensor_scalar(rt[:, 3, :], rt[:, 2, :], rt[:, 14, 2:3], None, ALU.mult).then_inc(top_ready_rw, 1)
            dve.wait_ge(loads_up, 1)
            rthen(nc.vector.tensor_scalar(rt[:, 7, :], PS[0:B, BANK:BANK + NE], float(TOK), None, ALU.mult))
            rthen(nc.vector.reciprocal(rt[:, 8, :], rt[:, 7, :]))
            rthen(nc.vector.tensor_scalar(rt[:, 9, :], rt[:, 8, :], CAPACITY, 1.0, ALU.mult, ALU.min))
            rthen(nc.vector.tensor_tensor(rt[:, 4, :], rt[:, 3, :], rt[:, 9, :], ALU.mult))
            rthen(nc.vector.tensor_reduce(rt[:, 14, 3:4], rt[:, 4, :], axis=X, op=ALU.max))
            nc.vector.tensor_scalar(rt[:, 5, :], rt[:, 4, :], rt[:, 14, 3:4], None, ALU.subtract).then_inc(rt_ready, 1)
            dve.wait_ge(rt_exp, 2)
            rthen(nc.vector.reduce_sum(rt[:, 14, 4:5], rt[:, 6, :], X))
            rthen(nc.vector.reciprocal(rt[:, 14, 5:6], rt[:, 14, 4:5]))
            rthen(nc.vector.tensor_scalar(rt[:, 10, :], rt[:, 6, :], rt[:, 14, 5:6], None, ALU.mult))
            rthen(nc.vector.max(top_v[:, :], rt[:, 10, :]))
            nc.vector.max_index(top_i[:, :], top_v[:, :], rt[:, 10, :]).then_inc(top_ready, 1)
            nc.vector.tensor_tensor(top_w[:, 0:1], top_v[:, 1:2], top_v[:, 0:1], ALU.subtract).then_inc(rt_ready, 1)
            dve.wait_ge(rt_exp, 3)
            rthen(nc.vector.tensor_scalar(top_w[:, 2:3], top_w[:, 1:2], 1.0, None, ALU.add))
            rthen(nc.vector.reciprocal(top_w[:, 2:3], top_w[:, 2:3]))
            rthen(nc.vector.tensor_tensor(top_w[:, 3:4], top_w[:, 1:2], top_w[:, 2:3], ALU.mult))
            for k in range(TOPK):
                last = nc.vector.tensor_scalar(w_diag[:, :, k], ident[0:B, 0:B], top_w[:, 2 + k:3 + k], None, ALU.mult)
            last.then_inc(w_diag_ready, 1)
            dve.wait_ge(w_all_up, 1)
            nc.vector.tensor_copy(w_all[:, :], bank(2, B * TOPK)).then_inc(w_all_ready, 1)
            dve.wait_ge(w_all_ready, 1)

            with nc.vector.Fori(0, B) as n:
                dve_order_e.count = 0

                def ethen(ins):
                    dve_order_e.after(dve, n, ins)

                dve.wait_ge(lnf_ready.sem, lnf_ready.at(n, 0))
                ethen(nc.vector.tensor_copy(t1[:, :, :], t2[:, bass.ds(n, 1), :, :].rearrange("p o k c -> p (o k) c")))
                token_norm(n, dve_order_e, t1, o_tok_v, 1e-5, f_var, 1, f_pow, 1, f_ready)
                dve.wait_ge(e_w2_in.sem, e_w2_in.at(n, 16 * 2 * TOPK))
                dve.wait_ge(y_e_up.sem, y_e_up.at(n, 0))
                ethen(nc.vector.tensor_scalar(b2_s[:, :], b2_e[:, 0, :], w_all[0:1, bass.ds(n * TOPK, 1)], None, ALU.mult))
                ethen(nc.vector.scalar_tensor_tensor(b2_s[:, :], b2_e[:, 1, :], w_all[0:1, bass.ds(n * TOPK + 1, 1)], b2_s[:, :],
                                                     ALU.mult, ALU.add))
                for k in range(TOPK):
                    last = nc.vector.tensor_scalar(w2_s[:, k, :, :], w2_e[:, k, :, :], w_all[:, bass.ds(n * TOPK + k, 1)],
                                                   None, ALU.mult)
                last.then_inc(e_w2_scaled.sem, 1)
                dve.wait_ge(fT_up.sem, fT_up.at(n, 1))
                nc.vector.tensor_copy(lnT[:, :].rearrange("p (a t) -> p a t", a=2), halves(0)).then_inc(fT_ready.sem, 1)
                dve.wait_ge(y_e_up.sem, y_e_up.at(n, 1))
                nc.vector.tensor_tensor(t1[:, :, :], o_tok_v, PS[0:TT, 2 * BANK:4 * BANK].rearrange("p (k c) -> p k c", c=C),
                                        ALU.add).then_inc(res_read.sem, 1)
                dve.wait_ge(res_read.sem, res_read.at(n, 1))
                dve.wait_ge(fin_ready.sem, fin_ready.at(n, 0))
                token_norm(n, dve_order_e, t1, ln_tok, 1e-5, f_var, 2, f_pow, 2, lnf_ready)
            assert dve_order_e.count == dve_order_e.per_turn, dve_order_e.count

        @block.tensor
        def _(pe):
            pe.wait_ge(consts_pool, 1)
            pe.wait_ge(consts_dve, 1)
            pe.wait_ge(weights_in, NW[0])

            def transposes_out(src, b, width=TT):
                for k in range(NT):
                    a, o = divmod(k * TT, HALF)
                    last = nc.tensor.transpose(PS[:, (b + a) * BANK + o:(b + a) * BANK + o + TT], src[:, k, :], ident[0:TT, 0:TT])
                return last

            def over_spans(b, lhsT, rhs, start=True, stop=True):
                for at, width in SPANS:
                    last = nc.tensor.matmul(PS[:, b * BANK + at:b * BANK + at + width], lhsT, rhs[:, at:at + width],
                                            start=start, stop=stop)
                return last

            with nc.tensor.Fori(0, B) as n:
                pe.wait_ge(x_in.sem, x_in.at(n, 16))
                pe.wait_ge(mean_read.sem, mean_read.at(n, 0))
                transposes_out(x_tok, 0).then_inc(xT_up.sem, 1)
                pe.wait_ge(chan_ready.sem, chan_ready.at(n, 1))
                nc.tensor.matmul(bank(2, NPART), group_avg[:, :], part_mean, start=True, stop=True).then_inc(gmean_up.sem, 1)
                pe.wait_ge(gdev_ready.sem, gdev_ready.at(n, 1))
                nc.tensor.matmul(bank(3, NPART), group_avg[:, :], part_dev[:, :], start=True, stop=True).then_inc(gvar_up.sem, 1)
                pe.wait_ge(xn_ready.sem, xn_ready.at(n, 1))
                for e, b in enumerate((2, 4, 6, 0)):
                    over_spans(b, w_in_sb[:, e * P:(e + 1) * P], xnT).then_inc(xz_up.sem, 1)
                pe.wait_ge(conv_done.sem, conv_done.at(n, 1))
                for k in range(NT):
                    last = nc.tensor.transpose(PS[0:TT, 2 * BANK + k * C:2 * BANK + (k + 1) * C], xnT[:, k * TT:(k + 1) * TT], ident[:, :])
                last.then_inc(gn_tok_up.sem, 1)
                pe.wait_ge(conv_done.sem, conv_done.at(n, 2))
                pe.wait_ge(silu_done.sem, silu_done.at(n, 2))
                for at, width in SPANS:
                    for ck in range(NC_):
                        last = nc.tensor.matmul(PS[:, 4 * BANK + at:4 * BANK + at + width], w_xp_sb[:, ck, :],
                                                xc[:, ck, at:at + width], start=(ck == 0), stop=(ck == NC_ - 1))
                last.then_inc(xd_up.sem, 1)
                pe.wait_ge(xd_ready.sem, xd_ready.at(n, 1))
                pe.wait_ge(silu_done.sem, silu_done.at(n, 4))
                over_spans(0, w_dt_sb[DT0:P, 0:P], xd[DT0:P, :]).then_inc(dt_up.sem, 1)
                pe.wait_ge(xs_ready.sem, xs_ready.at(n, 1))
                over_spans(2, w_dt_sb[DT0:P, P:2 * P], xd[DT0:P, :]).then_inc(dt_up.sem, 1)
                for k, (at, rows) in enumerate(ST):
                    last = nc.tensor.transpose(PS[0:rows, 6 * BANK + 32 * k:6 * BANK + 32 * (k + 1)], xd[DT0:P, at:at + rows],
                                               ident[DT0:P, DT0:P])
                last.then_inc(bT_up.sem, 1)
                pe.wait_ge(u_ready.sem, u_ready.at(n, 1))
                pe.wait_ge(b_tok_ready.sem, b_tok_ready.at(n, 1))
                for k, (at, rows) in enumerate(ST):
                    for ck in range(NC_):
                        o = 4 * BANK + k * DI + ck * P
                        last = nc.tensor.transpose(PS[0:rows, o:o + P], sp_l[:, ck, at:at + rows], ident[:, :])
                last.then_inc(uT_up.sem, 1)

                pe.wait_ge(c_ready.sem, c_ready.at(n, 1))
                pe.wait_ge(u_tok_ready.sem, u_tok_ready.at(n, 1))

                def sum_states(i):
                    ck, s = divmod(i, NS)
                    pe.wait_ge(g_ready.sem, g_ready.at(n, i + 1))
                    if s == 0 and ck:
                        pe.wait_ge(y_ready.sem, y_ready.at(n, ck))
                    over_spans(0, ident[:, :], g[:, i % 2, :], start=(s == 0), stop=(s == NS - 1)).then_inc(y_up.sem, 1)

                for i in range(NSTEP):
                    ck, s = divmod(i, NS)
                    pe.wait_ge(dbu_ready.sem, dbu_ready.at(n, i + 1))
                    if i >= 2:
                        pe.wait_ge(scan_done.sem, scan_done.at(n, i - 1))
                    for k, (at, rows) in enumerate(ST):
                        o = (2 + 2 * (i % 2)) * BANK + at
                        last = nc.tensor.transpose(PS[:, o:o + rows], dbu_tok[0:rows, i % 2, k, :], ident[0:rows, 0:rows])
                    last.then_inc(dbuT_up.sem, 1)
                    if i >= 1:
                        pe.wait_ge(g_ready.sem, g_ready.at(n, i))
                    over_spans(6, pick_c[:, s, :], c_parts).then_inc(cb_up.sem, 1)
                    if i >= 1:
                        sum_states(i - 1)
                sum_states(NSTEP - 1)

                pe.wait_ge(y_ready.sem, y_ready.at(n, NC_))
                for k in range(NT):
                    for ck in range(NC_):
                        last = nc.tensor.matmul(PS[0:TT, 2 * BANK + k * C:2 * BANK + (k + 1) * C], conv_acc[:, ck, k * TT:(k + 1) * TT],
                                                w_out_sb[:, ck, :], start=(ck == 0), stop=(ck == NC_ - 1))
                last.then_inc(out_up.sem, 1)
                pe.wait_ge(ln1_ready.sem, ln1_ready.at(n, 1))
                transposes_out(ln_tok, 4).then_inc(ln1T_up.sem, 1)
                pe.wait_ge(ln1T_ready.sem, ln1T_ready.at(n, 1))
                over_spans(6, w_qkv_sb[:, 0:C], lnT).then_inc(q_up.sem, 1)
                over_spans(0, w_qkv_sb[:, C:2 * C], lnT).then_inc(k_up.sem, 1)
                for k, (at, rows) in enumerate(ST):
                    last = nc.tensor.matmul(PS[0:rows, 2 * BANK + k * C:2 * BANK + (k + 1) * C], lnT[:, at:at + rows],
                                            w_qkv_sb[:, 2 * C:3 * C], start=True, stop=True)
                last.then_inc(v_up.sem, 1)

                pe.wait_ge(stacks_in.sem, stacks_in.at(n, 16 * NSTK))
                for i in range(NMAX):
                    kt, hp = divmod(i, H // 2)
                    at, rows = ST[kt]
                    if i == 1:
                        pe.wait_ge(v_copied.sem, v_copied.at(n, 1))
                    if i >= 2:
                        pe.wait_ge(smax_read.sem, smax_read.at(n, i - 1))
                    for a in range(2):
                        for o, width in SPANS:
                            last = nc.tensor.matmul(head_pair(4 * ((i + 1) % 2))[0:rows, a, o:o + width],
                                                    q_stack[0:KST, 2 * hp + a, at:at + rows],
                                                    k_stack[0:KST, 2 * hp + a, o:o + width], start=True, stop=True)
                    last.then_inc(smax_up.sem, 1)
                pe.wait_ge(smax_read.sem, smax_read.at(n, NMAX))
                for k, (at, rows) in enumerate(ST):
                    last = nc.tensor.transpose(PS[0:H, at:at + rows], q_max[0:rows, k, :], ident[0:rows, 0:rows])
                last.then_inc(maxT_up.sem, 1)

                pe.wait_ge(max_in.sem, max_in.at(n, 16 * 3))

                def times_v(i):
                    gq, rest = divmod(i, 2 * NST)
                    kt, hp = divmod(rest, 2)
                    pe.wait_ge(probs_ready.sem, probs_ready.at(n, i + 1))
                    if gq >= 2 and rest == 0:
                        pe.wait_ge(o_copied.sem, o_copied.at(n, gq - 1))
                    for a in range(2):
                        q = 2 * hp + a
                        h = 4 * (gq // 2) + q
                        last = nc.tensor.matmul(PS[32 * q:32 * (q + 1), (6 + gq % 2) * BANK:(6 + gq % 2) * BANK + HALF],
                                                v_ext[:, kt, h, :], probs[:, i % 4, a, :],
                                                start=(kt == 0), stop=(kt == NST - 1))
                    last.then_inc(pv_up.sem, 1)

                for i in range(NPAIR):
                    gq, rest = divmod(i, 2 * NST)
                    kt, hp = divmod(rest, 2)
                    at, rows = ST[kt]
                    q0 = (gq % 2) * HALF
                    if i >= 3:
                        pe.wait_ge(probs_ready.sem, probs_ready.at(n, i - 2))
                    for a in range(2):
                        h = 4 * (gq // 2) + 2 * hp + a
                        last = nc.tensor.matmul(halves(2 * (i % 3))[0:rows, a, :], k_stack[:, h, at:at + rows],
                                                q_stack[:, h, q0:q0 + HALF], start=True, stop=True)
                    last.then_inc(s_up.sem, 1)
                    if i >= 2:
                        times_v(i - 2)
                times_v(NPAIR - 2)
                times_v(NPAIR - 1)

                pe.wait_ge(o_copied.sem, o_copied.at(n, 4))
                for k in range(NT):
                    for gr in range(2):
                        o = k * 2 * P + gr * P
                        last = nc.tensor.transpose(PS[0:TT, o:o + P], o_raw[:, gr, k:TOK:NT], ident[:, :])
                last.then_inc(oTok_up.sem, 1)
                pe.wait_ge(o_tok_ready.sem, o_tok_ready.at(n, 1))
                transposes_out(o_tok_v, 4).then_inc(oT_up.sem, 1)
                pe.wait_ge(oT_ready.sem, oT_ready.at(n, 1))
                for k in range(NT):
                    o = 6 * BANK + k * C
                    nc.tensor.matmul(PS[0:TT, o:o + C], oT[:, k * TT:(k + 1) * TT], proj_w_sb[:, :], start=True, stop=False)
                    last = nc.tensor.matmul(PS[0:TT, o:o + C], ones[0:1, 0:TT], proj_b_sb[:, :], start=False, stop=True)
                last.then_inc(proj_up.sem, 1)
                pe.wait_ge(ln2_ready.sem, ln2_ready.at(n, 1))
                for k in range(NT):
                    last = nc.tensor.matmul(bank(0, 1), ln_tok[:, k, :], ones[0:TT, 0:1], start=(k == 0), stop=(k == NT - 1))
                last.then_inc(mean_up.sem, 1)

            pe.wait_ge(mean_read.sem, mean_read.at(B, 0))
            nc.tensor.matmul(PS[0:B, 0:NE], x_mean[:, :], w_r_sb[:, :], start=True, stop=False)
            nc.tensor.matmul(PS[0:B, 0:NE], ones[0:1, 0:B], b_r_sb[:, :], start=False, stop=True).then_inc(logits_up, 1)
            pe.wait_ge(top_ready_rw, 1)
            nc.tensor.matmul(PS[0:B, BANK:BANK + NE], ones[0:B, 0:B], rt[:, 3, :], start=True, stop=True).then_inc(loads_up, 1)
            pe.wait_ge(w_diag_ready, 1)
            nc.tensor.matmul(bank(2, B * TOPK), ones[0:B, :], w_diag[:, :, :].rearrange("p b k -> p (b k)"),
                             start=True, stop=True).then_inc(w_all_up, 1)
            pe.wait_ge(w_all_ready, 1)

            with nc.tensor.Fori(0, B) as n:
                pe.wait_ge(f_ready.sem, f_ready.at(n, 1))
                pe.wait_ge(h_ready.sem, h_ready.at(n, 0))
                transposes_out(o_tok_v, 0).then_inc(fT_up.sem, 1)
                pe.wait_ge(fT_ready.sem, fT_ready.at(n, 1))
                pe.wait_ge(e_w1_in.sem, e_w1_in.at(n, 16 * 2 * TOPK))
                pe.wait_ge(res_read.sem, res_read.at(n, 0))
                for i in range(TOPK * FC):
                    k, fc = divmod(i, FC)
                    over_spans(2 * i, w1_e[:, k, fc * P:(fc + 1) * P], lnT).then_inc(h_up.sem, 1)
                pe.wait_ge(h_ready.sem, h_ready.at(n, TOPK * FC))
                pe.wait_ge(e_w2_scaled.sem, e_w2_scaled.at(n, 1))
                for kt in range(NT):
                    o = 2 * BANK + kt * C
                    for i in range(TOPK * FC):
                        nc.tensor.matmul(PS[0:TT, o:o + C], hidden[:, i, kt * TT:(kt + 1) * TT], w2_s[:, i // FC, i % FC, :],
                                         start=(i == 0), stop=False)
                    last = nc.tensor.matmul(PS[0:TT, o:o + C], ones[0:1, 0:TT], b2_s[:, :], start=False, stop=True)
                last.then_inc(y_e_up.sem, 1)


_NAMES = ['x', 'L0_conv_W_in', 'L0_conv_conv_w', 'L0_conv_conv_b', 'L0_conv_W_xproj', 'L0_conv_W_dt', 'L0_conv_b_dt',
          'L0_conv_A_log', 'L0_conv_D_skip', 'L0_conv_W_out', 'L0_conv_ln_w', 'L1_attn_W', 'L1_attn_proj_w',
          'L1_attn_proj_b', 'L1_ffn_Wr', 'L1_ffn_br', 'L1_ffn_W1', 'L1_ffn_b1', 'L1_ffn_W2', 'L1_ffn_b2',
          'L1_ffn_gamma', 'L1_ffn_beta']
_TRANSPOSED = ('L0_conv_W_in', 'L0_conv_W_xproj', 'L0_conv_W_dt', 'L0_conv_W_out')

_BY_PARTITION = ('L0_conv_conv_b', 'L0_conv_b_dt', 'L0_conv_D_skip', 'L1_ffn_b1')


def kernel(**inputs):
    import numpy as _np
    import concourse.bacc as _bacc
    from concourse import mybir as _mybir
    from concourse.bass_utils import run_bass_kernel_spmd as _run

    nc = _bacc.Bacc("TRN2", target_bir_lowering=False, num_devices=1)
    arrays, args = {}, []
    for name in _NAMES:
        a = _np.asarray(inputs[name])
        if name in _TRANSPOSED:
            a = a.T
        if name in _BY_PARTITION:
            a = _np.swapaxes(a.reshape(*a.shape[:-1], -1, 128), -1, -2)
        a = _np.ascontiguousarray(a)
        arrays[f"in_{name}"] = a
        args.append(nc.dram_tensor(f"in_{name}", a.shape, _mybir.dt.from_np(a.dtype), kind="ExternalInput").ap())
    shape = arrays["in_x"].shape
    out = nc.dram_tensor("out_0", shape, _mybir.dt.float32, kind="ExternalOutput").ap()
    mamba_attention_moe(nc, *args, out)
    r = _run(nc, [arrays], core_ids=[0])
    return r.results[0]["out_0"]
```

```python
import concourse.bass as bass
from concourse import mybir
from contextlib import ExitStack


class Signal:

    def __init__(self, sem, per_turn, primed=0):
        self.sem = sem
        self.per_turn = per_turn
        self.primed = primed

    def at(self, turn, k):
        return turn * self.per_turn + k + self.primed


class Order:

    def __init__(self, sem, per_turn):
        self.sem = sem
        self.per_turn = per_turn
        self.count = 0

    def after(self, engine, turn, ins):
        self.count += 1
        ins.then_inc(self.sem, 1)
        engine.wait_ge(self.sem, turn * self.per_turn + self.count)


def mamba_attention_moe(nc, x, w_in_t, conv_w, conv_b, w_xp_t, w_dt_t, b_dt, a_log, d_skip, w_out_t,
                        ln_w, w_qkv, proj_w, proj_b, w_r, b_r, w1, b1, w2, b2, gamma, beta, out):
    f32 = mybir.dt.float32
    bf16 = mybir.dt.bfloat16
    u32 = mybir.dt.uint32
    ACT = mybir.ActivationFunctionType
    ALU = mybir.AluOpType
    X = mybir.AxisListType.X

    B, T, J, C = x.shape
    TOK = T * J
    P = 128
    GROUP = C // 32
    DI = w_out_t.shape[0]
    NC_ = DI // P
    NS = a_log.shape[1]
    TAPS = conv_w.shape[1]
    RANK = w_dt_t.shape[0]
    H = 8
    HD = C // H
    NE, _, F = w1.shape
    FC = F // P
    TOPK = 2
    TT = 100
    NT = TOK // TT
    HALF = TOK // 2
    ST = [(k * P, min(P, TOK - k * P)) for k in range((TOK + P - 1) // P)]
    NST = len(ST)
    BANK = 512
    SPANS = [(0, BANK), (BANK, TOK - BANK)]
    ATT_SCALE = float(C) ** -0.5
    CAPACITY = float(-(-(B * TOK * 5 // 4) // NE))
    Q_PARTS = [0, 0, 1, 1, 0, 2]
    K_PARTS = [0, 1, 0, 1, 2, 0]
    KST = len(Q_PARTS) * HD
    C_ROWS = 3 * 32
    DT0 = 96

    x_v = x.rearrange("n t j c -> n (t j) c").rearrange("n (k p) c -> n p k c", p=TT)
    out_v = out.rearrange("n t j c -> n (t j) c").rearrange("n (k p) c -> n p k c", p=TT)

    ctx = ExitStack()
    with ctx:
        def sb(name, shape, dt=f32):
            return ctx.enter_context(nc.sbuf_tensor(name, shape, dt))

        def sem(name):
            return ctx.enter_context(nc.semaphore(name))

        def sig(name, per_turn=1):
            return Signal(sem(name), per_turn)

        freed = []

        def freeing(name, per_turn=1):
            freed.append(Signal(sem(name), per_turn, primed=1))
            return freed[-1]

        w_in_sb = sb("w_in_sb", [P, 2 * DI])
        conv_w_sb = sb("conv_w_sb", [P, NC_, TAPS])
        conv_b_sb = sb("conv_b_sb", [P, NC_])
        w_xp_sb = sb("w_xp_sb", [P, NC_, P])
        w_dt_sb = sb("w_dt_sb", [P, DI])
        b_dt_sb = sb("b_dt_sb", [P, NC_])
        a_sb = sb("a_sb", [P, NC_, NS])
        d_skip_sb = sb("d_skip_sb", [P, NC_])
        w_out_sb = sb("w_out_sb", [P, NC_, C])
        ln_w_sb = sb("ln_w_sb", [TT, C])
        w_qkv_sb = sb("w_qkv_sb", [P, 3 * C])
        proj_w_sb = sb("proj_w_sb", [P, C])
        proj_b_sb = sb("proj_b_sb", [1, C])
        w_r_sb = sb("w_r_sb", [P, NE])
        b_r_sb = sb("b_r_sb", [1, NE])
        gamma_sb = sb("gamma_sb", [TT, C])
        beta_sb = sb("beta_sb", [TT, C])
        ident = sb("ident", [P, P])
        group_avg = sb("group_avg", [P, P])
        ones = sb("ones", [P, P])
        neg_half = sb("neg_half", [P, NT])
        pick_c = sb("pick_c", [C_ROWS, NS, P], bf16)
        x_mean = sb("x_mean", [P, B])

        def by_chunk(name):
            return sb(name, [P, NC_, TOK])

        x_tok = sb("x_tok", [TT, NT, C])
        chan_stats = sb("chan_stats", [P, 2, 6])
        NPART = 4
        part_mean = chan_stats[:, :, :].rearrange("p a (b c) -> p (a b) c", c=3)[:, :, 1]
        part_m2 = chan_stats[:, :, :].rearrange("p a (b c) -> p (a b) c", c=3)[:, :, 2]
        part_dev = sb("part_dev", [P, NPART])
        grp = sb("grp", [P, 6])
        xnT = sb("xnT", [P, TOK])
        conv_acc, z_act, xc, dt_sb, sp_e, sp_l = map(by_chunk, ("conv_acc", "z_act", "xc", "dt_sb", "sp_e", "sp_l"))
        xd = sb("xd", [P, TOK])
        c_mid = sb("c_mid", [C_ROWS, TOK], bf16)
        c_parts = sb("c_parts", [C_ROWS, TOK], bf16)
        NBB = 4
        b_all = sb("b_all", [P, NBB, TOK])
        dbu = sb("dbu", [P, 2, TOK])
        dA = sb("dA", [P, 2, TOK])
        hst = sb("hst", [P, 2, TOK])
        g = sb("g", [P, 2, TOK])
        x_sum = sb("x_sum", [TT, NT, C])
        rms_v = sb("rms_v", [TT, 3, NT])

        def over(tile, size, rows=P, **dims):
            spec = " ".join(dims)
            return tile[0:rows, :, :].rearrange("p a b -> p (a b)")[:, 0:size].rearrange(f"p ({spec}) -> p {spec}", **dims)

        sq = over(sp_e, NT * C, rows=TT, k=NT, c=C)
        o_rms = over(z_act, NT * C, rows=TT, k=NT, c=C)

        def norm_tiles(name):
            return {k: sb(f"{name}_{k}", [TT, a, NT]) if k != "stats" else sb(f"{name}_{k}", [TT, NT, a])
                    for k, a in (("stats", 6), ("mv", 3), ("r", 2))}

        norm1 = norm_tiles("norm1")
        norm2 = norm_tiles("norm2")
        t1 = sb("t1", [TT, NT, C])
        ln1_tok = sb("ln1_tok", [TT, NT, C])
        lnT = sb("lnT", [P, TOK])
        q_part = sb("q_part", [P, 3, TOK], bf16)
        k_part = sb("k_part", [P, 3, TOK], bf16)
        part_rest = sb("part_rest", [P, TOK])
        c_rest = part_rest[0:C_ROWS, :]
        v_ext = sb("v_ext", [P, NST, H, 32])
        NPROB = 4
        probs = sb("probs", [P, NPROB, HALF])
        q_stack = sb("q_stack", [KST + 3, H, TOK], bf16)
        k_stack = sb("k_stack", [KST + 3, H, TOK], bf16)
        q_max = sb("q_max", [P, NST, H])
        m_row = sb("m_row", [H, TOK])
        m_part = sb("m_part", [H, 3, TOK], bf16)
        o_raw = sb("o_raw", [P, 2, TOK])
        o_rec = sb("o_rec", [TT, NT * H])
        o_tok = sb("o_tok", [TT, H, NT, HD])
        oT = part_rest
        o_tok_v = o_tok[:, :, :, :].rearrange("p h i d -> p h (i d)")
        t2 = sb("t2", [TT, NT, C])
        f_tok = sb("f_tok", [TT, NT, C])
        fT = sb("fT", [P, TOK])
        w1_e = over(conv_acc, TOPK * F, k=TOPK, f=F)
        w2_e = over(dt_sb, TOPK * F, k=TOPK, a=FC, c=C)
        w2_s = over(xc, TOPK * F, k=TOPK, a=FC, c=C)
        hidden = [over(t, 2 * TOK, a=2, t=TOK)[:, i, :] for t in (sp_e, sp_l) for i in range(2)]
        b1_e = sb("b1_e", [P, TOPK, FC])
        b2_e = sb("b2_e", [1, TOPK, C])
        b2_s = sb("b2_s", [1, C])
        rt = sb("rt", [NE, 16, NE])
        top_v = sb("top_v", [B, 8])
        top_i = sb("top_i", [B, 8], u32)
        top_w = sb("top_w", [B, 4])
        w_diag = sb("w_diag", [B, B, TOPK])
        w_all = sb("w_all", [P, B * TOPK])
        idx = sb("idx", [1, B * TOPK], u32)

        PS = ctx.enter_context(nc.psum_tensor("PS", [P, 8 * BANK], f32))

        def bank(b, cols=BANK):
            return PS[:, b * BANK:b * BANK + cols]

        def wide(b):
            return PS[:, b * BANK:b * BANK + TOK]

        def halves(b):
            return PS[:, b * BANK:(b + 2) * BANK].rearrange("p (a t) -> p a t", a=2)[:, :, 0:HALF]

        def tokens(b):
            return PS[0:TT, b * BANK:(b + 2) * BANK].rearrange("p (k c) -> p k c", c=C)

        parts_dram = nc.dram_tensor("parts_dram", (2, P, 3, TOK), bf16).ap()
        max_dram = nc.dram_tensor("max_dram", (H, 3, TOK), bf16).ap()
        b_dram = nc.dram_tensor("b_dram", (NS, TOK), f32).ap()
        t2_dram = nc.dram_tensor("t2_dram", (B, TT, NT * C), f32).ap()
        f_dram = nc.dram_tensor("f_dram", (B, TT, NT * C), f32).ap()
        fT_dram = nc.dram_tensor("fT_dram", (B, P, TOK), f32).ap()
        top_dram = nc.dram_tensor("top_dram", (B, TOPK), u32).ap()

        weights_in = sem("weights_in")
        weights_set = sem("weights_set")
        consts_pool = sem("consts_pool")
        consts_dve = sem("consts_dve")
        a_exp = sem("a_exp")
        x_in = sig("x_in", 16)
        xT_up = sig("xT_up")
        chan_ready = sig("chan_ready")
        gmean_up = sig("gmean_up")
        gdev_ready = sig("gdev_ready")
        gvar_up = sig("gvar_up")
        gvar_ready = sig("gvar_ready")
        gstd_ready = sig("gstd_ready")
        xn_ready = sig("xn_ready")
        xz_up = sig("xz_up", 4)
        conv_done = sig("conv_done", 2)
        silu_done = sig("silu_done", 4)
        gn_tok_up = sig("gn_tok_up")
        xs_ready = freeing("xs_ready")
        xd_up = sig("xd_up")
        xd_ready = sig("xd_ready")
        b_out = sig("b_out", 16)
        dt_up = sig("dt_up", 2)
        dt_abs = sig("dt_abs", 2)
        dt_relu = sig("dt_relu", 2)
        sp_exp = sig("sp_exp")
        sp_ln = sig("sp_ln")
        dt_ready = sig("dt_ready")
        u_ready = sig("u_ready")
        c_ready = sig("c_ready")
        NSTEP = NC_ * NS
        b_in = [sig(f"b_in{k}", 16 * NSTEP // NBB) for k in range(NBB)]
        dbu_ready = sig("dbu_ready", NSTEP)
        dA_ready = sig("dA_ready", NSTEP)
        scan_done = sig("scan_done", NSTEP)
        cb_up = sig("cb_up", NSTEP)
        g_ready = sig("g_ready", NSTEP)
        y_up = sig("y_up", NSTEP)
        y_ready = sig("y_ready", NC_)
        out_up = sig("out_up")
        rms_sq = sig("rms_sq")
        ms_ready = sig("ms_ready")
        rms_ready = sig("rms_ready")
        ln1_var = sig("ln1_var")
        ln1_std = sig("ln1_std")
        ln1_ready = sig("ln1_ready")
        ln1T_up = sig("ln1T_up")
        ln1T_ready = freeing("ln1T_ready")
        q_up = sig("q_up")
        k_up = sig("k_up")
        v_up = sig("v_up")
        qk_first = sig("qk_first", 2)
        qk_parts = sig("qk_parts", 2)
        v_copied = sig("v_copied")
        parts_out = sig("parts_out", 32)
        NSTK = 2 * len(Q_PARTS)
        stacks_in = sig("stacks_in", 16 * NSTK)
        NMAX = NST * H
        smax_up = sig("smax_up", NMAX)
        smax_read = sig("smax_read", NMAX)
        maxT_up = sig("maxT_up")
        m_parts = sig("m_parts")
        max_out = sig("max_out", 16)
        max_in = sig("max_in", 16 * 3)
        NUNIT = 2 * 2 * NST * 4
        PER_ACC = NST * 4
        s_up = sig("s_up", NUNIT)
        probs_ready = sig("probs_ready", NUNIT)
        pv_up = sig("pv_up", NUNIT)
        o_copied = sig("o_copied", 4)
        oTok_up = sig("oTok_up")
        o_tok_ready = sig("o_tok_ready")
        oT_up = sig("oT_up")
        oT_ready = sig("oT_ready")
        proj_up = sig("proj_up")
        t2_ready = freeing("t2_ready")
        ln2_var = sig("ln2_var")
        ln2_std = sig("ln2_std")
        ln2_ready = sig("ln2_ready")
        mean_up = sig("mean_up")
        mean_read = freeing("mean_read")
        fT_up = sig("fT_up")
        fT_ready = sig("fT_ready")
        f_out = freeing("f_out", 16 * 3)
        logits_up = sem("logits_up")
        rt_ready = sem("rt_ready")
        rt_exp = sem("rt_exp")
        routed = sem("routed")
        loads_up = sem("loads_up")
        top_ready = sem("top_ready")
        top_moved = sem("top_moved")
        w_diag_ready = sem("w_diag_ready")
        w_all_up = sem("w_all_up")
        w_all_ready = sem("w_all_ready")
        e_w1_in = sig("e_w1_in", 16 * (2 * TOPK + 1))
        e_w2_in = sig("e_w2_in", 16 * 2 * TOPK)
        e_res_in = sig("e_res_in", 16 * 2)
        e_w2_scaled = freeing("e_w2_scaled")
        h_up = sig("h_up", TOPK * FC)
        h_ready = freeing("h_ready", TOPK * FC)
        y_e_up = freeing("y_e_up")
        res_read = freeing("res_read")
        lnf_var = sig("lnf_var")
        lnf_std = sig("lnf_std")
        lnf_ready = sig("lnf_ready")
        fin_ready = freeing("fin_ready")
        out_stored = freeing("out_stored", 16)

        dve_order_m = Order(sem("dve_order_m"), 26)
        dve_order_a = Order(sem("dve_order_a"), 12)
        dve_order_rt = Order(sem("dve_order_rt"), 0)
        dve_order_e = Order(sem("dve_order_e"), 5)
        act_order = Order(sem("act_order"), 0)
        pool_order = Order(sem("pool_order"), 0)
        pool_order_e = Order(sem("pool_order_e"), 2)

        block = ctx.enter_context(nc.Block())

        def max_share(i):
            return range(i * 2 * NMAX // NSTEP, min((i + 1) * 2 * NMAX // NSTEP, NMAX))

        def unit_share(i):
            j = i - NSTEP // 2
            return range(j * 2 * NUNIT // NSTEP, (j + 1) * 2 * NUNIT // NSTEP) if j >= 0 else range(0)

        def unit(i):
            acc, rest = divmod(i, PER_ACC)
            kt, q = divmod(rest, 4)
            return acc, kt, q, 4 * (acc // 2) + q, (acc % 2) * HALF

        NW = [0]

        @block.sync
        def _(sp):
            def load(dst, src):
                NW[0] += 16
                sp.dma_start(dst, src).then_inc(weights_in, 16)

            load(w_in_sb[:, :], w_in_t)
            load(conv_w_sb[:, :, :], conv_w.rearrange("(c p) k -> p c k", p=P))
            load(conv_b_sb[:, :], conv_b)
            load(b_dt_sb[:, :], b_dt)
            load(a_sb[:, :, :], a_log.rearrange("(c p) s -> p c s", p=P))
            load(d_skip_sb[:, :], d_skip)
            load(w_out_sb[:, :, :], w_out_t.rearrange("(c p) o -> p c o", p=P))
            load(ln_w_sb[:, :], ln_w.rearrange("(o c) -> o c", o=1).to_broadcast([TT, C]))
            load(w_qkv_sb[:, :], w_qkv)
            load(proj_w_sb[:, :], proj_w)
            load(proj_b_sb[:, :], proj_b.rearrange("(o c) -> o c", o=1))
            load(w_r_sb[:, :], w_r)
            load(b_r_sb[:, :], b_r.rearrange("(o c) -> o c", o=1))
            load(gamma_sb[:, :], gamma.rearrange("(o c) -> o c", o=1).to_broadcast([TT, C]))
            load(beta_sb[:, :], beta.rearrange("(o c) -> o c", o=1).to_broadcast([TT, C]))
            sp.wait_ge(weights_set, 1)
            xp_v = w_xp_t.rearrange("(c p) e -> p c e", p=P)
            for q in range(3):
                load(w_xp_sb[:, :, 32 * q:32 * q + NS], xp_v[:, :, RANK + NS:RANK + 2 * NS])
            load(w_xp_sb[:, :, DT0:DT0 + RANK + NS], xp_v[:, :, 0:RANK + NS])
            load(w_dt_sb[DT0:DT0 + RANK, :], w_dt_t)

            def turn(n, m):
                if m is not None:
                    sp.wait_ge(xs_ready.sem, xs_ready.at(m, 0))
                    sp.dma_start(x_tok[:, :, :], x_v[bass.ds(m, 1)].rearrange("o p k c -> (o p) k c")).then_inc(x_in.sem, 16)
                    sp.wait_ge(xd_ready.sem, xd_ready.at(m, 1))
                    sp.dma_start(b_dram, xd[DT0 + RANK:P, :]).then_inc(b_out.sem, 16)
                    sp.wait_ge(b_out.sem, b_out.at(m, 16))
                    for i in range(NSTEP):
                        if i >= NBB:
                            sp.wait_ge(dbu_ready.sem, dbu_ready.at(m, i - NBB + 1))
                        sp.dma_start(b_all[:, i % NBB, :], b_dram[i % NS:i % NS + 1, :].to_broadcast([P, TOK])
                                     ).then_inc(b_in[i % NBB].sem, 16)
                if n is not None:
                    sp.wait_ge(ln2_ready.sem, ln2_ready.at(n, 1))
                    sp.dma_start(t2_dram[bass.ds(n, 1)].rearrange("o p f -> (o p) f"), t2[:, :, :].rearrange("p k c -> p (k c)")).then_inc(f_out.sem, 16)
                    sp.dma_start(f_dram[bass.ds(n, 1)].rearrange("o p f -> (o p) f"), f_tok[:, :, :].rearrange("p k c -> p (k c)")).then_inc(f_out.sem, 16)
                    sp.wait_ge(fT_ready.sem, fT_ready.at(n, 1))
                    sp.dma_start(fT_dram[bass.ds(n, 1)].rearrange("o p f -> (o p) f"), fT[:, :]).then_inc(f_out.sem, 16)

            turn(None, 0)
            with nc.sync.Fori(0, B - 1) as n:
                turn(n, n + 1)
            turn(B - 1, None)

            sp.wait_ge(top_ready, 1)
            sp.dma_start(top_dram, top_i[:, 0:TOPK]).then_inc(top_moved, 16)
            sp.wait_ge(top_moved, 16)
            sp.dma_start(idx[:, :], top_dram.rearrange("(o b) k -> o (b k)", o=1)).then_inc(top_moved, 16)
            sp.wait_ge(top_moved, 32)
            sp.wait_ge(f_out.sem, f_out.at(B, 0))
            with nc.sync.Fori(0, B) as n:
                sp.wait_ge(h_ready.sem, h_ready.at(n, 0))
                sp.dma_start(fT[:, :], fT_dram[bass.ds(n, 1)].rearrange("o p f -> (o p) f")).then_inc(e_w1_in.sem, 16)
                experts = []
                for k in range(TOPK):
                    e = nc.sync.value_load(idx[0:1, bass.ds(n * TOPK + k, 1)], min_val=0, max_val=NE - 1)
                    experts.append(e)
                    sp.dma_start(w1_e[:, k, :], w1[bass.ds(e, 1)].rearrange("o d f -> (o d) f")).then_inc(e_w1_in.sem, 16)
                    sp.dma_start(b1_e[:, k, :], b1[bass.ds(e, 1)].rearrange("o p c -> (o p) c")).then_inc(e_w1_in.sem, 16)
                sp.wait_ge(e_w2_scaled.sem, e_w2_scaled.at(n, 0))
                for k, e in enumerate(experts):
                    sp.dma_start(w2_e[:, k, :, :], w2[bass.ds(e, 1)].rearrange("o (c p) d -> (o p) c d", p=P)).then_inc(e_w2_in.sem, 16)
                    sp.dma_start(b2_e[:, k, :], b2[bass.ds(e, 1)]).then_inc(e_w2_in.sem, 16)
                sp.wait_ge(res_read.sem, res_read.at(n, 0))
                sp.dma_start(f_tok[:, :, :].rearrange("p k c -> p (k c)"), f_dram[bass.ds(n, 1)].rearrange("o p f -> (o p) f")).then_inc(e_res_in.sem, 16)
                sp.wait_ge(fin_ready.sem, fin_ready.at(n, 0))
                sp.dma_start(t2[:, :, :].rearrange("p k c -> p (k c)"), t2_dram[bass.ds(n, 1)].rearrange("o p f -> (o p) f")).then_inc(e_res_in.sem, 16)

        @block.gpsimd
        def _(pool):
            nc.gpsimd.memset(w_xp_sb[:, :, :], 0.0)
            nc.gpsimd.memset(w_dt_sb[:, :], 0.0).then_inc(weights_set, 1)
            nc.gpsimd.memset(ones[:, :], 1.0)
            nc.gpsimd.memset(neg_half[:, :], -0.5)
            pool_order.after(pool, 0, nc.gpsimd.memset(ident[:, :], 0.0))
            nc.gpsimd.affine_select(out=ident[:, :], in_=ident[:, :], compare_op=ALU.not_equal, fill=1.0,
                                    base=0, pattern=[[-1, P]], channel_multiplier=1)
            pool_order.after(pool, 0, nc.gpsimd.memset(group_avg[:, :], 1.0 / GROUP))
            ga = group_avg[:, :].rearrange("p (g i) -> p g i", i=GROUP)
            pool_order.after(pool, 0, nc.gpsimd.affine_select(
                out=ga, in_=ga, compare_op=ALU.is_ge, fill=0.0, base=0,
                pattern=[[-GROUP, P // GROUP], [0, GROUP]], channel_multiplier=1))
            nc.gpsimd.affine_select(out=ga, in_=ga, compare_op=ALU.is_ge, fill=0.0, base=GROUP - 1,
                                    pattern=[[GROUP, P // GROUP], [0, GROUP]],
                                    channel_multiplier=-1).then_inc(consts_pool, 1)

            def rsqrt(out_, in_):
                return nc.gpsimd.tensor_tensor(out_, in_, neg_half[0:in_.shape[0], 0:in_.shape[1]], ALU.pow)

            def turn(n, m):
                if m is not None:
                    pool.wait_ge(gvar_ready.sem, gvar_ready.at(m, 1))
                    rsqrt(grp[:, 4:5], grp[:, 3:4]).then_inc(gstd_ready.sem, 1)
                    pool.wait_ge(u_ready.sem, u_ready.at(m, 1))
                    for i in range(NSTEP):
                        pool.wait_ge(b_in[i % NBB].sem, b_in[i % NBB].at(m, 16 * (i // NBB + 1)))
                        if i >= 2:
                            pool.wait_ge(scan_done.sem, scan_done.at(m, i - 1))
                        nc.gpsimd.tensor_tensor(dbu[:, i % 2, :], sp_l[:, i // NS, :], b_all[:, i % NBB, :],
                                                ALU.mult).then_inc(dbu_ready.sem, 1)
                    pool.wait_ge(ms_ready.sem, ms_ready.at(m, 1))
                    rsqrt(rms_v[:, 2, :], rms_v[:, 1, :]).then_inc(rms_ready.sem, 1)
                if n is not None:
                    pool.wait_ge(ln2_var.sem, ln2_var.at(n, 1))
                    rsqrt(norm2["r"][:, 1, :], norm2["r"][:, 0, :]).then_inc(ln2_std.sem, 1)
                if m is not None:
                    pool.wait_ge(ln1_var.sem, ln1_var.at(m, 1))
                    rsqrt(norm1["r"][:, 1, :], norm1["r"][:, 0, :]).then_inc(ln1_std.sem, 1)

            turn(None, 0)
            with nc.gpsimd.Fori(0, B - 1) as n:
                turn(n, n + 1)
            turn(B - 1, None)

            with nc.gpsimd.Fori(0, B) as n:
                pool.wait_ge(lnf_var.sem, lnf_var.at(n, 1))
                rsqrt(norm1["r"][:, 1, :], norm1["r"][:, 0, :]).then_inc(lnf_std.sem, 1)
                pool.wait_ge(lnf_ready.sem, lnf_ready.at(n, 1))
                pool.wait_ge(out_stored.sem, out_stored.at(n, 0))
                pool_order_e.count = 0
                pool_order_e.after(pool, n, nc.gpsimd.tensor_tensor(
                    o_rms[:, :, :], ln1_tok[:, :, :], gamma_sb[:, :].unsqueeze(1).to_broadcast([TT, NT, C]), ALU.mult))
                pool_order_e.after(pool, n, nc.gpsimd.tensor_tensor(
                    o_rms[:, :, :], o_rms[:, :, :], beta_sb[:, :].unsqueeze(1).to_broadcast([TT, NT, C]), ALU.add))
                pool.wait_ge(e_res_in.sem, e_res_in.at(n, 32))
                nc.gpsimd.tensor_tensor(o_rms[:, :, :], o_rms[:, :, :], t2[:, :, :], ALU.add).then_inc(fin_ready.sem, 1)

        @block.scalar
        def _(act):
            act.wait_ge(weights_in, NW[0])
            act_order.after(act, 0, nc.scalar.activation(a_sb[:, :, :], a_sb[:, :, :], ACT.Exp))
            nc.scalar.mul(a_sb[:, :, :], a_sb[:, :, :], -1.0).then_inc(a_exp, 1)
            act.wait_ge(a_exp, 1)

            def in_jt(ap):
                return ap.rearrange("p (j t) -> p t j", j=J)

            def by_tj(ap):
                return ap.rearrange("p (t j) -> p t j", j=J)

            def turn(n, m):
                if n is not None:
                    act.wait_ge(q_up.sem, q_up.at(n, 1))
                    nc.scalar.copy(q_part[:, 0, :], wide(4)).then_inc(qk_first.sem, 1)
                    act.wait_ge(k_up.sem, k_up.at(n, 1))
                    nc.scalar.copy(k_part[:, 0, :], wide(6)).then_inc(qk_first.sem, 1)
                    act.wait_ge(v_up.sem, v_up.at(n, 1))
                    nc.scalar.copy(v_ext[:, 0:NST - 1, :, 0:HD],
                                   PS[:, 4 * BANK:4 * BANK + (NST - 1) * C].rearrange("p (k h d) -> p k h d", k=NST - 1, h=H))
                    nc.scalar.copy(v_ext[0:32, NST - 1, :, 0:HD],
                                   PS[0:32, 4 * BANK + (NST - 1) * C:4 * BANK + NST * C].rearrange("p (h d) -> p h d", h=H)
                                   ).then_inc(v_copied.sem, 1)
                    for i, part in enumerate((q_part, k_part)):
                        act.wait_ge(qk_parts.sem, qk_parts.at(n, i + 1))
                        act.dma_start(parts_dram[i], part[:, :, :]).then_inc(parts_out.sem, 16)
                    act.wait_ge(parts_out.sem, parts_out.at(n, 32))
                    for i, (stack, which) in enumerate(((q_stack, Q_PARTS), (k_stack, K_PARTS))):
                        for r, a in enumerate(which):
                            act.dma_start(stack[HD * r:HD * (r + 1), :, :],
                                          parts_dram[i, :, a, :].rearrange("(h d) t -> d h t", h=H)
                                          ).then_inc(stacks_in.sem, 16)
                if m is not None:
                    for ck in range(NC_):
                        act.wait_ge(conv_done.sem, conv_done.at(m, ck + 1))
                        nc.scalar.activation(in_jt(xc[:, ck, :]), by_tj(conv_acc[:, ck, :]), ACT.Silu).then_inc(silu_done.sem, 1)
                    for ck in range(NC_):
                        act.wait_ge(xz_up.sem, xz_up.at(m, NC_ + ck + 1))
                        nc.scalar.activation(in_jt(z_act[:, ck, :]), by_tj(wide([2, 0][ck])), ACT.Silu).then_inc(silu_done.sem, 1)
                    act.wait_ge(xd_up.sem, xd_up.at(m, 1))
                    nc.scalar.copy(xd[:, :], wide(0)).then_inc(xd_ready.sem, 1)
                    for ck in range(NC_):
                        act.wait_ge(dt_up.sem, dt_up.at(m, ck + 1))
                        nc.scalar.activation(sp_e[:, ck, :], wide([2, 0][ck]), ACT.Abs, bias=b_dt_sb[:, ck:ck + 1]).then_inc(dt_abs.sem, 1)
                    act.wait_ge(dt_abs.sem, dt_abs.at(m, NC_))
                    nc.scalar.activation(sp_e[:, :, :], sp_e[:, :, :], ACT.Exp, scale=-1.0).then_inc(sp_exp.sem, 1)
                    act.wait_ge(sp_exp.sem, sp_exp.at(m, 1))
                    nc.scalar.activation(sp_l[:, :, :], sp_e[:, :, :], ACT.Ln, bias=1.0).then_inc(sp_ln.sem, 1)
                    act.wait_ge(dt_ready.sem, dt_ready.at(m, 1))
                for i in range(NSTEP):
                    if m is not None:
                        ck, s = divmod(i, NS)
                        if i >= 2:
                            act.wait_ge(scan_done.sem, scan_done.at(m, i - 1))
                        nc.scalar.activation(dA[:, i % 2, :].rearrange("p (j t) -> p j t", t=T)[:, :, 1:T],
                                             dt_sb[:, ck, :].rearrange("p (j t) -> p j t", t=T)[:, :, 1:T],
                                             ACT.Exp, scale=a_sb[:, ck, s:s + 1]).then_inc(dA_ready.sem, 1)
                    if n is not None:
                        if i == NSTEP // 2 - 1:
                            act.wait_ge(m_parts.sem, m_parts.at(n, 1))
                            act.dma_start(max_dram, m_part[:, :, :]).then_inc(max_out.sem, 16)
                            act.wait_ge(max_out.sem, max_out.at(n, 16))
                            for a in range(3):
                                act.dma_start(q_stack[KST + a:KST + a + 1, :, :],
                                              max_dram[:, a, :].rearrange("(o h) t -> o h t", o=1)).then_inc(max_in.sem, 16)
                        for j in unit_share(i):
                            rows = ST[unit(j)[1]][1]
                            act.wait_ge(s_up.sem, s_up.at(n, j + 1))
                            if j >= NPROB:
                                act.wait_ge(pv_up.sem, pv_up.at(n, j - NPROB + 1))
                            nc.scalar.activation(probs[0:rows, j % NPROB, :], bank(4 + j % 2, HALF)[0:rows], ACT.Exp,
                                                 scale=ATT_SCALE).then_inc(probs_ready.sem, 1)
                if m is not None:
                    act.wait_ge(out_up.sem, out_up.at(m, 1))
                    nc.scalar.activation(sq[:, :, :], tokens(2), ACT.Square).then_inc(rms_sq.sem, 1)
                if n is not None:
                    act.wait_ge(oT_up.sem, oT_up.at(n, 1))
                    nc.scalar.copy(oT[:, :].rearrange("p (a t) -> p a t", a=2), halves(4)).then_inc(oT_ready.sem, 1)
                    act.wait_ge(fT_up.sem, fT_up.at(n, 1))
                    act.wait_ge(f_out.sem, f_out.at(n, 0))
                    nc.scalar.copy(fT[:, :].rearrange("p (a t) -> p a t", a=2), halves(4)).then_inc(fT_ready.sem, 1)
                if m is not None:
                    act.wait_ge(ln1T_up.sem, ln1T_up.at(m, 1))
                    nc.scalar.copy(lnT[:, :].rearrange("p (a t) -> p a t", a=2), halves(0)).then_inc(ln1T_ready.sem, 1)

            turn(None, 0)
            with nc.scalar.Fori(0, B - 1) as n:
                turn(n, n + 1)
            turn(B - 1, None)

            for i in range(3):
                act.wait_ge(rt_ready, i + 1)
                src, dst = [(rt[:, 1, :], rt[:, 2, :]), (rt[:, 5, :], rt[:, 6, :]), (top_w[:, 0:1], top_w[:, 1:2])][i]
                nc.scalar.activation(dst, src, ACT.Exp).then_inc(rt_exp, 1)

            with nc.scalar.Fori(0, B) as n:
                act.wait_ge(e_w1_in.sem, e_w1_in.at(n, e_w1_in.per_turn))
                act.wait_ge(y_e_up.sem, y_e_up.at(n, 0))
                for i in range(TOPK * FC):
                    k, fc = divmod(i, FC)
                    act.wait_ge(h_up.sem, h_up.at(n, i + 1))
                    nc.scalar.activation(hidden[i], wide(2 * (i % 2)), ACT.Gelu, bias=b1_e[:, k, fc:fc + 1]).then_inc(h_ready.sem, 1)
                act.wait_ge(fin_ready.sem, fin_ready.at(n, 1))
                act.dma_start(out_v[bass.ds(n, 1)].rearrange("o p k c -> (o p) k c"), o_rms[:, :, :]).then_inc(out_stored.sem, 16)
            act.wait_ge(out_stored.sem, out_stored.at(B, 0))

        @block.vector
        def _(dve):
            for signal in freed:
                dve.sem_inc(signal.sem, 1)
            nc.vector.memset(dA[:, :, :], 0.0)
            nc.vector.memset(probs[:, :, :], 0.0)
            nc.vector.memset(k_stack[KST:KST + 3, :, :], 1.0)
            nc.vector.memset(v_ext[:, 0:NST - 1, :, :], 1.0)
            dve_order_rt.after(dve, 0, nc.vector.memset(v_ext[:, NST - 1, :, :], 0.0))
            nc.vector.memset(v_ext[0:ST[-1][1], NST - 1, :, :], 1.0)
            dve.wait_ge(consts_pool, 1)
            dve_order_rt.after(dve, 0, nc.vector.tensor_copy(
                pick_c[:, :, :], ident[0:C_ROWS, 0:NS].unsqueeze(2).to_broadcast([C_ROWS, NS, P])))
            for q in range(1, 3):
                dve_order_rt.after(dve, 0, nc.vector.tensor_tensor(
                    pick_c[:, :, :], pick_c[:, :, :],
                    ident[0:C_ROWS, 32 * q:32 * q + NS].unsqueeze(2).to_broadcast([C_ROWS, NS, P]), ALU.add))
            nc.vector.memset(w_diag[:, :, :], 0.0).then_inc(consts_dve, 1)
            dve.wait_ge(weights_in, NW[0])

            def norm_stats(then, tiles, src, eps):
                stats, mv, r = tiles["stats"], tiles["mv"], tiles["r"]
                for k in range(NT):
                    last = nc.vector.bn_stats(stats[:, k, :], src[:, k, :])
                then(last)
                even_m, even_m2, odd_m, odd_m2 = (stats[:, :, c] for c in (1, 2, 4, 5))
                nc.vector.tensor_tensor(mv[:, 0, :], even_m, odd_m, ALU.add)
                nc.vector.tensor_tensor(mv[:, 1, :], even_m, odd_m, ALU.subtract)
                then(nc.vector.tensor_tensor(mv[:, 2, :], even_m2, odd_m2, ALU.add))
                nc.vector.tensor_scalar(mv[:, 0, :], mv[:, 0, :], 0.5, None, ALU.mult)
                nc.vector.scalar_tensor_tensor(mv[:, 1, :], mv[:, 1, :], 0.25, mv[:, 1, :], ALU.mult, ALU.mult)
                then(nc.vector.tensor_scalar(mv[:, 2, :], mv[:, 2, :], 1.0 / C, eps, ALU.mult, ALU.add))
                return nc.vector.tensor_tensor(r[:, 0, :], mv[:, 2, :], mv[:, 1, :], ALU.add)

            def norm_apply(tiles, src, dst):
                for k in range(NT):
                    last = nc.vector.tensor_scalar(dst[:, k, :], src[:, k, :], tiles["mv"][:, 0, k:k + 1],
                                                   tiles["r"][:, 1, k:k + 1], ALU.subtract, ALU.mult)
                return last

            def turn(n, m):
                dve_order_m.count = 0
                dve_order_a.count = 0

                def mthen(ins):
                    dve_order_m.after(dve, m, ins)

                def athen(ins):
                    dve_order_a.after(dve, n, ins)

                def low_parts(i):
                    part, b = ((q_part, 4), (k_part, 6))[i]
                    dve.wait_ge(qk_first.sem, qk_first.at(n, i + 1))
                    athen(nc.vector.tensor_tensor(part_rest[:, :], wide(b), part[:, 0, :], ALU.subtract))
                    athen(nc.vector.tensor_copy(part[:, 1, :], part_rest[:, :]))
                    nc.vector.tensor_tensor(part[:, 2, :], part_rest[:, :], part[:, 1, :], ALU.subtract).then_inc(qk_parts.sem, 1)
                    dve.wait_ge(qk_parts.sem, qk_parts.at(n, i + 1))

                if m is not None:
                    dve.wait_ge(xT_up.sem, xT_up.at(m, 1))
                    nc.vector.bn_stats(chan_stats[:, 0, :], bank(0, HALF))
                    nc.vector.bn_stats(chan_stats[:, 1, :], bank(1, HALF)).then_inc(chan_ready.sem, 1)
                if n is not None:
                    low_parts(0)
                if m is not None:
                    dve.wait_ge(gmean_up.sem, gmean_up.at(m, 1))
                    mthen(nc.vector.reduce_sum(grp[:, 1:2], bank(2, NPART), X))
                    mthen(nc.vector.tensor_scalar(grp[:, 0:1], grp[:, 1:2], 1.0 / NPART, None, ALU.mult))
                    mthen(nc.vector.tensor_scalar(part_dev[:, :], part_mean, grp[:, 0:1], None, ALU.subtract))
                    mthen(nc.vector.tensor_tensor(part_dev[:, :], part_dev[:, :], part_dev[:, :], ALU.mult))
                    nc.vector.scalar_tensor_tensor(part_dev[:, :], part_m2, float(NPART) / TOK, part_dev[:, :],
                                                   ALU.mult, ALU.add).then_inc(gdev_ready.sem, 1)
                    dve.wait_ge(gvar_up.sem, gvar_up.at(m, 1))
                    mthen(nc.vector.reduce_sum(grp[:, 2:3], bank(3, NPART), X))
                    nc.vector.tensor_scalar(grp[:, 3:4], grp[:, 2:3], 1.0 / NPART, 1e-5, ALU.mult, ALU.add).then_inc(gvar_ready.sem, 1)
                if n is not None:
                    low_parts(1)
                if m is not None:
                    dve.wait_ge(gstd_ready.sem, gstd_ready.at(m, 1))
                    nc.vector.tensor_scalar(xnT[:, :].rearrange("p (a t) -> p a t", a=2), halves(0), grp[:, 0:1], grp[:, 4:5],
                                            ALU.subtract, ALU.mult).then_inc(xn_ready.sem, 1)
                    for ck in range(NC_):
                        dve.wait_ge(xz_up.sem, xz_up.at(m, ck + 1))
                        src = wide([2, 0][ck])
                        mthen(nc.vector.tensor_scalar(conv_acc[:, ck, :], src, conv_w_sb[:, ck, TAPS - 1:TAPS],
                                                      conv_b_sb[:, ck:ck + 1], ALU.mult, ALU.add))
                        for back in range(1, TAPS):
                            ins = nc.vector.scalar_tensor_tensor(
                                conv_acc[:, ck, back * J:], src[:, 0:TOK - back * J],
                                conv_w_sb[:, ck, TAPS - 1 - back:TAPS - back], conv_acc[:, ck, back * J:], ALU.mult, ALU.add)
                            if back < TAPS - 1:
                                mthen(ins)
                        ins.then_inc(conv_done.sem, 1)
                    dve.wait_ge(gn_tok_up.sem, gn_tok_up.at(m, 1))
                    nc.vector.tensor_tensor(x_sum[:, :, :], x_tok[:, :, :], tokens(2), ALU.add).then_inc(xs_ready.sem, 1)
                    dve.wait_ge(xd_ready.sem, xd_ready.at(m, 1))
                    mthen(nc.vector.tensor_copy(c_parts[:, :], xd[0:C_ROWS, :]))
                    mthen(nc.vector.tensor_tensor(c_rest[:, :], xd[0:C_ROWS, :], c_parts[:, :], ALU.subtract))
                    nc.vector.tensor_copy(c_parts[32:64, :], c_rest[32:64, :])
                    mthen(nc.vector.tensor_copy(c_mid[64:96, :], c_rest[64:96, :]))
                    nc.vector.tensor_tensor(c_parts[64:96, :], c_rest[64:96, :], c_mid[64:96, :], ALU.subtract).then_inc(c_ready.sem, 1)
                    for ck in range(NC_):
                        dve.wait_ge(dt_abs.sem, dt_abs.at(m, ck + 1))
                        nc.vector.tensor_scalar(dt_sb[:, ck, :], wide([2, 0][ck]), b_dt_sb[:, ck:ck + 1], 0.0,
                                                ALU.add, ALU.max).then_inc(dt_relu.sem, 1)
                    dve.wait_ge(sp_exp.sem, sp_exp.at(m, 1))
                    mthen(nc.vector.tensor_scalar(conv_acc[:, :, :], sp_e[:, :, :], 1.0, 1.0, ALU.add, ALU.subtract))
                    mthen(nc.vector.tensor_tensor(conv_acc[:, :, :], sp_e[:, :, :], conv_acc[:, :, :], ALU.subtract))
                    dve.wait_ge(dt_relu.sem, dt_relu.at(m, NC_))
                    mthen(nc.vector.tensor_tensor(dt_sb[:, :, :], dt_sb[:, :, :], conv_acc[:, :, :], ALU.add))
                    dve.wait_ge(sp_ln.sem, sp_ln.at(m, 1))
                    nc.vector.tensor_tensor(dt_sb[:, :, :], dt_sb[:, :, :], sp_l[:, :, :], ALU.add).then_inc(dt_ready.sem, 1)
                    dve.wait_ge(dt_ready.sem, dt_ready.at(m, 1))
                    nc.vector.tensor_tensor(sp_l[:, :, :], dt_sb[:, :, :], xc[:, :, :], ALU.mult).then_inc(u_ready.sem, 1)

                for i in range(NSTEP):
                    if m is not None:
                        ck, s = divmod(i, NS)
                        dve.wait_ge(dA_ready.sem, dA_ready.at(m, i + 1))
                        dve.wait_ge(dbu_ready.sem, dbu_ready.at(m, i + 1))
                        nc.vector.tensor_tensor_scan(hst[:, i % 2, :], dA[:, i % 2, :], dbu[:, i % 2, :], 0.0,
                                                     ALU.mult, ALU.add).then_inc(scan_done.sem, 1)
                        dve.wait_ge(cb_up.sem, cb_up.at(m, i + 1))
                        if i >= 2:
                            dve.wait_ge(y_up.sem, y_up.at(m, i - 1))
                        dve.wait_ge(scan_done.sem, scan_done.at(m, i + 1))
                        nc.vector.tensor_tensor(g[:, i % 2, :], hst[:, i % 2, :], wide(2), ALU.mult).then_inc(g_ready.sem, 1)
                    if n is not None:
                        for j in max_share(i):
                            kt, h = divmod(j, H)
                            rows = ST[kt][1]
                            dve.wait_ge(smax_up.sem, smax_up.at(n, j + 1))
                            nc.vector.tensor_reduce(q_max[0:rows, kt, h:h + 1], wide(4 + 2 * (j % 2))[0:rows], axis=X,
                                                    op=ALU.max, negate=True).then_inc(smax_read.sem, 1)
                        if i == NSTEP // 2 - 1:
                            dve.wait_ge(maxT_up.sem, maxT_up.at(n, 1))
                            athen(nc.vector.tensor_copy(m_row[:, :], PS[0:H, 4 * BANK:4 * BANK + TOK]))
                            athen(nc.vector.tensor_copy(m_part[:, 0, :], m_row[:, :]))
                            athen(nc.vector.tensor_tensor(m_row[:, :], m_row[:, :], m_part[:, 0, :], ALU.subtract))
                            athen(nc.vector.tensor_copy(m_part[:, 1, :], m_row[:, :]))
                            nc.vector.tensor_tensor(m_part[:, 2, :], m_row[:, :], m_part[:, 1, :], ALU.subtract).then_inc(m_parts.sem, 1)
                        for acc in range(4):
                            if i == min(NSTEP // 2 + (acc + 1) * NSTEP // 8, NSTEP - 1) and acc < 3:
                                dve.wait_ge(pv_up.sem, pv_up.at(n, (acc + 1) * PER_ACC))
                                nc.vector.tensor_copy(o_raw[:, acc // 2, (acc % 2) * HALF:(acc % 2 + 1) * HALF],
                                                      bank(6 + acc % 2, HALF)).then_inc(o_copied.sem, 1)
                    if m is not None and s == NS - 1:
                        dve.wait_ge(y_up.sem, y_up.at(m, i + 1))
                        mthen(nc.vector.scalar_tensor_tensor(xc[:, ck, :], xc[:, ck, :], d_skip_sb[:, ck:ck + 1], wide(0),
                                                             ALU.mult, ALU.add))
                        nc.vector.tensor_tensor(conv_acc[:, ck, :].rearrange("p (t j) -> p j t", j=J),
                                                xc[:, ck, :].rearrange("p (j t) -> p j t", j=J),
                                                z_act[:, ck, :].rearrange("p (j t) -> p j t", j=J),
                                                ALU.mult).then_inc(y_ready.sem, 1)

                if n is not None:
                    dve.wait_ge(pv_up.sem, pv_up.at(n, 4 * PER_ACC))
                    nc.vector.tensor_copy(o_raw[:, 1, HALF:TOK], bank(7, HALF)).then_inc(o_copied.sem, 1)
                if m is not None:
                    dve.wait_ge(rms_sq.sem, rms_sq.at(m, 1))
                    mthen(nc.vector.reduce_sum(rms_v[:, 0, :], sq[:, :, :], X))
                    nc.vector.tensor_scalar(rms_v[:, 1, :], rms_v[:, 0, :], 1.0 / C, 1e-6, ALU.mult, ALU.add).then_inc(ms_ready.sem, 1)
                if n is not None:
                    dve.wait_ge(oTok_up.sem, oTok_up.at(n, 1))
                    for b in range(4):
                        src = PS[0:TT, (4 + b) * BANK:(5 + b) * BANK].rearrange("p (k d) -> p k d", d=32)
                        last = nc.vector.reciprocal(o_rec[:, 16 * b:16 * (b + 1)], src[:, :, HD])
                    athen(last)
                    for b in range(4):
                        src = PS[0:TT, (4 + b) * BANK:(5 + b) * BANK].rearrange("p (k d) -> p k d", d=32)
                        rec = o_rec[:, 16 * b:16 * (b + 1)].unsqueeze(2).to_broadcast([TT, 16, HD])
                        last = nc.vector.tensor_tensor(o_tok[:, :, 2 * b:2 * b + 2, :].rearrange("p h i d -> p i h d"),
                                                       src[:, :, 0:HD].rearrange("p (i h) d -> p i h d", h=H),
                                                       rec.rearrange("p (i h) d -> p i h d", h=H), ALU.mult)
                    last.then_inc(o_tok_ready.sem, 1)
                if m is not None:
                    dve.wait_ge(rms_ready.sem, rms_ready.at(m, 1))
                    mthen(nc.vector.tensor_tensor(o_rms[:, :, :], tokens(2),
                                                  rms_v[:, 2, :].unsqueeze(2).to_broadcast([TT, NT, C]), ALU.mult))
                    mthen(nc.vector.tensor_tensor(o_rms[:, :, :], o_rms[:, :, :],
                                                  ln_w_sb[:, :].unsqueeze(1).to_broadcast([TT, NT, C]), ALU.mult))
                if n is not None:
                    dve.wait_ge(proj_up.sem, proj_up.at(n, 1))
                    dve.wait_ge(f_out.sem, f_out.at(n, 0))
                    nc.vector.scalar_tensor_tensor(t2[:, :, :].rearrange("p k c -> p (k c)"), PS[0:TT, 6 * BANK:8 * BANK], 0.0,
                                                   t1[:, :, :].rearrange("p k c -> p (k c)"), ALU.max, ALU.add).then_inc(t2_ready.sem, 1)
                    dve.wait_ge(t2_ready.sem, t2_ready.at(n, 1))
                    norm_stats(athen, norm2, t2, 1e-5).then_inc(ln2_var.sem, 1)
                if m is not None:
                    dve.wait_ge(t2_ready.sem, t2_ready.at(m, 0))
                    mthen(nc.vector.tensor_tensor(t1[:, :, :], x_sum[:, :, :], o_rms[:, :, :], ALU.add))
                    norm_stats(mthen, norm1, t1, 1e-5).then_inc(ln1_var.sem, 1)
                if n is not None:
                    dve.wait_ge(ln2_std.sem, ln2_std.at(n, 1))
                    norm_apply(norm2, t2, f_tok).then_inc(ln2_ready.sem, 1)
                if m is not None:
                    dve.wait_ge(ln1_std.sem, ln1_std.at(m, 1))
                    norm_apply(norm1, t1, ln1_tok).then_inc(ln1_ready.sem, 1)
                if n is not None:
                    dve.wait_ge(mean_up.sem, mean_up.at(n, 1))
                    nc.vector.tensor_scalar(x_mean[:, bass.ds(n, 1)], bank(6, 1), 1.0 / TOK, None, ALU.mult).then_inc(mean_read.sem, 1)
                assert m is None or dve_order_m.count == dve_order_m.per_turn, dve_order_m.count
                assert n is None or dve_order_a.count == dve_order_a.per_turn, dve_order_a.count

            turn(None, 0)
            with nc.vector.Fori(0, B - 1) as n:
                turn(n, n + 1)
            turn(B - 1, None)

            def rthen(ins):
                dve_order_rt.after(dve, 0, ins)

            dve.wait_ge(logits_up, 1)
            rthen(nc.vector.tensor_copy(rt[:, 0, :], PS[0:B, 0:NE]))
            rthen(nc.vector.tensor_reduce(rt[:, 14, 0:1], rt[:, 0, :], axis=X, op=ALU.max))
            nc.vector.tensor_scalar(rt[:, 1, :], rt[:, 0, :], rt[:, 14, 0:1], None, ALU.subtract).then_inc(rt_ready, 1)
            dve.wait_ge(rt_exp, 1)
            rthen(nc.vector.reduce_sum(rt[:, 14, 1:2], rt[:, 2, :], X))
            rthen(nc.vector.reciprocal(rt[:, 14, 2:3], rt[:, 14, 1:2]))
            nc.vector.tensor_scalar(rt[:, 3, :], rt[:, 2, :], rt[:, 14, 2:3], None, ALU.mult).then_inc(routed, 1)
            dve.wait_ge(loads_up, 1)
            rthen(nc.vector.tensor_scalar(rt[:, 7, :], PS[0:B, BANK:BANK + NE], float(TOK), None, ALU.mult))
            rthen(nc.vector.reciprocal(rt[:, 8, :], rt[:, 7, :]))
            rthen(nc.vector.tensor_scalar(rt[:, 9, :], rt[:, 8, :], CAPACITY, 1.0, ALU.mult, ALU.min))
            rthen(nc.vector.tensor_tensor(rt[:, 4, :], rt[:, 3, :], rt[:, 9, :], ALU.mult))
            rthen(nc.vector.tensor_reduce(rt[:, 14, 3:4], rt[:, 4, :], axis=X, op=ALU.max))
            nc.vector.tensor_scalar(rt[:, 5, :], rt[:, 4, :], rt[:, 14, 3:4], None, ALU.subtract).then_inc(rt_ready, 1)
            dve.wait_ge(rt_exp, 2)
            rthen(nc.vector.reduce_sum(rt[:, 14, 4:5], rt[:, 6, :], X))
            rthen(nc.vector.reciprocal(rt[:, 14, 5:6], rt[:, 14, 4:5]))
            rthen(nc.vector.tensor_scalar(rt[:, 10, :], rt[:, 6, :], rt[:, 14, 5:6], None, ALU.mult))
            rthen(nc.vector.max(top_v[:, :], rt[:, 10, :]))
            nc.vector.max_index(top_i[:, :], top_v[:, :], rt[:, 10, :]).then_inc(top_ready, 1)
            nc.vector.tensor_tensor(top_w[:, 0:1], top_v[:, 1:2], top_v[:, 0:1], ALU.subtract).then_inc(rt_ready, 1)
            dve.wait_ge(rt_exp, 3)
            rthen(nc.vector.tensor_scalar(top_w[:, 2:3], top_w[:, 1:2], 1.0, None, ALU.add))
            rthen(nc.vector.reciprocal(top_w[:, 2:3], top_w[:, 2:3]))
            rthen(nc.vector.tensor_tensor(top_w[:, 3:4], top_w[:, 1:2], top_w[:, 2:3], ALU.mult))
            for k in range(TOPK):
                last = nc.vector.tensor_scalar(w_diag[:, :, k], ident[0:B, 0:B], top_w[:, 2 + k:3 + k], None, ALU.mult)
            last.then_inc(w_diag_ready, 1)
            dve.wait_ge(w_all_up, 1)
            nc.vector.tensor_copy(w_all[:, :], bank(2, B * TOPK)).then_inc(w_all_ready, 1)
            dve.wait_ge(w_all_ready, 1)

            with nc.vector.Fori(0, B) as n:
                dve_order_e.count = 0

                def ethen(ins):
                    dve_order_e.after(dve, n, ins)

                dve.wait_ge(e_w2_in.sem, e_w2_in.at(n, e_w2_in.per_turn))
                dve.wait_ge(y_e_up.sem, y_e_up.at(n, 0))
                ethen(nc.vector.tensor_scalar(b2_s[:, :], b2_e[:, 0, :], w_all[0:1, bass.ds(n * TOPK, 1)], None, ALU.mult))
                ethen(nc.vector.scalar_tensor_tensor(b2_s[:, :], b2_e[:, 1, :], w_all[0:1, bass.ds(n * TOPK + 1, 1)], b2_s[:, :],
                                                     ALU.mult, ALU.add))
                for k in range(TOPK):
                    last = nc.vector.tensor_scalar(w2_s[:, k, :, :], w2_e[:, k, :, :], w_all[:, bass.ds(n * TOPK + k, 1)],
                                                   None, ALU.mult)
                last.then_inc(e_w2_scaled.sem, 1)
                dve.wait_ge(e_res_in.sem, e_res_in.at(n, 32))
                dve.wait_ge(y_e_up.sem, y_e_up.at(n, 1))
                nc.vector.tensor_tensor(t1[:, :, :], f_tok[:, :, :], tokens(4), ALU.add).then_inc(res_read.sem, 1)
                dve.wait_ge(res_read.sem, res_read.at(n, 1))
                norm_stats(ethen, norm1, t1, 1e-5).then_inc(lnf_var.sem, 1)
                dve.wait_ge(lnf_std.sem, lnf_std.at(n, 1))
                dve.wait_ge(fin_ready.sem, fin_ready.at(n, 0))
                norm_apply(norm1, t1, ln1_tok).then_inc(lnf_ready.sem, 1)
                dve.wait_ge(lnf_ready.sem, lnf_ready.at(n, 1))
            assert dve_order_e.count == dve_order_e.per_turn, dve_order_e.count

        @block.tensor
        def _(pe):
            pe.wait_ge(consts_pool, 1)
            pe.wait_ge(consts_dve, 1)
            pe.wait_ge(weights_in, NW[0])

            def channel_major(src, b):
                for k in range(NT):
                    a, o = divmod(k * TT, HALF)
                    last = nc.tensor.transpose(PS[:, (b + a) * BANK + o:(b + a) * BANK + o + TT], src[:, k, :], ident[0:TT, 0:TT])
                return last

            def over_spans(b, lhsT, rhs, start=True, stop=True):
                for at, width in SPANS:
                    last = nc.tensor.matmul(PS[:, b * BANK + at:b * BANK + at + width], lhsT, rhs[:, at:at + width],
                                            start=start, stop=stop)
                return last

            def turn(n, m):
                def sum_states(i):
                    ck, s = divmod(i, NS)
                    pe.wait_ge(g_ready.sem, g_ready.at(m, i + 1))
                    if s == 0 and ck:
                        pe.wait_ge(y_ready.sem, y_ready.at(m, ck))
                    over_spans(0, ident[:, :], g[:, i % 2, :], start=(s == 0), stop=(s == NS - 1)).then_inc(y_up.sem, 1)

                def max_scores(j):
                    kt, h = divmod(j, H)
                    at, rows = ST[kt]
                    if j == 0:
                        pe.wait_ge(stacks_in.sem, stacks_in.at(n, 16 * NSTK))
                        pe.wait_ge(v_copied.sem, v_copied.at(n, 1))
                    if j >= 2:
                        pe.wait_ge(smax_read.sem, smax_read.at(n, j - 1))
                    b = 4 + 2 * (j % 2)
                    for o, width in SPANS:
                        last = nc.tensor.matmul(PS[0:rows, b * BANK + o:b * BANK + o + width], q_stack[0:KST, h, at:at + rows],
                                                k_stack[0:KST, h, o:o + width], start=True, stop=True)
                    last.then_inc(smax_up.sem, 1)

                def times_v(j):
                    acc, kt, q, h, _ = unit(j)
                    pe.wait_ge(probs_ready.sem, probs_ready.at(n, j + 1))
                    if acc >= 2 and j % PER_ACC == 0:
                        pe.wait_ge(o_copied.sem, o_copied.at(n, acc - 1))
                    nc.tensor.matmul(PS[32 * q:32 * (q + 1), (6 + acc % 2) * BANK:(6 + acc % 2) * BANK + HALF],
                                     v_ext[:, kt, h, :], probs[:, j % NPROB, :],
                                     start=(kt == 0), stop=(kt == NST - 1)).then_inc(pv_up.sem, 1)

                def scores(j):
                    _, kt, _, h, q0 = unit(j)
                    at, rows = ST[kt]
                    if j == 0:
                        pe.wait_ge(max_in.sem, max_in.at(n, 16 * 3))
                    if j >= 2:
                        pe.wait_ge(probs_ready.sem, probs_ready.at(n, j - 1))
                    nc.tensor.matmul(bank(4 + j % 2, HALF)[0:rows], k_stack[:, h, at:at + rows],
                                     q_stack[:, h, q0:q0 + HALF], start=True, stop=True).then_inc(s_up.sem, 1)

                if n is not None:
                    pe.wait_ge(ln1T_ready.sem, ln1T_ready.at(n, 1))
                    pe.wait_ge(mean_read.sem, mean_read.at(n, 0))
                    over_spans(4, w_qkv_sb[:, 0:C], lnT).then_inc(q_up.sem, 1)
                    over_spans(6, w_qkv_sb[:, C:2 * C], lnT).then_inc(k_up.sem, 1)
                if m is not None:
                    pe.wait_ge(x_in.sem, x_in.at(m, 16))
                    pe.wait_ge(ln1T_ready.sem, ln1T_ready.at(m, 0))
                    channel_major(x_tok, 0).then_inc(xT_up.sem, 1)
                    pe.wait_ge(chan_ready.sem, chan_ready.at(m, 1))
                    nc.tensor.matmul(bank(2, NPART), group_avg[:, :], part_mean, start=True, stop=True).then_inc(gmean_up.sem, 1)
                    pe.wait_ge(gdev_ready.sem, gdev_ready.at(m, 1))
                    nc.tensor.matmul(bank(3, NPART), group_avg[:, :], part_dev[:, :], start=True, stop=True).then_inc(gvar_up.sem, 1)
                if n is not None:
                    pe.wait_ge(qk_parts.sem, qk_parts.at(n, 1))
                    for k, (at, rows) in enumerate(ST):
                        last = nc.tensor.matmul(PS[0:rows, 4 * BANK + k * C:4 * BANK + (k + 1) * C], lnT[:, at:at + rows],
                                                w_qkv_sb[:, 2 * C:3 * C], start=True, stop=True)
                    last.then_inc(v_up.sem, 1)
                if m is not None:
                    pe.wait_ge(xn_ready.sem, xn_ready.at(m, 1))
                    over_spans(2, w_in_sb[:, 0:P], xnT).then_inc(xz_up.sem, 1)
                    over_spans(0, w_in_sb[:, P:2 * P], xnT).then_inc(xz_up.sem, 1)
                    pe.wait_ge(conv_done.sem, conv_done.at(m, 1))
                    over_spans(2, w_in_sb[:, 2 * P:3 * P], xnT).then_inc(xz_up.sem, 1)
                    pe.wait_ge(conv_done.sem, conv_done.at(m, 2))
                    over_spans(0, w_in_sb[:, 3 * P:4 * P], xnT).then_inc(xz_up.sem, 1)
                    pe.wait_ge(silu_done.sem, silu_done.at(m, 3))
                    for k in range(NT):
                        last = nc.tensor.transpose(PS[0:TT, 2 * BANK + k * C:2 * BANK + (k + 1) * C], xnT[:, k * TT:(k + 1) * TT], ident[:, :])
                    last.then_inc(gn_tok_up.sem, 1)
                    pe.wait_ge(silu_done.sem, silu_done.at(m, 4))
                    for at, width in SPANS:
                        for ck in range(NC_):
                            last = nc.tensor.matmul(PS[:, at:at + width], w_xp_sb[:, ck, :],
                                                    xc[:, ck, at:at + width], start=(ck == 0), stop=(ck == NC_ - 1))
                    last.then_inc(xd_up.sem, 1)
                    pe.wait_ge(xs_ready.sem, xs_ready.at(m, 1))
                    pe.wait_ge(xd_ready.sem, xd_ready.at(m, 1))
                    over_spans(2, w_dt_sb[DT0:P, 0:P], xd[DT0:P, :]).then_inc(dt_up.sem, 1)
                    over_spans(0, w_dt_sb[DT0:P, P:2 * P], xd[DT0:P, :]).then_inc(dt_up.sem, 1)
                    pe.wait_ge(c_ready.sem, c_ready.at(m, 1))
                    pe.wait_ge(dt_relu.sem, dt_relu.at(m, NC_))

                for i in range(NSTEP):
                    if m is not None:
                        if i >= 1:
                            pe.wait_ge(g_ready.sem, g_ready.at(m, i))
                        over_spans(2, pick_c[:, i % NS, :], c_parts).then_inc(cb_up.sem, 1)
                        if i >= 1:
                            sum_states(i - 1)
                    if n is not None:
                        for j in max_share(i):
                            max_scores(j)
                        if i == NSTEP // 2 - 1:
                            pe.wait_ge(smax_read.sem, smax_read.at(n, NMAX))
                            for k, (at, rows) in enumerate(ST):
                                last = nc.tensor.transpose(PS[0:H, 4 * BANK + at:4 * BANK + at + rows], q_max[0:rows, k, :],
                                                           ident[0:rows, 0:rows])
                            last.then_inc(maxT_up.sem, 1)
                        for j in unit_share(i):
                            scores(j)
                            if j >= 2:
                                times_v(j - 2)
                if n is not None:
                    times_v(NUNIT - 2)
                    times_v(NUNIT - 1)
                if m is not None:
                    sum_states(NSTEP - 1)
                if n is not None:
                    pe.wait_ge(o_copied.sem, o_copied.at(n, 4))
                    for k in range(NT):
                        for gr in range(2):
                            o = 4 * BANK + k * 2 * P + gr * P
                            last = nc.tensor.transpose(PS[0:TT, o:o + P], o_raw[:, gr, k:TOK:NT], ident[:, :])
                    last.then_inc(oTok_up.sem, 1)
                if m is not None:
                    pe.wait_ge(y_ready.sem, y_ready.at(m, NC_))
                    for k in range(NT):
                        for ck in range(NC_):
                            last = nc.tensor.matmul(PS[0:TT, 2 * BANK + k * C:2 * BANK + (k + 1) * C], conv_acc[:, ck, k * TT:(k + 1) * TT],
                                                    w_out_sb[:, ck, :], start=(ck == 0), stop=(ck == NC_ - 1))
                    last.then_inc(out_up.sem, 1)
                if n is not None:
                    pe.wait_ge(o_tok_ready.sem, o_tok_ready.at(n, 1))
                    channel_major(o_tok_v, 4).then_inc(oT_up.sem, 1)
                    pe.wait_ge(oT_ready.sem, oT_ready.at(n, 1))
                    for k in range(NT):
                        o = 6 * BANK + k * C
                        nc.tensor.matmul(PS[0:TT, o:o + C], oT[:, k * TT:(k + 1) * TT], proj_w_sb[:, :], start=True, stop=False)
                        last = nc.tensor.matmul(PS[0:TT, o:o + C], ones[0:1, 0:TT], proj_b_sb[:, :], start=False, stop=True)
                    last.then_inc(proj_up.sem, 1)
                    pe.wait_ge(ln2_ready.sem, ln2_ready.at(n, 1))
                    channel_major(f_tok, 4).then_inc(fT_up.sem, 1)
                    for k in range(NT):
                        last = nc.tensor.matmul(bank(6, 1), f_tok[:, k, :], ones[0:TT, 0:1], start=(k == 0), stop=(k == NT - 1))
                    last.then_inc(mean_up.sem, 1)
                if m is not None:
                    pe.wait_ge(ln1_ready.sem, ln1_ready.at(m, 1))
                    channel_major(ln1_tok, 0).then_inc(ln1T_up.sem, 1)

            turn(None, 0)
            with nc.tensor.Fori(0, B - 1) as n:
                turn(n, n + 1)
            turn(B - 1, None)

            pe.wait_ge(mean_read.sem, mean_read.at(B, 0))
            nc.tensor.matmul(PS[0:B, 0:NE], x_mean[:, :], w_r_sb[:, :], start=True, stop=False)
            nc.tensor.matmul(PS[0:B, 0:NE], ones[0:1, 0:B], b_r_sb[:, :], start=False, stop=True).then_inc(logits_up, 1)
            pe.wait_ge(routed, 1)
            nc.tensor.matmul(PS[0:B, BANK:BANK + NE], ones[0:B, 0:B], rt[:, 3, :], start=True, stop=True).then_inc(loads_up, 1)
            pe.wait_ge(w_diag_ready, 1)
            nc.tensor.matmul(bank(2, B * TOPK), ones[0:B, :], w_diag[:, :, :].rearrange("p b k -> p (b k)"),
                             start=True, stop=True).then_inc(w_all_up, 1)
            pe.wait_ge(w_all_ready, 1)

            with nc.tensor.Fori(0, B) as n:
                pe.wait_ge(e_w1_in.sem, e_w1_in.at(n, e_w1_in.per_turn))
                for i in range(TOPK * FC):
                    k, fc = divmod(i, FC)
                    if i >= 2:
                        pe.wait_ge(h_ready.sem, h_ready.at(n, i - 1))
                    over_spans(2 * (i % 2), w1_e[:, k, fc * P:(fc + 1) * P], fT).then_inc(h_up.sem, 1)
                pe.wait_ge(h_ready.sem, h_ready.at(n, TOPK * FC))
                pe.wait_ge(e_w2_scaled.sem, e_w2_scaled.at(n, 1))
                pe.wait_ge(res_read.sem, res_read.at(n, 0))
                for kt in range(NT):
                    o = 4 * BANK + kt * C
                    for i in range(TOPK * FC):
                        nc.tensor.matmul(PS[0:TT, o:o + C], hidden[i][:, kt * TT:(kt + 1) * TT], w2_s[:, i // FC, i % FC, :],
                                         start=(i == 0), stop=False)
                    last = nc.tensor.matmul(PS[0:TT, o:o + C], ones[0:1, 0:TT], b2_s[:, :], start=False, stop=True)
                last.then_inc(y_e_up.sem, 1)


_NAMES = ['x', 'L0_conv_W_in', 'L0_conv_conv_w', 'L0_conv_conv_b', 'L0_conv_W_xproj', 'L0_conv_W_dt', 'L0_conv_b_dt',
          'L0_conv_A_log', 'L0_conv_D_skip', 'L0_conv_W_out', 'L0_conv_ln_w', 'L1_attn_W', 'L1_attn_proj_w',
          'L1_attn_proj_b', 'L1_ffn_Wr', 'L1_ffn_br', 'L1_ffn_W1', 'L1_ffn_b1', 'L1_ffn_W2', 'L1_ffn_b2',
          'L1_ffn_gamma', 'L1_ffn_beta']
_TRANSPOSED = ('L0_conv_W_in', 'L0_conv_W_xproj', 'L0_conv_W_dt', 'L0_conv_W_out')

_BY_PARTITION = ('L0_conv_conv_b', 'L0_conv_b_dt', 'L0_conv_D_skip', 'L1_ffn_b1')


def kernel(**inputs):
    import numpy as _np
    import concourse.bacc as _bacc
    from concourse import mybir as _mybir
    from concourse.bass_utils import run_bass_kernel_spmd as _run

    nc = _bacc.Bacc("TRN2", target_bir_lowering=False, num_devices=1)
    arrays, args = {}, []
    for name in _NAMES:
        a = _np.asarray(inputs[name])
        if name in _TRANSPOSED:
            a = a.T
        if name in _BY_PARTITION:
            a = _np.swapaxes(a.reshape(*a.shape[:-1], -1, 128), -1, -2)
        a = _np.ascontiguousarray(a)
        arrays[f"in_{name}"] = a
        args.append(nc.dram_tensor(f"in_{name}", a.shape, _mybir.dt.from_np(a.dtype), kind="ExternalInput").ap())
    shape = arrays["in_x"].shape
    out = nc.dram_tensor("out_0", shape, _mybir.dt.float32, kind="ExternalOutput").ap()
    mamba_attention_moe(nc, *args, out)
    r = _run(nc, [arrays], core_ids=[0])
    return r.results[0]["out_0"]
```

```python
import concourse.bass as bass
from concourse import mybir
from contextlib import ExitStack


class Signal:

    def __init__(self, sem, per_turn, primed=0):
        self.sem = sem
        self.per_turn = per_turn
        self.primed = primed

    def at(self, turn, k):
        return turn * self.per_turn + k + self.primed


class Order:

    def __init__(self, sem, per_turn):
        self.sem = sem
        self.per_turn = per_turn
        self.count = 0

    def after(self, engine, turn, ins):
        self.count += 1
        ins.then_inc(self.sem, 1)
        engine.wait_ge(self.sem, turn * self.per_turn + self.count)


def mamba_attention_moe(nc, x, w_in_t, conv_w, conv_b, w_xp_t, w_dt_t, b_dt, a_log, d_skip, w_out_t,
                        ln_w, w_qkv, proj_w, proj_b, w_r, b_r, w1, b1, w2, b2, gamma, beta, out):
    f32 = mybir.dt.float32
    bf16 = mybir.dt.bfloat16
    u32 = mybir.dt.uint32
    ACT = mybir.ActivationFunctionType
    ALU = mybir.AluOpType
    X = mybir.AxisListType.X

    B, T, J, C = x.shape
    TOK = T * J
    P = 128
    GROUP = C // 32
    DI = w_out_t.shape[0]
    NC_ = DI // P
    NS = a_log.shape[1]
    TAPS = conv_w.shape[1]
    RANK = w_dt_t.shape[0]
    H = 8
    HD = C // H
    NE, _, F = w1.shape
    FC = F // P
    TOPK = 2
    TT = 100
    NT = TOK // TT
    HALF = TOK // 2
    ST = [(k * P, min(P, TOK - k * P)) for k in range((TOK + P - 1) // P)]
    NST = len(ST)
    BANK = 512
    SPANS = [(0, BANK), (BANK, TOK - BANK)]
    ATT_SCALE = float(C) ** -0.5
    CAPACITY = float(-(-(B * TOK * 5 // 4) // NE))
    Q_PARTS = [0, 0, 1, 1, 0, 2]
    K_PARTS = [0, 1, 0, 1, 2, 0]
    LOWEST = -3.4e38
    KST = len(Q_PARTS) * HD
    DT0 = 96

    x_v = x.rearrange("n t j c -> n (t j) c").rearrange("n (k p) c -> n p k c", p=TT)
    out_v = out.rearrange("n t j c -> n (t j) c").rearrange("n (k p) c -> n p k c", p=TT)

    ctx = ExitStack()
    with ctx:
        def sb(name, shape, dt=f32):
            return ctx.enter_context(nc.sbuf_tensor(name, shape, dt))

        def sem(name):
            return ctx.enter_context(nc.semaphore(name))

        def sig(name, per_turn=1):
            return Signal(sem(name), per_turn)

        freed = []

        def freeing(name, per_turn=1):
            freed.append(Signal(sem(name), per_turn, primed=1))
            return freed[-1]

        w_in_sb = sb("w_in_sb", [P, 2 * DI])
        conv_w_sb = sb("conv_w_sb", [P, NC_, TAPS])
        conv_b_sb = sb("conv_b_sb", [P, NC_])
        w_xp_sb = sb("w_xp_sb", [P, NC_, P])
        w_dt_sb = sb("w_dt_sb", [P, DI])
        b_dt_sb = sb("b_dt_sb", [P, NC_])
        a_sb = sb("a_sb", [P, NC_, NS])
        d_skip_sb = sb("d_skip_sb", [P, NC_])
        w_out_sb = sb("w_out_sb", [P, NC_, C])
        ln_w_sb = sb("ln_w_sb", [TT, C])
        w_qkv_sb = sb("w_qkv_sb", [P, 3 * C])
        proj_w_sb = sb("proj_w_sb", [P, C])
        proj_b_sb = sb("proj_b_sb", [1, C])
        w_r_sb = sb("w_r_sb", [P, NE])
        b_r_sb = sb("b_r_sb", [1, NE])
        gamma_sb = sb("gamma_sb", [TT, C])
        beta_sb = sb("beta_sb", [TT, C])
        ident = sb("ident", [P, P])
        ident_bf = sb("ident_bf", [P, P], bf16)
        group_avg = sb("group_avg", [P, P])
        ones = sb("ones", [P, P])
        neg_half = sb("neg_half", [P, NT])
        x_mean = sb("x_mean", [P, B])

        def by_chunk(name):
            return sb(name, [P, NC_, TOK])

        x_tok = sb("x_tok", [TT, NT, C])
        chan_stats = sb("chan_stats", [P, 2, 6])
        NPART = 4
        part_mean = chan_stats[:, :, :].rearrange("p a (b c) -> p (a b) c", c=3)[:, :, 1]
        part_m2 = chan_stats[:, :, :].rearrange("p a (b c) -> p (a b) c", c=3)[:, :, 2]
        part_dev = sb("part_dev", [P, NPART])
        grp = sb("grp", [P, 6])
        xnT = sb("xnT", [P, TOK])
        conv_acc, z_act, xc, dt_sb, sp_e, sp_l = map(by_chunk, ("conv_acc", "z_act", "xc", "dt_sb", "sp_e", "sp_l"))
        xd = sb("xd", [P, TOK])
        NBB = 2
        b_all = sb("b_all", [P, NBB, TOK])
        c_all = sb("c_all", [P, NBB, TOK])
        dbu = sb("dbu", [P, 2, TOK])
        dA = sb("dA", [P, 2, TOK])
        hst = sb("hst", [P, 2, TOK])
        g = sb("g", [P, 2, TOK])
        x_sum = sb("x_sum", [TT, NT, C])
        rms_v = sb("rms_v", [TT, 3, NT])

        def over(tile, size, rows=P, **dims):
            spec = " ".join(dims)
            return tile[0:rows, :, :].rearrange("p a b -> p (a b)")[:, 0:size].rearrange(f"p ({spec}) -> p {spec}", **dims)

        sq = over(hst, NT * C, rows=TT, k=NT, c=C)
        o_rms = over(dbu, NT * C, rows=TT, k=NT, c=C)

        def norm_tiles(name):
            return {k: sb(f"{name}_{k}", [TT, a, NT]) if k != "stats" else sb(f"{name}_{k}", [TT, NT, a])
                    for k, a in (("stats", 6), ("mv", 3), ("r", 2))}

        norm1 = norm_tiles("norm1")
        norm2 = norm_tiles("norm2")
        t1 = sb("t1", [TT, NT, C])
        ln1_tok = over(g, NT * C, rows=TT, k=NT, c=C)
        lnT = sb("lnT", [P, TOK])
        q_part = sb("q_part", [P, 3, TOK], bf16)
        k_part = sb("k_part", [P, 3, TOK], bf16)
        part_rest = sb("part_rest", [P, TOK])
        v_ext = sb("v_ext", [P, NST, H, 32])
        NPROB = 8
        probs = sb("probs", [P, NPROB, HALF])
        q_stack = sb("q_stack", [KST + 3, H, TOK], bf16)
        k_stack = sb("k_stack", [KST + 3, H, TOK], bf16)
        k_neg = sb("k_neg", [KST, H, HALF], bf16)
        q_max = sb("q_max", [P, NST, H])
        q_max_rest = sb("q_max_rest", [P, NST, H])
        q_max_parts = sb("q_max_parts", [P, NST, H, 3], bf16)
        m_rows = sb("m_rows", [H * 3, TOK], bf16)
        o_raw = sb("o_raw", [P, 2, TOK])
        o_rec = sb("o_rec", [TT, NT * H])
        o_tok = sb("o_tok", [TT, H, NT, HD])
        oT = part_rest
        o_tok_v = o_tok[:, :, :, :].rearrange("p h i d -> p h (i d)")
        t2 = sb("t2", [TT, NT, C])
        f_tok = over(sp_e, NT * C, rows=TT, k=NT, c=C)
        fT = o_raw[:, 0, :]
        def pair(tile, size, rows=P, **dims):
            both = over(tile, 2 * size, rows, z=2, **{"s": size})
            spec = " ".join(dims)
            return [both[:, z, :].rearrange(f"p ({spec}) -> p {spec}", **dims) for z in range(2)]

        w1_e = pair(conv_acc, TOPK * F, k=TOPK, f=F)
        w2_e = pair(dt_sb, TOPK * F, k=TOPK, a=FC, c=C)
        w2_s = pair(xc, TOPK * F, k=TOPK, a=FC, c=C)
        fT_e = [dbu[:, z, :] for z in range(2)]
        hidden = [[t[:, i, :] for t in tiles for i in range(2)] for tiles in ((dA, hst), (z_act, sp_e))]
        f_e = pair(probs, NT * C, rows=TT, k=NT, c=C)
        t2_e = [over(t, NT * C, rows=TT, k=NT, c=C) for t in (b_all, c_all)]
        fin_e = [x_tok, x_sum]
        b1_e = [sb(f"b1_e{z}", [P, TOPK, FC]) for z in range(2)]
        b2_e = [sb(f"b2_e{z}", [TT, TOPK, C]) for z in range(2)]
        b2_s = [sb(f"b2_s{z}", [TT, C]) for z in range(2)]
        rt = sb("rt", [NE, 16, NE])
        top_v = sb("top_v", [B, 8])
        top_i = sb("top_i", [B, 8], u32)
        top_w = sb("top_w", [B, 4])
        w_diag = sb("w_diag", [B, B, TOPK])
        w_all = sb("w_all", [P, B * TOPK])
        idx = sb("idx", [1, B * TOPK], u32)

        PS = ctx.enter_context(nc.psum_tensor("PS", [P, 8 * BANK], f32))

        def bank(b, cols=BANK):
            return PS[:, b * BANK:b * BANK + cols]

        def wide(b):
            return PS[:, b * BANK:b * BANK + TOK]

        def halves(b):
            return PS[:, b * BANK:(b + 2) * BANK].rearrange("p (a t) -> p a t", a=2)[:, :, 0:HALF]

        def tokens(b):
            return PS[0:TT, b * BANK:(b + 2) * BANK].rearrange("p (k c) -> p k c", c=C)

        parts_dram = nc.dram_tensor("parts_dram", (2, P, 3, TOK), bf16).ap()
        b_dram = nc.dram_tensor("b_dram", (NS, TOK), f32).ap()
        c_dram = nc.dram_tensor("c_dram", (NS, TOK), f32).ap()
        t2_dram = nc.dram_tensor("t2_dram", (B, TT, NT * C), f32).ap()
        f_dram = nc.dram_tensor("f_dram", (B, TT, NT * C), f32).ap()
        fT_dram = nc.dram_tensor("fT_dram", (B, P, TOK), f32).ap()
        top_dram = nc.dram_tensor("top_dram", (B, TOPK), u32).ap()

        weights_in = sem("weights_in")
        weights_set = sem("weights_set")
        consts_pool = sem("consts_pool")
        consts_dve = sem("consts_dve")
        pads_set = sem("pads_set")
        a_exp = sem("a_exp")
        x_in = sig("x_in", 16)
        xT_up = sig("xT_up")
        chan_ready = sig("chan_ready")
        gmean_up = sig("gmean_up")
        gdev_ready = sig("gdev_ready")
        gvar_up = sig("gvar_up")
        gvar_ready = sig("gvar_ready")
        gstd_ready = sig("gstd_ready")
        xn_ready = sig("xn_ready")
        xz_up = sig("xz_up", 4)
        conv_done = sig("conv_done", 2)
        silu_done = sig("silu_done", 4)
        gn_tok_up = sig("gn_tok_up")
        xs_ready = freeing("xs_ready")
        xd_up = sig("xd_up")
        xd_ready = sig("xd_ready")
        bc_out = sig("bc_out", 32)
        dt_up = sig("dt_up", 2)
        dt_abs = sig("dt_abs", 2)
        dt_relu = sig("dt_relu", 2)
        sp_exp = sig("sp_exp")
        sp_ln = sig("sp_ln")
        sp_u = sig("sp_u")
        sp_rest1 = sig("sp_rest1")
        sp_low1 = sig("sp_low1")
        dt_ready = sig("dt_ready", NC_)
        u_ready = sig("u_ready", NC_)
        NSTEP = NC_ * NS
        MAX_FROM, MAX_TO = 3, 8
        UNIT_FROM, UNIT_TO = MAX_TO + 4, NSTEP - 6
        PAIR_FROM = MAX_TO // 4 * 4 + 4

        def paired(i):
            return i >= PAIR_FROM and i // NC_ % 2 == 1

        def summed(i):
            return i < NSTEP and not paired(i + NC_)

        def sums(i):
            return sum(map(summed, range(i)))

        b_in = [sig(f"b_in{k}", 16 * NS // NBB) for k in range(NBB)]
        c_in = [sig(f"c_in{k}", 16 * NS // NBB) for k in range(NBB)]
        dbu_ready = sig("dbu_ready", NSTEP)
        dA_ready = sig("dA_ready", NSTEP)
        scan_done = sig("scan_done", NSTEP)
        g_ready = sig("g_ready", NSTEP)
        g_added = sig("g_added", sum(map(paired, range(NSTEP))))
        y_up = sig("y_up", sums(NSTEP))
        y_summed = sig("y_summed", NC_)
        y_ready = [sig(f"y_ready{k}") for k in range(NC_)]
        out_up = sig("out_up")
        rms_sq = sig("rms_sq")
        ms_ready = sig("ms_ready")
        rms_ready = sig("rms_ready")
        normed = sig("normed")
        weighted = sig("weighted")
        ln1_var = sig("ln1_var")
        ln1_std = sig("ln1_std")
        ln1_ready = sig("ln1_ready")
        ln1T_up = sig("ln1T_up")
        ln1T_ready = sig("ln1T_ready")
        q_up = sig("q_up")
        k_up = sig("k_up")
        v_up = sig("v_up")
        qk_first = sig("qk_first", 2)
        qk_parts = sig("qk_parts", 2)
        v_copied = sig("v_copied")
        parts_out = sig("parts_out", 32)
        NSTK = 2 * len(Q_PARTS)
        stacks_in = sig("stacks_in", 16 * NSTK)
        NMAX = NST * H
        diff_up = sig("diff_up", NMAX)
        smax_up = sig("smax_up", NMAX)
        k_neg_ready = sig("k_neg_ready")
        relu_ready = sig("relu_ready", NMAX)
        tile_seen = sig("tile_seen", NMAX)
        smax_read = sig("smax_read", NMAX)
        max_split = sig("max_split")
        maxT_up = sig("maxT_up")
        m_rows_ready = sig("m_rows_ready")
        max_in = sig("max_in", 16 * H)
        NUNIT = 2 * 2 * NST * 4
        PER_ACC = NST * 4
        s_up = sig("s_up", NUNIT)
        probs_ready = sig("probs_ready", NUNIT)
        pv_up = sig("pv_up", NUNIT // 4)
        o_copied = sig("o_copied", 4)
        oTok_up = sig("oTok_up")
        o_tok_ready = sig("o_tok_ready")
        oT_up = sig("oT_up")
        oT_ready = sig("oT_ready")
        proj_up = sig("proj_up")
        t2_ready = freeing("t2_ready")
        ln2_var = sig("ln2_var")
        ln2_std = sig("ln2_std")
        ln2_ready = sig("ln2_ready")
        mean_read = freeing("mean_read")
        fT_up = sig("fT_up")
        fT_ready = freeing("fT_ready")
        f_out = freeing("f_out", 16 * 3)
        means_ready = sem("means_ready")
        logits_up = sem("logits_up")
        rt_ready = sem("rt_ready")
        rt_exp = sem("rt_exp")
        routed = sem("routed")
        loads_up = sem("loads_up")
        top_ready = sem("top_ready")
        top_moved = sem("top_moved")
        w_diag_ready = sem("w_diag_ready")
        w_all_up = sem("w_all_up")
        w_all_ready = sem("w_all_ready")
        def sigs(name, per_turn=1):
            return [sig(f"{name}{z}", per_turn) for z in range(2)]

        def freeings(name, per_turn=1):
            return [freeing(f"{name}{z}", per_turn) for z in range(2)]

        e_w1_in = sigs("e_w1_in", 16 * (2 * TOPK + 1))
        e_w2_in = sigs("e_w2_in", 16 * TOPK)
        e_f_in = sigs("e_f_in", 16 * (1 + TOPK))
        e_t2_in = sigs("e_t2_in", 16)
        e_w2_scaled = freeings("e_w2_scaled")
        h_up = sigs("h_up", TOPK * FC)
        h_ready = freeings("h_ready", TOPK * FC)
        y_e_up = freeings("y_e_up")
        res_read = freeings("res_read")
        lnf_var = sigs("lnf_var")
        lnf_std = sigs("lnf_std")
        lnf_ready = sigs("lnf_ready")
        lnf_read = freeings("lnf_read")
        fin_ready = freeings("fin_ready")
        out_stored = sigs("out_stored", 16)

        dve_order_m = Order(sem("dve_order_m"), 13)
        dve_order_t = Order(sem("dve_order_t"), 5)
        dve_order_a = Order(sem("dve_order_a"), 12)
        dve_order_rt = Order(sem("dve_order_rt"), 0)
        dve_order_e = Order(sem("dve_order_e"), 14)
        act_order = Order(sem("act_order"), 0)
        pool_order = Order(sem("pool_order"), 0)

        block = ctx.enter_context(nc.Block())

        def share(i, first, end, work):
            lo, hi = max(i - first, 0), max(i + 1 - first, 0)
            return range(min(lo * work // (end - first), work), min(hi * work // (end - first), work))

        def max_share(i):
            return share(i, MAX_FROM, MAX_TO, NMAX)

        def unit_share(i):
            return share(i, UNIT_FROM, UNIT_TO, NUNIT)

        def unit(i):
            acc, rest = divmod(i, PER_ACC)
            kt, q = divmod(rest, 4)
            return acc, kt, q, 4 * (acc // 2) + q, (acc % 2) * HALF

        def in_tj(ap):
            return ap.rearrange("p (t j) -> p j t", j=J)

        def by_jt(ap):
            return ap.rearrange("p (j t) -> p j t", j=J)

        NW = [0]

        @block.sync
        def _(sp):
            def load(dst, src):
                NW[0] += 16
                sp.dma_start(dst, src).then_inc(weights_in, 16)

            def load_x(m):
                sp.dma_start(x_tok[:, :, :], x_v[bass.ds(m, 1)].rearrange("o p k c -> (o p) k c")).then_inc(x_in.sem, 16)

            load_x(0)
            load(w_in_sb[:, :], w_in_t)
            load(conv_w_sb[:, :, :], conv_w.rearrange("(c p) k -> p c k", p=P))
            load(conv_b_sb[:, :], conv_b)
            load(b_dt_sb[:, :], b_dt)
            load(a_sb[:, :, :], a_log.rearrange("(c p) s -> p c s", p=P))
            load(d_skip_sb[:, :], d_skip)
            load(w_out_sb[:, :, :], w_out_t.rearrange("(c p) o -> p c o", p=P))
            load(ln_w_sb[:, :], ln_w.rearrange("(o c) -> o c", o=1).to_broadcast([TT, C]))
            load(w_qkv_sb[:, :], w_qkv)
            load(proj_w_sb[:, :], proj_w)
            load(proj_b_sb[:, :], proj_b.rearrange("(o c) -> o c", o=1))
            load(w_r_sb[:, :], w_r)
            load(b_r_sb[:, :], b_r.rearrange("(o c) -> o c", o=1))
            load(gamma_sb[:, :], gamma.rearrange("(o c) -> o c", o=1).to_broadcast([TT, C]))
            load(beta_sb[:, :], beta.rearrange("(o c) -> o c", o=1).to_broadcast([TT, C]))
            sp.wait_ge(weights_set, 1)
            xp_v = w_xp_t.rearrange("(c p) e -> p c e", p=P)
            load(w_xp_sb[:, :, 0:NS], xp_v[:, :, RANK + NS:RANK + 2 * NS])
            load(w_xp_sb[:, :, DT0:DT0 + RANK + NS], xp_v[:, :, 0:RANK + NS])
            load(w_dt_sb[DT0:DT0 + RANK, :], w_dt_t)

            def load_bc(m, state):
                k, last = state % NBB, (state - NBB + 1) * NC_
                if last > 0:
                    sp.wait_ge(dbu_ready.sem, dbu_ready.at(m, last))
                sp.dma_start(b_all[:, k, :], b_dram[state:state + 1, :].to_broadcast([P, TOK])).then_inc(b_in[k].sem, 16)
                if last > 0:
                    sp.wait_ge(g_ready.sem, g_ready.at(m, last))
                sp.dma_start(c_all[:, k, :], c_dram[state:state + 1, :].to_broadcast([P, TOK])).then_inc(c_in[k].sem, 16)

            def turn(n, m):
                if n is not None and m is not None:
                    sp.wait_ge(xs_ready.sem, xs_ready.at(m, 0))
                    load_x(m)
                if m is not None:
                    sp.wait_ge(xd_ready.sem, xd_ready.at(m, 1))
                    sp.dma_start(b_dram, xd[DT0 + RANK:P, :]).then_inc(bc_out.sem, 16)
                    sp.dma_start(c_dram, xd[0:NS, :]).then_inc(bc_out.sem, 16)
                    sp.wait_ge(bc_out.sem, bc_out.at(m, 32))
                    for state in range(NBB):
                        load_bc(m, state)
                if n is not None:
                    for i, part in enumerate((q_part, k_part)):
                        sp.wait_ge(qk_parts.sem, qk_parts.at(n, i + 1))
                        sp.dma_start(parts_dram[i], part[:, :, :]).then_inc(parts_out.sem, 16)
                    sp.wait_ge(parts_out.sem, parts_out.at(n, 32))
                    for i, (stack, which) in enumerate(((q_stack, Q_PARTS), (k_stack, K_PARTS))):
                        for r, a in enumerate(which):
                            sp.dma_start(stack[HD * r:HD * (r + 1), :, :],
                                         parts_dram[i, :, a, :].rearrange("(h d) t -> d h t", h=H)
                                         ).then_inc(stacks_in.sem, 16)
                for state in range(NBB, NS):
                    if m is not None:
                        load_bc(m, state)
                    if n is not None and state == MAX_TO // NC_ + 1:
                        sp.wait_ge(m_rows_ready.sem, m_rows_ready.at(n, 1))
                        for h in range(H):
                            sp.dma_start(q_stack[KST:KST + 3, h, :], m_rows[3 * h:3 * (h + 1), :]).then_inc(max_in.sem, 16)
                if n is not None:
                    sp.wait_ge(ln2_ready.sem, ln2_ready.at(n, 1))
                    sp.dma_start(t2_dram[bass.ds(n, 1)].rearrange("o p f -> (o p) f"), t2[:, :, :].rearrange("p k c -> p (k c)")).then_inc(f_out.sem, 16)
                    sp.dma_start(f_dram[bass.ds(n, 1)].rearrange("o p f -> (o p) f"), f_tok.rearrange("p k c -> p (k c)")).then_inc(f_out.sem, 16)
                    sp.wait_ge(fT_ready.sem, fT_ready.at(n, 1))
                    sp.dma_start(fT_dram[bass.ds(n, 1)].rearrange("o p f -> (o p) f"), fT).then_inc(f_out.sem, 16)

            turn(None, 0)
            with nc.sync.Fori(0, B - 1) as n:
                turn(n, n + 1)
            turn(B - 1, None)

            sp.wait_ge(top_ready, 1)
            sp.dma_start(top_dram, top_i[:, 0:TOPK]).then_inc(top_moved, 16)
            sp.wait_ge(top_moved, 16)
            sp.dma_start(idx[:, :], top_dram.rearrange("(o b) k -> o (b k)", o=1)).then_inc(top_moved, 16)
            sp.wait_ge(top_moved, 32)
            sp.wait_ge(f_out.sem, f_out.at(B, 0))
            with nc.sync.Fori(0, B // 2) as n:
                for z in range(2):
                    bt = n * 2 + z
                    sp.wait_ge(h_ready[z].sem, h_ready[z].at(n, 0))
                    sp.dma_start(fT_e[z], fT_dram[bass.ds(bt, 1)].rearrange("o p f -> (o p) f")).then_inc(e_w1_in[z].sem, 16)
                    experts = []
                    for k in range(TOPK):
                        e = nc.sync.value_load(idx[0:1, bass.ds(bt * TOPK + k, 1)], min_val=0, max_val=NE - 1)
                        experts.append(e)
                        sp.dma_start(w1_e[z][:, k, :], w1[bass.ds(e, 1)].rearrange("o d f -> (o d) f")).then_inc(e_w1_in[z].sem, 16)
                        sp.dma_start(b1_e[z][:, k, :], b1[bass.ds(e, 1)].rearrange("o p c -> (o p) c")).then_inc(e_w1_in[z].sem, 16)
                    sp.wait_ge(e_w2_scaled[z].sem, e_w2_scaled[z].at(n, 0))
                    for k, e in enumerate(experts):
                        sp.dma_start(w2_e[z][:, k, :, :], w2[bass.ds(e, 1)].rearrange("o (c p) d -> (o p) c d", p=P)).then_inc(e_w2_in[z].sem, 16)
                    sp.wait_ge(res_read[z].sem, res_read[z].at(n, 0))
                    for k, e in enumerate(experts):
                        sp.dma_start(b2_e[z][:, k, :], b2[bass.ds(e, 1)].to_broadcast([TT, C])).then_inc(e_f_in[z].sem, 16)
                    sp.dma_start(f_e[z].rearrange("p k c -> p (k c)"), f_dram[bass.ds(bt, 1)].rearrange("o p f -> (o p) f")).then_inc(e_f_in[z].sem, 16)

        @block.gpsimd
        def _(pool):
            nc.gpsimd.memset(w_xp_sb[:, :, :], 0.0)
            nc.gpsimd.memset(w_dt_sb[:, :], 0.0).then_inc(weights_set, 1)
            nc.gpsimd.memset(ones[:, :], 1.0)
            nc.gpsimd.memset(neg_half[:, :], -0.5)
            pool_order.after(pool, 0, nc.gpsimd.memset(ident[:, :], 0.0))
            nc.gpsimd.affine_select(out=ident[:, :], in_=ident[:, :], compare_op=ALU.not_equal, fill=1.0,
                                    base=0, pattern=[[-1, P]], channel_multiplier=1)
            pool_order.after(pool, 0, nc.gpsimd.memset(group_avg[:, :], 1.0 / GROUP))
            ga = group_avg[:, :].rearrange("p (g i) -> p g i", i=GROUP)
            pool_order.after(pool, 0, nc.gpsimd.affine_select(
                out=ga, in_=ga, compare_op=ALU.is_ge, fill=0.0, base=0,
                pattern=[[-GROUP, P // GROUP], [0, GROUP]], channel_multiplier=1))
            nc.gpsimd.affine_select(out=ga, in_=ga, compare_op=ALU.is_ge, fill=0.0, base=GROUP - 1,
                                    pattern=[[GROUP, P // GROUP], [0, GROUP]],
                                    channel_multiplier=-1).then_inc(consts_pool, 1)

            def rsqrt(out_, in_):
                return nc.gpsimd.tensor_tensor(out_, in_, neg_half[0:in_.shape[0], 0:in_.shape[1]], ALU.pow)

            def turn(n, m):
                if m is not None:
                    pool.wait_ge(gvar_ready.sem, gvar_ready.at(m, 1))
                    rsqrt(grp[:, 4:5], grp[:, 3:4]).then_inc(gstd_ready.sem, 1)
                    if n is None:
                        pool.wait_ge(gstd_ready.sem, gstd_ready.at(m, 1))
                        pool_order.after(pool, 0, nc.gpsimd.memset(probs[:, :, :], 0.0))
                        pool_order.after(pool, 0, nc.gpsimd.memset(q_max[:, :, :], 0.0))
                        pool_order.after(pool, 0, nc.gpsimd.memset(v_ext[:, 0:NST - 1, :, :], 1.0))
                        pool_order.after(pool, 0, nc.gpsimd.memset(v_ext[:, NST - 1, :, :], 0.0))
                        pool_order.after(pool, 0, nc.gpsimd.memset(v_ext[0:ST[-1][1], NST - 1, :, :], 1.0))
                        nc.gpsimd.memset(k_stack[KST:KST + 3, :, :], 1.0).then_inc(pads_set, 1)
                        pool.wait_ge(pads_set, 1)
                if n is not None:
                    pool.wait_ge(ms_ready.sem, ms_ready.at(n, 1))
                    rsqrt(rms_v[:, 2, :], rms_v[:, 1, :]).then_inc(rms_ready.sem, 1)
                if n is not None:
                    pool.wait_ge(normed.sem, normed.at(n, 1))
                    nc.gpsimd.tensor_tensor(o_rms, o_rms, ln_w_sb[:, :].unsqueeze(1).to_broadcast([TT, NT, C]), ALU.mult).then_inc(weighted.sem, 1)
                    pool.wait_ge(ln1_var.sem, ln1_var.at(n, 1))
                    rsqrt(norm1["r"][:, 1, :], norm1["r"][:, 0, :]).then_inc(ln1_std.sem, 1)
                if m is not None:
                    pool.wait_ge(sp_u.sem, sp_u.at(m, 1))
                    nc.gpsimd.tensor_tensor(conv_acc[:, 1, :], sp_e[:, 1, :], conv_acc[:, 1, :], ALU.subtract).then_inc(sp_rest1.sem, 1)
                    pool.wait_ge(sp_rest1.sem, sp_rest1.at(m, 1))
                    pool.wait_ge(dt_relu.sem, dt_relu.at(m, NC_))
                    nc.gpsimd.tensor_tensor(dt_sb[:, 1, :], dt_sb[:, 1, :], conv_acc[:, 1, :], ALU.add).then_inc(sp_low1.sem, 1)
                for i in range(NSTEP):
                    if m is not None:
                        state, ck = divmod(i, NC_)
                        k = state % NBB
                        if state == 0:
                            pool.wait_ge(u_ready.sem, u_ready.at(m, ck + 1))
                        pool.wait_ge(b_in[k].sem, b_in[k].at(m, 16 * (state // NBB + 1)))
                        if i >= 2:
                            pool.wait_ge(scan_done.sem, scan_done.at(m, i - 1))
                        nc.gpsimd.tensor_tensor(dbu[:, i % 2, :], sp_l[:, ck, :], b_all[:, k, :],
                                                ALU.mult).then_inc(dbu_ready.sem, 1)
                    if n is not None and i == UNIT_TO + 4:
                        pool.wait_ge(ln2_var.sem, ln2_var.at(n, 1))
                        rsqrt(norm2["r"][:, 1, :], norm2["r"][:, 0, :]).then_inc(ln2_std.sem, 1)
                if m is not None:
                    pool.wait_ge(y_summed.sem, y_summed.at(m, 1))
                    nc.gpsimd.tensor_tensor(in_tj(conv_acc[:, 1, :]), by_jt(xc[:, 1, :]), by_jt(z_act[:, 1, :]),
                                            ALU.mult).then_inc(y_ready[1].sem, 1)

            turn(None, 0)
            with nc.gpsimd.Fori(0, B - 1) as n:
                turn(n, n + 1)
            turn(B - 1, None)

            with nc.gpsimd.Fori(0, B // 2) as n:
                for z in range(2):
                    pool.wait_ge(lnf_var[z].sem, lnf_var[z].at(n, 1))
                    rsqrt(norm1["r"][:, 1, :], norm1["r"][:, 0, :]).then_inc(lnf_std[z].sem, 1)
                    fin = fin_e[z][:, :, :]
                    pool.wait_ge(lnf_ready[z].sem, lnf_ready[z].at(n, 1))
                    nc.gpsimd.tensor_tensor(fin, ln1_tok, beta_sb[:, :].unsqueeze(1).to_broadcast([TT, NT, C]),
                                            ALU.add).then_inc(lnf_read[z].sem, 1)
                    pool.wait_ge(lnf_read[z].sem, lnf_read[z].at(n, 1))
                    pool.wait_ge(e_t2_in[z].sem, e_t2_in[z].at(n, 16))
                    nc.gpsimd.tensor_tensor(fin, fin, t2_e[z], ALU.add).then_inc(fin_ready[z].sem, 1)
                    pool.wait_ge(fin_ready[z].sem, fin_ready[z].at(n, 1))
                    pool.dma_start(out_v[bass.ds(n * 2 + z, 1)].rearrange("o p k c -> (o p) k c"), fin).then_inc(out_stored[z].sem, 16)
                for z in range(2):
                    pool.wait_ge(out_stored[z].sem, out_stored[z].at(n, 16))

        @block.scalar
        def _(act):
            act.wait_ge(weights_in, NW[0])
            act_order.after(act, 0, nc.scalar.activation(a_sb[:, :, :], a_sb[:, :, :], ACT.Exp))
            nc.scalar.mul(a_sb[:, :, :], a_sb[:, :, :], -1.0).then_inc(a_exp, 1)
            act.wait_ge(a_exp, 1)

            def in_jt(ap):
                return ap.rearrange("p (j t) -> p t j", j=J)

            def by_tj(ap):
                return ap.rearrange("p (t j) -> p t j", j=J)

            def turn(n, m):
                def silu_x(ck):
                    act.wait_ge(conv_done.sem, conv_done.at(m, ck + 1))
                    nc.scalar.activation(in_jt(xc[:, ck, :]), by_tj(conv_acc[:, ck, :]), ACT.Silu).then_inc(silu_done.sem, 1)

                def silu_z(ck):
                    act.wait_ge(xz_up.sem, xz_up.at(m, NC_ + ck + 1))
                    nc.scalar.activation(in_jt(z_act[:, ck, :]), by_tj(wide(2 * ck)), ACT.Silu).then_inc(silu_done.sem, 1)

                if n is not None:
                    act.wait_ge(out_up.sem, out_up.at(n, 1))
                    nc.scalar.activation(sq, tokens(4), ACT.Square).then_inc(rms_sq.sem, 1)
                if m is not None:
                    silu_x(0)
                    silu_z(0)
                    silu_x(1)
                    silu_z(1)
                    act.wait_ge(xd_up.sem, xd_up.at(m, 1))
                    nc.scalar.copy(xd[:, :], wide(0)).then_inc(xd_ready.sem, 1)
                if m is not None:
                    if n is not None:
                        act.wait_ge(f_out.sem, f_out.at(n, 0))
                    for ck in range(NC_):
                        act.wait_ge(dt_up.sem, dt_up.at(m, ck + 1))
                        nc.scalar.activation(sp_e[:, ck, :], wide(2 * ck), ACT.Abs, bias=b_dt_sb[:, ck:ck + 1]).then_inc(dt_abs.sem, 1)
                if n is not None:
                    act.wait_ge(ln1T_up.sem, ln1T_up.at(n, 1))
                    nc.scalar.copy(lnT[:, :].rearrange("p (a t) -> p a t", a=2), halves(6)).then_inc(ln1T_ready.sem, 1)
                if m is not None:
                    act.wait_ge(dt_abs.sem, dt_abs.at(m, NC_))
                    nc.scalar.activation(sp_e[:, :, :], sp_e[:, :, :], ACT.Exp, scale=-1.0).then_inc(sp_exp.sem, 1)
                if n is not None:
                    act.wait_ge(q_up.sem, q_up.at(n, 1))
                    nc.scalar.copy(q_part[:, 0, :], wide(4)).then_inc(qk_first.sem, 1)
                    act.wait_ge(k_up.sem, k_up.at(n, 1))
                    nc.scalar.copy(k_part[:, 0, :], wide(6)).then_inc(qk_first.sem, 1)
                if m is not None:
                    act.wait_ge(sp_exp.sem, sp_exp.at(m, 1))
                    nc.scalar.activation(sp_l[:, :, :], sp_e[:, :, :], ACT.Ln, bias=1.0).then_inc(sp_ln.sem, 1)
                for i in range(NSTEP):
                    if m is not None:
                        s, ck = divmod(i, NC_)
                        if s == 0:
                            act.wait_ge(dt_ready.sem, dt_ready.at(m, ck + 1))
                        if i >= 2:
                            act.wait_ge(scan_done.sem, scan_done.at(m, i - 1))
                        nc.scalar.activation(dA[:, i % 2, :].rearrange("p (j t) -> p j t", t=T)[:, :, 1:T],
                                             dt_sb[:, ck, :].rearrange("p (j t) -> p j t", t=T)[:, :, 1:T],
                                             ACT.Exp, scale=a_sb[:, ck, s:s + 1]).then_inc(dA_ready.sem, 1)
                    if n is not None:
                        if i == 0:
                            act.wait_ge(v_up.sem, v_up.at(n, 1))
                            nc.scalar.copy(v_ext[:, 0:NST - 1, :, 0:HD],
                                           PS[:, 4 * BANK:4 * BANK + (NST - 1) * C].rearrange("p (k h d) -> p k h d", k=NST - 1, h=H))
                            nc.scalar.copy(v_ext[0:32, NST - 1, :, 0:HD],
                                           PS[0:32, 4 * BANK + (NST - 1) * C:4 * BANK + NST * C].rearrange("p (h d) -> p h d", h=H)
                                           ).then_inc(v_copied.sem, 1)
                        for j in max_share(i):
                            for k in ([0, 1] if j == 0 else [j + 1] if j + 1 < NMAX else []):
                                rows = ST[k // H][1]
                                act.wait_ge(diff_up.sem, diff_up.at(n, k + 1))
                                if k >= NPROB:
                                    act.wait_ge(smax_read.sem, smax_read.at(n, k - NPROB + 1))
                                nc.scalar.activation(probs[0:rows, k % NPROB, :], bank(5 + 2 * (k % 2), HALF)[0:rows], ACT.Relu
                                                     ).then_inc(relu_ready.sem, 1)
                        if i == MAX_TO:
                            act.wait_ge(maxT_up.sem, maxT_up.at(n, 1))
                            nc.scalar.copy(m_rows[:, :], PS[0:3 * H, 4 * BANK:4 * BANK + TOK]).then_inc(m_rows_ready.sem, 1)
                        for j in unit_share(i):
                            rows = ST[unit(j)[1]][1]
                            act.wait_ge(s_up.sem, s_up.at(n, j + 1))
                            if j >= NPROB and j % 4 == 0:
                                act.wait_ge(pv_up.sem, pv_up.at(n, (j - NPROB) // 4 + 1))
                            nc.scalar.activation(probs[0:rows, j % NPROB, :], bank(4 + j % 3, HALF)[0:rows], ACT.Exp,
                                                 scale=ATT_SCALE).then_inc(probs_ready.sem, 1)
                        if i == UNIT_TO + 2:
                            act.wait_ge(oT_up.sem, oT_up.at(n, 1))
                            nc.scalar.copy(oT[:, :].rearrange("p (a t) -> p a t", a=2), halves(4)).then_inc(oT_ready.sem, 1)
                        if i == UNIT_TO + 5:
                            act.wait_ge(fT_up.sem, fT_up.at(n, 1))
                            nc.scalar.copy(fT.rearrange("p (a t) -> p a t", a=2), halves(4)).then_inc(fT_ready.sem, 1)

            turn(None, 0)
            act.wait_ge(pads_set, 1)
            with nc.scalar.Fori(0, B - 1) as n:
                turn(n, n + 1)
            turn(B - 1, None)

            for i in range(3):
                act.wait_ge(rt_ready, i + 1)
                src, dst = [(rt[:, 1, :], rt[:, 2, :]), (rt[:, 5, :], rt[:, 6, :]), (top_w[:, 0:1], top_w[:, 1:2])][i]
                nc.scalar.activation(dst, src, ACT.Exp).then_inc(rt_exp, 1)

            act.wait_ge(w_all_ready, 1)
            with nc.scalar.Fori(0, B // 2) as n:
                for z in range(2):
                    act.wait_ge(e_w1_in[z].sem, e_w1_in[z].at(n, e_w1_in[z].per_turn))
                    act.wait_ge(y_e_up[z].sem, y_e_up[z].at(n, 0))
                    for i in range(TOPK * FC):
                        k, fc = divmod(i, FC)
                        act.wait_ge(h_up[z].sem, h_up[z].at(n, i + 1))
                        nc.scalar.activation(hidden[z][i], wide(2 * (i % 2)), ACT.Gelu, bias=b1_e[z][:, k, fc:fc + 1]).then_inc(h_ready[z].sem, 1)
                    act.wait_ge(e_w2_in[z].sem, e_w2_in[z].at(n, e_w2_in[z].per_turn))
                    for k in range(TOPK):
                        last = nc.scalar.activation(w2_s[z][:, k, :, :], w2_e[z][:, k, :, :], ACT.Copy,
                                                    scale=w_all[:, bass.ds(n * 2 * TOPK + z * TOPK + k, 1)])
                    last.then_inc(e_w2_scaled[z].sem, 1)
                    act.wait_ge(fin_ready[z].sem, fin_ready[z].at(n, 0))
                    act.dma_start(t2_e[z].rearrange("p k c -> p (k c)"), t2_dram[bass.ds(n * 2 + z, 1)].rearrange("o p f -> (o p) f")).then_inc(e_t2_in[z].sem, 16)

        @block.vector
        def _(dve):
            for signal in freed:
                dve.sem_inc(signal.sem, 1)
            nc.vector.memset(dA[:, :, :], 0.0)
            dve.wait_ge(consts_pool, 1)
            nc.vector.tensor_copy(ident_bf[:, :], ident[:, :])
            nc.vector.memset(w_diag[:, :, :], 0.0).then_inc(consts_dve, 1)

            def norm_stats(then, tiles, src, eps):
                stats, mv, r = tiles["stats"], tiles["mv"], tiles["r"]
                for k in range(NT):
                    last = nc.vector.bn_stats(stats[:, k, :], src[:, k, :])
                then(last)
                even_m, even_m2, odd_m, odd_m2 = (stats[:, :, c] for c in (1, 2, 4, 5))
                nc.vector.tensor_tensor(mv[:, 0, :], even_m, odd_m, ALU.add)
                nc.vector.tensor_tensor(mv[:, 1, :], even_m, odd_m, ALU.subtract)
                then(nc.vector.tensor_tensor(mv[:, 2, :], even_m2, odd_m2, ALU.add))
                nc.vector.tensor_scalar(mv[:, 0, :], mv[:, 0, :], 0.5, None, ALU.mult)
                nc.vector.scalar_tensor_tensor(mv[:, 1, :], mv[:, 1, :], 0.25, mv[:, 1, :], ALU.mult, ALU.mult)
                then(nc.vector.tensor_scalar(mv[:, 2, :], mv[:, 2, :], 1.0 / C, eps, ALU.mult, ALU.add))
                return nc.vector.tensor_tensor(r[:, 0, :], mv[:, 2, :], mv[:, 1, :], ALU.add)

            def norm_apply(tiles, src, dst):
                for k in range(NT):
                    last = nc.vector.tensor_scalar(dst[:, k, :], src[:, k, :], tiles["mv"][:, 0, k:k + 1],
                                                   tiles["r"][:, 1, k:k + 1], ALU.subtract, ALU.mult)
                return last

            def turn(n, m):
                dve_order_m.count = 0
                dve_order_a.count = 0
                dve_order_t.count = 0

                def mthen(ins):
                    dve_order_m.after(dve, m, ins)

                def tthen(ins):
                    dve_order_t.after(dve, n, ins)

                def athen(ins):
                    dve_order_a.after(dve, n, ins)

                def low_parts(i):
                    part, b = ((q_part, 4), (k_part, 6))[i]
                    dve.wait_ge(qk_first.sem, qk_first.at(n, i + 1))
                    athen(nc.vector.tensor_tensor(part_rest[:, :], wide(b), part[:, 0, :], ALU.subtract))
                    athen(nc.vector.tensor_copy(part[:, 1, :], part_rest[:, :]))
                    nc.vector.tensor_tensor(part[:, 2, :], part_rest[:, :], part[:, 1, :], ALU.subtract).then_inc(qk_parts.sem, 1)
                    dve.wait_ge(qk_parts.sem, qk_parts.at(n, i + 1))

                if m is not None:
                    dve.wait_ge(xT_up.sem, xT_up.at(m, 1))
                    nc.vector.bn_stats(chan_stats[:, 0, :], bank(2, HALF))
                    nc.vector.bn_stats(chan_stats[:, 1, :], bank(3, HALF)).then_inc(chan_ready.sem, 1)
                if m is not None:
                    dve.wait_ge(gmean_up.sem, gmean_up.at(m, 1))
                    mthen(nc.vector.reduce_sum(grp[:, 1:2], bank(0, NPART), X))
                    mthen(nc.vector.tensor_scalar(grp[:, 0:1], grp[:, 1:2], 1.0 / NPART, None, ALU.mult))
                    mthen(nc.vector.tensor_scalar(part_dev[:, :], part_mean, grp[:, 0:1], None, ALU.subtract))
                    mthen(nc.vector.tensor_tensor(part_dev[:, :], part_dev[:, :], part_dev[:, :], ALU.mult))
                    nc.vector.scalar_tensor_tensor(part_dev[:, :], part_m2, float(NPART) / TOK, part_dev[:, :],
                                                   ALU.mult, ALU.add).then_inc(gdev_ready.sem, 1)
                    dve.wait_ge(gvar_up.sem, gvar_up.at(m, 1))
                    mthen(nc.vector.reduce_sum(grp[:, 2:3], bank(1, NPART), X))
                    nc.vector.tensor_scalar(grp[:, 3:4], grp[:, 2:3], 1.0 / NPART, 1e-5, ALU.mult, ALU.add).then_inc(gvar_ready.sem, 1)
                if m is not None:
                    dve.wait_ge(gstd_ready.sem, gstd_ready.at(m, 1))
                    nc.vector.tensor_scalar(xnT[:, :].rearrange("p (a t) -> p a t", a=2), halves(2), grp[:, 0:1], grp[:, 4:5],
                                            ALU.subtract, ALU.mult).then_inc(xn_ready.sem, 1)

                def convolve(ck):
                    dve.wait_ge(xz_up.sem, xz_up.at(m, ck + 1))
                    src = wide(2 * ck)
                    mthen(nc.vector.tensor_scalar(conv_acc[:, ck, :], src, conv_w_sb[:, ck, TAPS - 1:TAPS],
                                                  conv_b_sb[:, ck:ck + 1], ALU.mult, ALU.add))
                    for back in range(1, TAPS):
                        ins = nc.vector.scalar_tensor_tensor(
                            conv_acc[:, ck, back * J:], src[:, 0:TOK - back * J],
                            conv_w_sb[:, ck, TAPS - 1 - back:TAPS - back], conv_acc[:, ck, back * J:], ALU.mult, ALU.add)
                        if back < TAPS - 1:
                            mthen(ins)
                    ins.then_inc(conv_done.sem, 1)

                if m is not None:
                    if n is None:
                        dve.wait_ge(weights_in, NW[0])
                    convolve(0)
                if n is not None:
                    dve.wait_ge(rms_sq.sem, rms_sq.at(n, 1))
                    tthen(nc.vector.reduce_sum(rms_v[:, 0, :], sq, X))
                    nc.vector.tensor_scalar(rms_v[:, 1, :], rms_v[:, 0, :], 1.0 / C, 1e-6, ALU.mult, ALU.add).then_inc(ms_ready.sem, 1)
                if m is not None:
                    convolve(1)
                if n is not None:
                    dve.wait_ge(rms_ready.sem, rms_ready.at(n, 1))
                    nc.vector.tensor_tensor(o_rms, tokens(4), rms_v[:, 2, :].unsqueeze(2).to_broadcast([TT, NT, C]),
                                            ALU.mult).then_inc(normed.sem, 1)
                if n is not None:
                    dve.wait_ge(weighted.sem, weighted.at(n, 1))
                    dve.wait_ge(t2_ready.sem, t2_ready.at(n, 0))
                    tthen(nc.vector.tensor_tensor(t1[:, :, :], x_sum[:, :, :], o_rms, ALU.add))
                if m is not None:
                    dve.wait_ge(gn_tok_up.sem, gn_tok_up.at(m, 1))
                    nc.vector.tensor_tensor(x_sum[:, :, :], x_tok[:, :, :], tokens(6), ALU.add).then_inc(xs_ready.sem, 1)
                if n is not None:
                    norm_stats(tthen, norm1, t1, 1e-5).then_inc(ln1_var.sem, 1)
                if n is not None:
                    dve.wait_ge(ln1_std.sem, ln1_std.at(n, 1))
                    norm_apply(norm1, t1, ln1_tok).then_inc(ln1_ready.sem, 1)
                if m is not None:
                    for ck in range(NC_):
                        dve.wait_ge(dt_abs.sem, dt_abs.at(m, ck + 1))
                        nc.vector.tensor_scalar(dt_sb[:, ck, :], wide(2 * ck), b_dt_sb[:, ck:ck + 1], 0.0,
                                                ALU.add, ALU.max).then_inc(dt_relu.sem, 1)
                if m is not None:
                    dve.wait_ge(sp_exp.sem, sp_exp.at(m, 1))
                    nc.vector.tensor_scalar(conv_acc[:, :, :], sp_e[:, :, :], 1.0, 1.0, ALU.add, ALU.subtract).then_inc(sp_u.sem, 1)
                    dve.wait_ge(sp_u.sem, sp_u.at(m, 1))
                    mthen(nc.vector.tensor_tensor(conv_acc[:, 0, :], sp_e[:, 0, :], conv_acc[:, 0, :], ALU.subtract))
                    dve.wait_ge(dt_relu.sem, dt_relu.at(m, 1))
                    mthen(nc.vector.tensor_tensor(dt_sb[:, 0, :], dt_sb[:, 0, :], conv_acc[:, 0, :], ALU.add))
                if n is not None:
                    low_parts(0)
                    low_parts(1)
                if m is not None:
                    dve.wait_ge(sp_low1.sem, sp_low1.at(m, 1))
                    dve.wait_ge(sp_ln.sem, sp_ln.at(m, 1))
                    for ck in range(NC_):
                        nc.vector.tensor_tensor(dt_sb[:, ck, :], dt_sb[:, ck, :], sp_l[:, ck, :], ALU.add).then_inc(dt_ready.sem, 1)
                        dve.wait_ge(dt_ready.sem, dt_ready.at(m, ck + 1))
                        nc.vector.tensor_tensor(sp_l[:, ck, :], dt_sb[:, ck, :], xc[:, ck, :], ALU.mult).then_inc(u_ready.sem, 1)
                def sum_up(ck):
                    return nc.vector.scalar_tensor_tensor(xc[:, ck, :], xc[:, ck, :], d_skip_sb[:, ck:ck + 1], wide(2 * ck),
                                                          ALU.mult, ALU.add)

                for i in range(NSTEP):
                    if m is not None:
                        dve.wait_ge(dA_ready.sem, dA_ready.at(m, i + 1))
                        dve.wait_ge(dbu_ready.sem, dbu_ready.at(m, i + 1))
                        nc.vector.tensor_tensor_scan(hst[:, i % 2, :], dA[:, i % 2, :], dbu[:, i % 2, :], 0.0,
                                                     ALU.mult, ALU.add).then_inc(scan_done.sem, 1)
                        s, ck = divmod(i, NC_)
                        k = s % NBB
                        dve.wait_ge(c_in[k].sem, c_in[k].at(m, 16 * (s // NBB + 1)))
                        dve.wait_ge(scan_done.sem, scan_done.at(m, i + 1))
                        if paired(i):
                            nc.vector.tensor_tensor(hst[:, ck, :], hst[:, ck, :], c_all[:, k, :], ALU.mult).then_inc(g_ready.sem, 1)
                            dve.wait_ge(g_ready.sem, g_ready.at(m, i + 1))
                            nc.vector.tensor_tensor(g[:, ck, :], g[:, ck, :], hst[:, ck, :], ALU.add).then_inc(g_added.sem, 1)
                            dve.wait_ge(g_added.sem, g_added.at(m, sum(map(paired, range(i + 1)))))
                        else:
                            if i >= NC_:
                                dve.wait_ge(y_up.sem, y_up.at(m, sums(i - NC_ + 1)))
                            nc.vector.tensor_tensor(g[:, ck, :], hst[:, ck, :], c_all[:, k, :], ALU.mult).then_inc(g_ready.sem, 1)
                    if n is not None:
                        if i == MAX_FROM:
                            dve.wait_ge(stacks_in.sem, stacks_in.at(n, 16 * NSTK))
                            nc.vector.tensor_scalar(k_neg[:, :, :], k_stack[0:KST, :, 0:HALF], -1.0, None, ALU.mult).then_inc(k_neg_ready.sem, 1)
                        for j in max_share(i):
                            kt, h = divmod(j, H)
                            rows = ST[kt][1]
                            dve.wait_ge(relu_ready.sem, relu_ready.at(n, j + 1))
                            dve.wait_ge(smax_up.sem, smax_up.at(n, j + 1))
                            dve.sem_inc(tile_seen.sem, 1)
                            nc.vector.tensor_tensor_reduce(probs[0:rows, j % NPROB, :], bank(4 + 2 * (j % 2), HALF)[0:rows],
                                                           probs[0:rows, j % NPROB, :], 1.0, LOWEST, ALU.add, ALU.max,
                                                           q_max[0:rows, kt, h:h + 1]).then_inc(smax_read.sem, 1)
                        if i == MAX_TO - 1:
                            dve.wait_ge(smax_read.sem, smax_read.at(n, NMAX))
                            athen(nc.vector.tensor_scalar(q_max_rest[:, :, :], q_max[:, :, :], -1.0, None, ALU.mult))
                            athen(nc.vector.tensor_copy(q_max_parts[:, :, :, 0], q_max_rest[:, :, :]))
                            athen(nc.vector.tensor_tensor(q_max_rest[:, :, :], q_max_rest[:, :, :], q_max_parts[:, :, :, 0], ALU.subtract))
                            athen(nc.vector.tensor_copy(q_max_parts[:, :, :, 1], q_max_rest[:, :, :]))
                            nc.vector.tensor_tensor(q_max_parts[:, :, :, 2], q_max_rest[:, :, :], q_max_parts[:, :, :, 1],
                                                    ALU.subtract).then_inc(max_split.sem, 1)
                        for acc in range(4):
                            if (i == UNIT_TO if acc == 3 else (acc + 1) * PER_ACC + 2 in unit_share(i)):
                                if acc == 0:
                                    dve.wait_ge(f_out.sem, f_out.at(n, 0))
                                dve.wait_ge(pv_up.sem, pv_up.at(n, (acc + 1) * PER_ACC // 4))
                                nc.vector.tensor_copy(o_raw[:, acc // 2, (acc % 2) * HALF:(acc % 2 + 1) * HALF],
                                                      bank(7, HALF)).then_inc(o_copied.sem, 1)
                        if i == UNIT_TO + 1:
                            dve.wait_ge(oTok_up.sem, oTok_up.at(n, 1))
                            for b in range(4):
                                src = PS[0:TT, (4 + b) * BANK:(5 + b) * BANK].rearrange("p (k d) -> p k d", d=32)
                                last = nc.vector.reciprocal(o_rec[:, 16 * b:16 * (b + 1)], src[:, :, HD])
                            athen(last)
                            for b in range(4):
                                src = PS[0:TT, (4 + b) * BANK:(5 + b) * BANK].rearrange("p (k d) -> p k d", d=32)
                                rec = o_rec[:, 16 * b:16 * (b + 1)].unsqueeze(2).to_broadcast([TT, 16, HD])
                                last = nc.vector.tensor_tensor(o_tok[:, :, 2 * b:2 * b + 2, :].rearrange("p h i d -> p i h d"),
                                                               src[:, :, 0:HD].rearrange("p (i h) d -> p i h d", h=H),
                                                               rec.rearrange("p (i h) d -> p i h d", h=H), ALU.mult)
                            last.then_inc(o_tok_ready.sem, 1)
                        if i == UNIT_TO + 3:
                            dve.wait_ge(proj_up.sem, proj_up.at(n, 1))
                            nc.vector.scalar_tensor_tensor(t2[:, :, :].rearrange("p k c -> p (k c)"), PS[0:TT, 6 * BANK:8 * BANK], 0.0,
                                                           t1[:, :, :].rearrange("p k c -> p (k c)"), ALU.max, ALU.add).then_inc(t2_ready.sem, 1)
                            dve.wait_ge(t2_ready.sem, t2_ready.at(n, 1))
                            norm_stats(athen, norm2, t2, 1e-5).then_inc(ln2_var.sem, 1)
                        if i == UNIT_TO + 4:
                            dve.wait_ge(ln2_std.sem, ln2_std.at(n, 1))
                            norm_apply(norm2, t2, f_tok).then_inc(ln2_ready.sem, 1)
                        if i == UNIT_TO + 5:
                            dve.wait_ge(fT_ready.sem, fT_ready.at(n, 1))
                            nc.vector.reduce_sum(x_mean[:, bass.ds(n, 1)], fT, X).then_inc(mean_read.sem, 1)
                if m is not None:
                    dve.wait_ge(y_up.sem, y_up.at(m, sums(NSTEP)))
                    sum_up(1).then_inc(y_summed.sem, 1)
                    sum_up(0).then_inc(y_summed.sem, 1)
                    dve.wait_ge(y_summed.sem, y_summed.at(m, 2))
                    nc.vector.tensor_tensor(in_tj(conv_acc[:, 0, :]), by_jt(xc[:, 0, :]), by_jt(z_act[:, 0, :]),
                                            ALU.mult).then_inc(y_ready[0].sem, 1)
                assert n is None or dve_order_t.count == dve_order_t.per_turn, dve_order_t.count
                assert m is None or dve_order_m.count == dve_order_m.per_turn, dve_order_m.count
                assert n is None or dve_order_a.count == dve_order_a.per_turn, dve_order_a.count

            turn(None, 0)
            dve.wait_ge(pads_set, 1)
            with nc.vector.Fori(0, B - 1) as n:
                turn(n, n + 1)
            turn(B - 1, None)

            def rthen(ins):
                dve_order_rt.after(dve, 0, ins)

            dve.wait_ge(mean_read.sem, mean_read.at(B, 0))
            nc.vector.tensor_scalar(x_mean[:, :], x_mean[:, :], 1.0 / TOK, None, ALU.mult).then_inc(means_ready, 1)
            dve.wait_ge(logits_up, 1)
            rthen(nc.vector.tensor_copy(rt[:, 0, :], PS[0:B, 0:NE]))
            rthen(nc.vector.tensor_reduce(rt[:, 14, 0:1], rt[:, 0, :], axis=X, op=ALU.max))
            nc.vector.tensor_scalar(rt[:, 1, :], rt[:, 0, :], rt[:, 14, 0:1], None, ALU.subtract).then_inc(rt_ready, 1)
            dve.wait_ge(rt_exp, 1)
            rthen(nc.vector.reduce_sum(rt[:, 14, 1:2], rt[:, 2, :], X))
            rthen(nc.vector.reciprocal(rt[:, 14, 2:3], rt[:, 14, 1:2]))
            nc.vector.tensor_scalar(rt[:, 3, :], rt[:, 2, :], rt[:, 14, 2:3], None, ALU.mult).then_inc(routed, 1)
            dve.wait_ge(loads_up, 1)
            rthen(nc.vector.tensor_scalar(rt[:, 7, :], PS[0:B, BANK:BANK + NE], float(TOK), None, ALU.mult))
            rthen(nc.vector.reciprocal(rt[:, 8, :], rt[:, 7, :]))
            rthen(nc.vector.tensor_scalar(rt[:, 9, :], rt[:, 8, :], CAPACITY, 1.0, ALU.mult, ALU.min))
            rthen(nc.vector.tensor_tensor(rt[:, 4, :], rt[:, 3, :], rt[:, 9, :], ALU.mult))
            rthen(nc.vector.tensor_reduce(rt[:, 14, 3:4], rt[:, 4, :], axis=X, op=ALU.max))
            nc.vector.tensor_scalar(rt[:, 5, :], rt[:, 4, :], rt[:, 14, 3:4], None, ALU.subtract).then_inc(rt_ready, 1)
            dve.wait_ge(rt_exp, 2)
            rthen(nc.vector.reduce_sum(rt[:, 14, 4:5], rt[:, 6, :], X))
            rthen(nc.vector.reciprocal(rt[:, 14, 5:6], rt[:, 14, 4:5]))
            rthen(nc.vector.tensor_scalar(rt[:, 10, :], rt[:, 6, :], rt[:, 14, 5:6], None, ALU.mult))
            rthen(nc.vector.max(top_v[:, :], rt[:, 10, :]))
            nc.vector.max_index(top_i[:, :], top_v[:, :], rt[:, 10, :]).then_inc(top_ready, 1)
            nc.vector.tensor_tensor(top_w[:, 0:1], top_v[:, 1:2], top_v[:, 0:1], ALU.subtract).then_inc(rt_ready, 1)
            dve.wait_ge(rt_exp, 3)
            rthen(nc.vector.tensor_scalar(top_w[:, 2:3], top_w[:, 1:2], 1.0, None, ALU.add))
            rthen(nc.vector.reciprocal(top_w[:, 2:3], top_w[:, 2:3]))
            rthen(nc.vector.tensor_tensor(top_w[:, 3:4], top_w[:, 1:2], top_w[:, 2:3], ALU.mult))
            for k in range(TOPK):
                last = nc.vector.tensor_scalar(w_diag[:, :, k], ident[0:B, 0:B], top_w[:, 2 + k:3 + k], None, ALU.mult)
            last.then_inc(w_diag_ready, 1)
            dve.wait_ge(w_all_up, 1)
            nc.vector.tensor_copy(w_all[:, :], bank(2, B * TOPK)).then_inc(w_all_ready, 1)
            dve.wait_ge(w_all_ready, 1)

            with nc.vector.Fori(0, B // 2) as n:
                dve_order_e.count = 0

                def ethen(ins):
                    dve_order_e.after(dve, n, ins)

                for z in range(2):
                    weight = [bass.ds(n * 2 * TOPK + z * TOPK + k, 1) for k in range(TOPK)]
                    dve.wait_ge(e_f_in[z].sem, e_f_in[z].at(n, e_f_in[z].per_turn))
                    ethen(nc.vector.tensor_scalar(b2_s[z][:, :], b2_e[z][:, 0, :], w_all[0:TT, weight[0]], None, ALU.mult))
                    ethen(nc.vector.scalar_tensor_tensor(b2_s[z][:, :], b2_e[z][:, 1, :], w_all[0:TT, weight[1]], b2_s[z][:, :],
                                                         ALU.mult, ALU.add))
                    ethen(nc.vector.tensor_tensor(f_e[z], f_e[z], b2_s[z][:, :].unsqueeze(1).to_broadcast([TT, NT, C]), ALU.add))
                    dve.wait_ge(y_e_up[z].sem, y_e_up[z].at(n, 1))
                    nc.vector.tensor_tensor(t1[:, :, :], f_e[z], tokens(4 + 2 * z), ALU.add).then_inc(res_read[z].sem, 1)
                    dve.wait_ge(res_read[z].sem, res_read[z].at(n, 1))
                    norm_stats(ethen, norm1, t1, 1e-5).then_inc(lnf_var[z].sem, 1)
                    dve.wait_ge(lnf_std[z].sem, lnf_std[z].at(n, 1))
                    dve.wait_ge(lnf_read[1 - z].sem, lnf_read[1 - z].at(n, z))
                    ethen(norm_apply(norm1, t1, ln1_tok))
                    nc.vector.tensor_tensor(ln1_tok, ln1_tok, gamma_sb[:, :].unsqueeze(1).to_broadcast([TT, NT, C]),
                                            ALU.mult).then_inc(lnf_ready[z].sem, 1)
                    dve.wait_ge(lnf_ready[z].sem, lnf_ready[z].at(n, 1))
            assert dve_order_e.count == dve_order_e.per_turn, dve_order_e.count

        @block.tensor
        def _(pe):
            pe.wait_ge(consts_pool, 1)

            def channel_major(src, b):
                for k in range(NT):
                    a, o = divmod(k * TT, HALF)
                    last = nc.tensor.transpose(PS[:, (b + a) * BANK + o:(b + a) * BANK + o + TT], src[:, k, :], ident[0:TT, 0:TT])
                return last

            def over_spans(b, lhsT, rhs, start=True, stop=True):
                for at, width in SPANS:
                    last = nc.tensor.matmul(PS[:, b * BANK + at:b * BANK + at + width], lhsT, rhs[:, at:at + width],
                                            start=start, stop=stop)
                return last

            def turn(n, m):
                def sum_states(i):
                    state, ck = divmod(i, NC_)
                    if not summed(i):
                        return
                    if paired(i):
                        pe.wait_ge(g_added.sem, g_added.at(m, sum(map(paired, range(i + 1)))))
                    else:
                        pe.wait_ge(g_ready.sem, g_ready.at(m, i + 1))
                    over_spans(2 * ck, ident[:, :], g[:, ck, :], start=(state == 0), stop=(state == NS - 1)).then_inc(y_up.sem, 1)

                def max_scores(j):
                    def queries(j):
                        kt, h = divmod(j, H)
                        at, rows = ST[kt]
                        return h, rows, q_stack[0:KST, h, at:at + rows]

                    if j == 0:
                        pe.wait_ge(k_neg_ready.sem, k_neg_ready.at(n, 1))
                        pe.wait_ge(v_copied.sem, v_copied.at(n, 1))
                    for k in ([0, 1] if j == 0 else [j + 1] if j + 1 < NMAX else []):
                        h, rows, q = queries(k)
                        if k >= 2:
                            pe.wait_ge(relu_ready.sem, relu_ready.at(n, k - 1))
                        nc.tensor.matmul(bank(5 + 2 * (k % 2), HALF)[0:rows], q, k_stack[0:KST, h, HALF:TOK], start=True, stop=False)
                        nc.tensor.matmul(bank(5 + 2 * (k % 2), HALF)[0:rows], q, k_neg[:, h, :], start=False, stop=True).then_inc(diff_up.sem, 1)
                    h, rows, q = queries(j)
                    if j >= 2:
                        pe.wait_ge(smax_read.sem, smax_read.at(n, j - 1))
                    nc.tensor.matmul(bank(4 + 2 * (j % 2), HALF)[0:rows], q, k_stack[0:KST, h, 0:HALF], start=True, stop=True).then_inc(smax_up.sem, 1)

                def four_times_v(group):
                    for j in range(4 * group, 4 * group + 4):
                        acc, kt, q, h, _ = unit(j)
                        if q == 0:
                            pe.wait_ge(probs_ready.sem, probs_ready.at(n, j + 4))
                            if acc and kt == 0:
                                pe.wait_ge(o_copied.sem, o_copied.at(n, acc))
                        last = nc.tensor.matmul(PS[32 * q:32 * (q + 1), 7 * BANK:7 * BANK + HALF],
                                                v_ext[:, kt, h, :], probs[:, j % NPROB, :],
                                                start=(kt == 0), stop=(kt == NST - 1))
                    last.then_inc(pv_up.sem, 1)

                def scores(j):
                    _, kt, _, h, q0 = unit(j)
                    at, rows = ST[kt]
                    if j == 0:
                        pe.wait_ge(max_in.sem, max_in.at(n, 16 * H))
                    if j >= 3:
                        pe.wait_ge(probs_ready.sem, probs_ready.at(n, j - 2))
                    nc.tensor.matmul(bank(4 + j % 3, HALF)[0:rows], k_stack[:, h, at:at + rows],
                                     q_stack[:, h, q0:q0 + HALF], start=True, stop=True).then_inc(s_up.sem, 1)

                if m is not None:
                    if n is not None:
                        pe.wait_ge(y_summed.sem, y_summed.at(n, NC_))
                    pe.wait_ge(x_in.sem, x_in.at(m, 16))
                    channel_major(x_tok, 2).then_inc(xT_up.sem, 1)
                if m is not None:
                    pe.wait_ge(chan_ready.sem, chan_ready.at(m, 1))
                    nc.tensor.matmul(bank(0, NPART), group_avg[:, :], part_mean, start=True, stop=True).then_inc(gmean_up.sem, 1)
                    pe.wait_ge(gdev_ready.sem, gdev_ready.at(m, 1))
                    nc.tensor.matmul(bank(1, NPART), group_avg[:, :], part_dev[:, :], start=True, stop=True).then_inc(gvar_up.sem, 1)
                if n is not None:
                    for ck in range(NC_):
                        pe.wait_ge(y_ready[ck].sem, y_ready[ck].at(n, 1))
                    pe.wait_ge(fT_ready.sem, fT_ready.at(n, 0))
                    for k in range(NT):
                        for ck in range(NC_):
                            last = nc.tensor.matmul(PS[0:TT, 4 * BANK + k * C:4 * BANK + (k + 1) * C], conv_acc[:, ck, k * TT:(k + 1) * TT],
                                                    w_out_sb[:, ck, :], start=(ck == 0), stop=(ck == NC_ - 1))
                    last.then_inc(out_up.sem, 1)
                if m is not None:
                    if n is None:
                        pe.wait_ge(weights_in, NW[0])
                    pe.wait_ge(xn_ready.sem, xn_ready.at(m, 1))
                    over_spans(0, w_in_sb[:, 0:P], xnT).then_inc(xz_up.sem, 1)
                    over_spans(2, w_in_sb[:, P:2 * P], xnT).then_inc(xz_up.sem, 1)
                    for k in range(NT):
                        last = nc.tensor.transpose(PS[0:TT, 6 * BANK + k * C:6 * BANK + (k + 1) * C], xnT[:, k * TT:(k + 1) * TT], ident[:, :])
                    last.then_inc(gn_tok_up.sem, 1)
                    pe.wait_ge(conv_done.sem, conv_done.at(m, 1))
                    over_spans(0, w_in_sb[:, 2 * P:3 * P], xnT).then_inc(xz_up.sem, 1)
                    pe.wait_ge(conv_done.sem, conv_done.at(m, 2))
                    over_spans(2, w_in_sb[:, 3 * P:4 * P], xnT).then_inc(xz_up.sem, 1)
                    pe.wait_ge(silu_done.sem, silu_done.at(m, 3))
                    for at, width in SPANS:
                        for ck in range(NC_):
                            last = nc.tensor.matmul(PS[:, at:at + width], w_xp_sb[:, ck, :],
                                                    xc[:, ck, at:at + width], start=(ck == 0), stop=(ck == NC_ - 1))
                    last.then_inc(xd_up.sem, 1)
                    pe.wait_ge(xd_ready.sem, xd_ready.at(m, 1))
                    over_spans(0, w_dt_sb[DT0:P, 0:P], xd[DT0:P, :]).then_inc(dt_up.sem, 1)
                    pe.wait_ge(silu_done.sem, silu_done.at(m, 4))
                    over_spans(2, w_dt_sb[DT0:P, P:2 * P], xd[DT0:P, :]).then_inc(dt_up.sem, 1)
                if n is not None:
                    pe.wait_ge(ln1_ready.sem, ln1_ready.at(n, 1))
                    channel_major(ln1_tok, 6).then_inc(ln1T_up.sem, 1)
                if n is not None:
                    pe.wait_ge(ln1T_ready.sem, ln1T_ready.at(n, 1))
                    over_spans(4, w_qkv_sb[:, 0:C], lnT).then_inc(q_up.sem, 1)
                    over_spans(6, w_qkv_sb[:, C:2 * C], lnT).then_inc(k_up.sem, 1)
                    pe.wait_ge(qk_parts.sem, qk_parts.at(n, 1))
                    for k, (at, rows) in enumerate(ST):
                        last = nc.tensor.matmul(PS[0:rows, 4 * BANK + k * C:4 * BANK + (k + 1) * C], lnT[:, at:at + rows],
                                                w_qkv_sb[:, 2 * C:3 * C], start=True, stop=True)
                    last.then_inc(v_up.sem, 1)
                if m is not None:
                    pe.wait_ge(dt_relu.sem, dt_relu.at(m, NC_))

                for i in range(NSTEP):
                    if m is not None:
                        if i >= 1:
                            sum_states(i - 1)
                    if n is not None:
                        for j in max_share(i):
                            max_scores(j)
                        if i == MAX_TO:
                            pe.wait_ge(max_split.sem, max_split.at(n, 1))
                            for k, (at, rows) in enumerate(ST):
                                last = nc.tensor.matmul(PS[0:3 * H, 4 * BANK + at:4 * BANK + at + rows],
                                                        q_max_parts[0:rows, k, :, :].rearrange("p h a -> p (h a)"),
                                                        ident_bf[0:rows, 0:rows], start=True, stop=True)
                            last.then_inc(maxT_up.sem, 1)
                        for j in unit_share(i):
                            scores(j)
                            if j % 4 == 2 and j >= 4:
                                four_times_v(j // 4 - 1)
                            if j == NUNIT - 1:
                                four_times_v(NUNIT // 4 - 1)
                        if i == UNIT_TO + 1:
                            pe.wait_ge(o_copied.sem, o_copied.at(n, 4))
                            for k in range(NT):
                                for gr in range(2):
                                    o = 4 * BANK + k * 2 * P + gr * P
                                    last = nc.tensor.transpose(PS[0:TT, o:o + P], o_raw[:, gr, k:TOK:NT], ident[:, :])
                            last.then_inc(oTok_up.sem, 1)
                        if i == UNIT_TO + 2:
                            pe.wait_ge(o_tok_ready.sem, o_tok_ready.at(n, 1))
                            channel_major(o_tok_v, 4).then_inc(oT_up.sem, 1)
                        if i == UNIT_TO + 3:
                            pe.wait_ge(oT_ready.sem, oT_ready.at(n, 1))
                            for k in range(NT):
                                o = 6 * BANK + k * C
                                nc.tensor.matmul(PS[0:TT, o:o + C], oT[:, k * TT:(k + 1) * TT], proj_w_sb[:, :], start=True, stop=False)
                                last = nc.tensor.matmul(PS[0:TT, o:o + C], ones[0:1, 0:TT], proj_b_sb[:, :], start=False, stop=True)
                            last.then_inc(proj_up.sem, 1)
                        if i == UNIT_TO + 5:
                            pe.wait_ge(ln2_ready.sem, ln2_ready.at(n, 1))
                            channel_major(f_tok, 4).then_inc(fT_up.sem, 1)
                if m is not None:
                    sum_states(NSTEP - 1)

            turn(None, 0)
            pe.wait_ge(pads_set, 1)
            pe.wait_ge(consts_dve, 1)
            with nc.tensor.Fori(0, B - 1) as n:
                turn(n, n + 1)
            turn(B - 1, None)

            pe.wait_ge(means_ready, 1)
            nc.tensor.matmul(PS[0:B, 0:NE], x_mean[:, :], w_r_sb[:, :], start=True, stop=False)
            nc.tensor.matmul(PS[0:B, 0:NE], ones[0:1, 0:B], b_r_sb[:, :], start=False, stop=True).then_inc(logits_up, 1)
            pe.wait_ge(routed, 1)
            nc.tensor.matmul(PS[0:B, BANK:BANK + NE], ones[0:B, 0:B], rt[:, 3, :], start=True, stop=True).then_inc(loads_up, 1)
            pe.wait_ge(w_diag_ready, 1)
            nc.tensor.matmul(bank(2, B * TOPK), ones[0:B, :], w_diag[:, :, :].rearrange("p b k -> p (b k)"),
                             start=True, stop=True).then_inc(w_all_up, 1)
            pe.wait_ge(w_all_ready, 1)

            with nc.tensor.Fori(0, B // 2) as n:
                for z in range(2):
                    pe.wait_ge(e_w1_in[z].sem, e_w1_in[z].at(n, e_w1_in[z].per_turn))
                    for i in range(TOPK * FC):
                        k, fc = divmod(i, FC)
                        if i >= 2:
                            pe.wait_ge(h_ready[z].sem, h_ready[z].at(n, i - 1))
                        over_spans(2 * (i % 2), w1_e[z][:, k, fc * P:(fc + 1) * P], fT_e[z]).then_inc(h_up[z].sem, 1)
                    pe.wait_ge(h_ready[z].sem, h_ready[z].at(n, TOPK * FC))
                    pe.wait_ge(e_w2_scaled[z].sem, e_w2_scaled[z].at(n, 1))
                    pe.wait_ge(res_read[z].sem, res_read[z].at(n, 0))
                    for kt in range(NT):
                        o = (4 + 2 * z) * BANK + kt * C
                        for i in range(TOPK * FC):
                            last = nc.tensor.matmul(PS[0:TT, o:o + C], hidden[z][i][:, kt * TT:(kt + 1) * TT], w2_s[z][:, i // FC, i % FC, :],
                                                    start=(i == 0), stop=(i == TOPK * FC - 1))
                    last.then_inc(y_e_up[z].sem, 1)


_NAMES = ['x', 'L0_conv_W_in', 'L0_conv_conv_w', 'L0_conv_conv_b', 'L0_conv_W_xproj', 'L0_conv_W_dt', 'L0_conv_b_dt',
          'L0_conv_A_log', 'L0_conv_D_skip', 'L0_conv_W_out', 'L0_conv_ln_w', 'L1_attn_W', 'L1_attn_proj_w',
          'L1_attn_proj_b', 'L1_ffn_Wr', 'L1_ffn_br', 'L1_ffn_W1', 'L1_ffn_b1', 'L1_ffn_W2', 'L1_ffn_b2',
          'L1_ffn_gamma', 'L1_ffn_beta']
_TRANSPOSED = ('L0_conv_W_in', 'L0_conv_W_xproj', 'L0_conv_W_dt', 'L0_conv_W_out')

_BY_PARTITION = ('L0_conv_conv_b', 'L0_conv_b_dt', 'L0_conv_D_skip', 'L1_ffn_b1')


def kernel(**inputs):
    import numpy as _np
    import concourse.bacc as _bacc
    from concourse import mybir as _mybir
    from concourse.bass_utils import run_bass_kernel_spmd as _run

    nc = _bacc.Bacc("TRN2", target_bir_lowering=False, num_devices=1)
    arrays, args = {}, []
    for name in _NAMES:
        a = _np.asarray(inputs[name])
        if name in _TRANSPOSED:
            a = a.T
        if name in _BY_PARTITION:
            a = _np.swapaxes(a.reshape(*a.shape[:-1], -1, 128), -1, -2)
        a = _np.ascontiguousarray(a)
        arrays[f"in_{name}"] = a
        args.append(nc.dram_tensor(f"in_{name}", a.shape, _mybir.dt.from_np(a.dtype), kind="ExternalInput").ap())
    shape = arrays["in_x"].shape
    out = nc.dram_tensor("out_0", shape, _mybir.dt.float32, kind="ExternalOutput").ap()
    mamba_attention_moe(nc, *args, out)
    r = _run(nc, [arrays], core_ids=[0])
    return r.results[0]["out_0"]
```
